# Optimizing a Trainium2 kernel written in Bass

```python
import numpy as np
import jax
import jax.numpy as jnp

def _softmax(x, axis=-1):
    return jax.nn.softmax(x, axis=axis)

def _gelu(x):
    return jax.nn.gelu(x, approximate=True)

def _silu(x):
    return jax.nn.silu(x)

def _sigmoid(x):
    return jax.nn.sigmoid(x)

def _layernorm(x, axis=-1, eps=1e-05):
    m = jnp.mean(x, axis=axis, keepdims=True)
    v = jnp.var(x, axis=axis, keepdims=True)
    return (x - m) / jnp.sqrt(v + eps)

def _scatter_add(tgt, idx, src, axis=0):
    return tgt.at[idx].add(src)

def _segment_sum(src, seg, n):
    return jax.ops.segment_sum(src, seg, n)
kernel_name = 'mk_gps_d1_gnn_r8_ff7e29'

def setup_inputs(seed: int=0):
    np.random.seed(seed)
    _w = jnp.asarray

    def _rec_inputs():
        import jax
        import jax.numpy as jnp
        _gk = jax.random.key(seed)
        x = -0.0002117 + 1 * jax.random.normal(jax.random.fold_in(_gk, 1), (12500, 256), jnp.float32)
        src = jax.random.randint(jax.random.fold_in(_gk, 2), (200000,), 0, 12500, jnp.int32)
        dst = jax.random.randint(jax.random.fold_in(_gk, 3), (200000,), 0, 12500, jnp.int32)
        _o = jnp.argsort(dst, stable=True)
        src = src[_o]
        dst = dst[_o]
        edge_weight = jax.random.uniform(jax.random.fold_in(_gk, 12), (200000,), jnp.float32, 0.0, 1)
        return (x, src, dst, edge_weight)
    x, src, dst, edge_weight = _rec_inputs()

    def _L0_gnn_setup():
        import jax, jax.numpy as jnp
        import numpy as np
        N_NODES = 12500
        key = jax.random.key(seed)
        k1, k2, k3, k4 = jax.random.split(key, 4)
        inp = jax.random.normal(k1, (12500, 256), dtype=jnp.float32)
        edge_index = jax.random.randint(k2, (2, 400000), 0, N_NODES, dtype=jnp.int64)
        edge_weight = jax.random.uniform(k3, (400000,), dtype=jnp.float32)
        fan_in, fan_out = (256, 256)
        limit = float(np.sqrt(6.0 / (fan_in + fan_out)))
        weight = jax.random.uniform(k4, (256, 256), dtype=jnp.float32, minval=-limit, maxval=limit)
        return {'input': inp, 'edge_index': edge_index, 'edge_weight': edge_weight, 'weight': weight}
    _L0_gnn_all = _L0_gnn_setup()
    _L0_gnn_in = {k: v for k, v in _L0_gnn_all.items() if k in ('weight',)}
    del _L0_gnn_all

    def _L0_mix_setup():
        import jax, jax.numpy as jnp
        import numpy as np
        import math
        EMBED = 256
        HEADS = 4
        HEAD_DIM = EMBED // HEADS
        OUT_DIM = 256
        LN_EPS = 1e-05

        def _qkv_init(key):
            spread = math.sqrt(3.0 / EMBED)
            gain, delta = (0.01, 0.01)
            w = jax.random.uniform(key, (EMBED, EMBED), minval=-spread, maxval=spread) * gain
            return w + delta * jnp.eye(EMBED, dtype=w.dtype)

        def _layer_norm(x, g, b):
            mu = jnp.mean(x, axis=-1, keepdims=True)
            var = jnp.mean(jnp.square(x - mu), axis=-1, keepdims=True)
            return (x - mu) * jax.lax.rsqrt(var + LN_EPS) * g + b

        def _split_heads(x, B, S):
            return x.reshape(B, S, HEADS, HEAD_DIM).transpose(0, 2, 1, 3)
        key = jax.random.key(seed)
        ks = jax.random.split(key, 6)
        seq = jax.random.normal(ks[0], (4, 1024, EMBED), dtype=jnp.float32)
        wq = _qkv_init(ks[1])
        wk = _qkv_init(ks[2])
        wv = _qkv_init(ks[3])
        bound = 1.0 / math.sqrt(EMBED)
        wo = jax.random.uniform(ks[4], (OUT_DIM, EMBED), minval=-bound, maxval=bound)
        bo = jax.random.uniform(ks[5], (OUT_DIM,), minval=-bound, maxval=bound)
        ln_k_g = jnp.ones((HEAD_DIM,), jnp.float32)
        ln_k_b = jnp.zeros((HEAD_DIM,), jnp.float32)
        ln_v_g = jnp.ones((HEAD_DIM,), jnp.float32)
        ln_v_b = jnp.zeros((HEAD_DIM,), jnp.float32)
        return {'seq': seq, 'wq': wq, 'wk': wk, 'wv': wv, 'wo': wo, 'bo': bo, 'ln_k_g': ln_k_g, 'ln_k_b': ln_k_b, 'ln_v_g': ln_v_g, 'ln_v_b': ln_v_b}
    _L0_mix_all = _L0_mix_setup()
    _L0_mix_in = {k: v for k, v in _L0_mix_all.items() if k in ('wq', 'wk', 'wv', 'wo', 'bo', 'ln_k_g', 'ln_k_b', 'ln_v_g', 'ln_v_b')}
    del _L0_mix_all

    def _L0_ffn_setup():
        import jax, jax.numpy as jnp
        import numpy as np
        C = 256
        EPS = 1e-05
        N_ITERS = 30

        def _layernorm(x, w, bias):
            mu = jnp.mean(x, axis=-1, keepdims=True)
            var = jnp.mean(jnp.square(x - mu), axis=-1, keepdims=True)
            return (x - mu) * jax.lax.rsqrt(var + EPS) * w + bias
        key = jax.random.key(seed)
        kx, kw, kb, klw, klb = jax.random.split(key, 5)
        x = jax.random.normal(kx, (8, 256, C), dtype=jnp.float32)
        bound = 1.0 / np.sqrt(C)
        W = jax.random.uniform(kw, (C, C), minval=-bound, maxval=bound, dtype=jnp.float32)
        b = jax.random.uniform(kb, (C,), minval=-bound, maxval=bound, dtype=jnp.float32)
        ln_w = jnp.ones((C,), dtype=jnp.float32)
        ln_b = jnp.zeros((C,), dtype=jnp.float32)
        return {'x': x, 'ln_w': ln_w, 'ln_b': ln_b, 'W': W, 'b': b}
    _L0_ffn_all = _L0_ffn_setup()
    _L0_ffn_in = {k: v for k, v in _L0_ffn_all.items() if k in ('ln_w', 'ln_b', 'W', 'b')}
    del _L0_ffn_all
    return {'x': x, 'src': src, 'dst': dst, 'edge_weight': edge_weight, 'L0_gnn_weight': _L0_gnn_in['weight'], 'L0_mix_wq': _L0_mix_in['wq'], 'L0_mix_wk': _L0_mix_in['wk'], 'L0_mix_wv': _L0_mix_in['wv'], 'L0_mix_wo': _L0_mix_in['wo'], 'L0_mix_bo': _L0_mix_in['bo'], 'L0_mix_ln_k_g': _L0_mix_in['ln_k_g'], 'L0_mix_ln_k_b': _L0_mix_in['ln_k_b'], 'L0_mix_ln_v_g': _L0_mix_in['ln_v_g'], 'L0_mix_ln_v_b': _L0_mix_in['ln_v_b'], 'L0_ffn_ln_w': _L0_ffn_in['ln_w'], 'L0_ffn_ln_b': _L0_ffn_in['ln_b'], 'L0_ffn_W': _L0_ffn_in['W'], 'L0_ffn_b': _L0_ffn_in['b']}

def reference(x, src, dst, edge_weight, L0_gnn_weight, L0_mix_wq, L0_mix_wk, L0_mix_wv, L0_mix_wo, L0_mix_bo, L0_mix_ln_k_g, L0_mix_ln_k_b, L0_mix_ln_v_g, L0_mix_ln_v_b, L0_ffn_ln_w, L0_ffn_ln_b, L0_ffn_W, L0_ffn_b):
    import jax
    import jax.numpy as jnp

    def _L0_gnn_ref(input, edge_index, edge_weight, weight):
        import jax, jax.numpy as jnp
        import numpy as np
        N_NODES = 12500
        support = input @ weight
        src, dst = (edge_index[0], edge_index[1])
        msgs = support[src] * edge_weight[:, None]
        agg = jax.ops.segment_sum(msgs, dst, num_segments=N_NODES)
        return jax.nn.relu(agg)

    def _L0_mix_ref(seq, wq, wk, wv, wo, bo, ln_k_g, ln_k_b, ln_v_g, ln_v_b):
        import jax, jax.numpy as jnp
        import numpy as np
        import math
        EMBED = 256
        HEADS = 4
        HEAD_DIM = EMBED // HEADS
        OUT_DIM = 256
        LN_EPS = 1e-05

        def _qkv_init(key):
            spread = math.sqrt(3.0 / EMBED)
            gain, delta = (0.01, 0.01)
            w = jax.random.uniform(key, (EMBED, EMBED), minval=-spread, maxval=spread) * gain
            return w + delta * jnp.eye(EMBED, dtype=w.dtype)

        def _layer_norm(x, g, b):
            mu = jnp.mean(x, axis=-1, keepdims=True)
            var = jnp.mean(jnp.square(x - mu), axis=-1, keepdims=True)
            return (x - mu) * jax.lax.rsqrt(var + LN_EPS) * g + b

        def _split_heads(x, B, S):
            return x.reshape(B, S, HEADS, HEAD_DIM).transpose(0, 2, 1, 3)
        B, S, _ = seq.shape
        q = _split_heads(seq @ wq.T, B, S)
        k = _split_heads(seq @ wk.T, B, S)
        v = _split_heads(seq @ wv.T, B, S)
        k = _layer_norm(k, ln_k_g, ln_k_b)
        v = _layer_norm(v, ln_v_g, ln_v_b)
        kv = jnp.einsum('bhsd,bhse->bhde', k, v) / S
        ga = jnp.einsum('bhsd,bhde->bhse', q, kv)
        ga = ga.transpose(0, 2, 1, 3).reshape(B, S, EMBED)
        return ga @ wo.T + bo

    def _L0_ffn_ref(x, ln_w, ln_b, W, b):
        import jax, jax.numpy as jnp
        import numpy as np
        C = 256
        EPS = 1e-05
        N_ITERS = 30

        def _layernorm(x, w, bias):
            mu = jnp.mean(x, axis=-1, keepdims=True)
            var = jnp.mean(jnp.square(x - mu), axis=-1, keepdims=True)
            return (x - mu) * jax.lax.rsqrt(var + EPS) * w + bias

        def step(h, _):
            h = h + 0.01 * jnp.tanh(h)
            h = h * jax.nn.sigmoid(h)
            h = _layernorm(h, ln_w, ln_b)
            h = jnp.einsum('bsc,dc->bsd', h, W) + b
            return (h, None)
        x, _ = jax.lax.scan(step, x, None, length=N_ITERS)
        return x
    edge_index = jnp.stack([src, dst])
    xn = _layernorm(x, axis=-1)
    x = x + _L0_gnn_ref(xn, edge_index, edge_weight, L0_gnn_weight) + _L0_mix_ref(xn[None], L0_mix_wq, L0_mix_wk, L0_mix_wv, L0_mix_wo, L0_mix_bo, L0_mix_ln_k_g, L0_mix_ln_k_b, L0_mix_ln_v_g, L0_mix_ln_v_b)[0]
    x = x + _L0_ffn_ref(_layernorm(x, axis=-1)[None], L0_ffn_ln_w, L0_ffn_ln_b, L0_ffn_W, L0_ffn_b)[0]
    return x

_drawn_inputs = setup_inputs


def setup_inputs(seed=0):
    import zlib

    import numpy as np

    out = dict(_drawn_inputs(seed))
    spreads = {'L0_mix_ln_k_g': (1.0, 0.6),
     'L0_mix_ln_k_b': (0.0, 0.8),
     'L0_mix_ln_v_g': (1.0, 0.6),
     'L0_mix_ln_v_b': (0.0, 0.8),
     'L0_ffn_ln_w': (1.0, 0.2),
     'L0_ffn_ln_b': (0.0, 0.1)}
    factors = {'L0_mix_wq': 8.0, 'L0_mix_wk': 8.0, 'L0_mix_wv': 8.0, 'L0_mix_wo': 8.0, 'L0_mix_bo': 4.023}
    for name, (base, spread) in spreads.items():
        noise = np.random.default_rng([zlib.crc32(name.encode()), seed]).standard_normal(out[name].shape)
        drawn = base * np.exp(spread * noise) if base else spread * noise
        out[name] = jnp.asarray(drawn.astype(out[name].dtype))
    for name, factor in factors.items():
        out[name] = (out[name] * factor).astype(out[name].dtype)
    return out
```

```python
from contextlib import ExitStack

import concourse.bass as bass
from concourse import mybir

F32 = mybir.dt.float32
I32 = mybir.dt.int32
U32 = mybir.dt.uint32
ALU = mybir.AluOpType
ACT = mybir.ActivationFunctionType
AX_X = mybir.AxisListType.X

N, D, E = 12500, 256, 200000
HEADS, HD = 4, 64
STEPS = 30
EPS = 1e-5
R = 125
TILES = N // R
KC = 17
CAP = KC * 128
PAIRS = 5
ROUND = 2 * PAIRS
ROUNDS = TILES // ROUND
SLOTS = 3 * PAIRS
TRIPS = STEPS // 3
NSLOT = ROUNDS * TRIPS * SLOTS
EARLY_G = 20
EARLY_X = 10
KV_STEPS = 10
K_RING = 5
LAST_B = TILES // KV_STEPS - 1
G_ROUNDS = (TILES - EARLY_G) // ROUND
UC = 125
BLOCKS, BLOCK = 125, 1600


def spread(n, steps):
    return [list(range(n * s // steps, n * (s + 1) // steps)) for s in range(steps)]


class Plan:
    def __init__(self, steps, first, over, hot_lag, mul_lag, tail):
        self.gather = [[] for _ in range(steps)]
        self.hot = [[] for _ in range(steps)]
        self.mul = [[] for _ in range(steps)]
        for k, chunks in enumerate(spread(KC, over)):
            self.gather[first + k] += chunks
            self.hot[first + k + hot_lag] += chunks
            self.mul[first + k + mul_lag] += chunks
        self.first = first
        self.copy, self.transpose, self.multiply, self.read = tail


F_G = Plan(SLOTS, 1, 10, 1, 2, (12, 13, 14, 14))
B_G = [Plan(KV_STEPS, 0, 4, 1, 1, (4, 5, 6, 6)), Plan(KV_STEPS, 4, 4, 1, 1, (8, 9, 9, 9))]
X_BIAS, X_TRANSPOSE, X_MULTIPLY, X_STATS, X_MEAN, X_VAR, X_NORM = 1, 2, 4, 5, 6, 7, 9


def build(nc, x, src, dst, ew, w_gnn, wq, wk_t, wv_t, wo_t, bo, gk, bk, gv, bv, ln_w, ln_b, wf_t, bf, out):
    xn_d = nc.dram_tensor("xn_d", [N, D], F32).ap()
    x1a_d = nc.dram_tensor("x1a_d", [N, D], F32).ap()
    x1_d = nc.dram_tensor("x1_d", [N, D], F32).ap()
    h0_d = nc.dram_tensor("h0_d", [N, D], F32).ap()
    gen_d = nc.dram_tensor("gen_d", [N + R, D], F32).ap()

    def rows(t, tile, n=1):
        return t[bass.ds(tile * R, n * R), :].rearrange("(t p) f -> p t f", p=R)

    ctx = ExitStack()
    with ctx:
        def sb(name, shape, dt=F32):
            return ctx.enter_context(nc.sbuf_tensor(name, shape, dt))

        made = {}

        def S(name):
            if name not in made:
                made[name] = ctx.enter_context(nc.semaphore(name))
            return made[name]

        ident = sb("ident", [128, 128])
        ones = sb("ones", [128, 128])
        iota_i = sb("iota_i", [128, R], I32)
        iota_f = sb("iota_f", [128, R])
        lane_i = sb("lane_i", [128, 3], I32)
        lane_f = sb("lane_f", [128, 3])
        below = sb("below", [128, R])
        base_i = sb("base_i", [128, TILES], I32)
        base_f = sb("base_f", [128, TILES])
        minus_half = sb("minus_half", [128, 8])
        zeros = sb("zeros", [128, 2, D])
        w_kv = sb("w_kv", [128, 2, 2 * D])
        w_mean = sb("w_mean", [128, 2, 8])
        w_agg = sb("w_agg", [128, 2, D])
        w_wq = sb("w_wq", [128, 2, D])
        w_wo = sb("w_wo", [128, 2, D])
        w_raw = sb("w_raw", [128, 2, D])
        w_ffn = sb("w_ffn", [128, 2, D])
        w_mix = sb("w_mix", [128, 2, D])
        lnw_c = sb("lnw_c", [128, 2])
        lnb_c = sb("lnb_c", [128, 2])
        lnb_b = sb("lnb_b", [128, 2, 128])
        c_row = sb("c_row", [128, D])
        bo_row = sb("bo_row", [128, D])
        gk_row = sb("gk_row", [128, 128])
        bk_row = sb("bk_row", [128, 128])
        gv_col = sb("gv_col", [128, 1])
        bv_col = sb("bv_col", [128, 1])
        d_blk = sb("d_blk", [128, BLOCK], I32)
        d_nxt = sb("d_nxt", [128, BLOCK], I32)
        d_cmp = sb("d_cmp", [128, BLOCK])
        d_row = [sb(f"d_row{k}", [128, BLOCK], I32) for k in range(2)]
        heads = sb("heads", [128, 128])
        p_t = sb("p_t", [128, 24])
        blk_i = sb("blk_i", [128, 2], I32)
        off_row = sb("off_row", [1, TILES + 4], I32)
        ok_col = sb("ok_col", [128, 2])
        u_src = sb("u_src", [128, 1], I32)
        u_dst = sb("u_dst", [128, 1], I32)
        u_w = sb("u_w", [128, 1])
        u_row = sb("u_row", [128, R], I32)
        u_eq = sb("u_eq", [128, R])
        u_low = sb("u_low", [128, R])
        u_t = sb("u_t", [128, 4])
        u_idx = sb("u_idx", [128, 1], I32)
        u_g = sb("u_g", [128, D])
        u_gw = sb("u_gw", [128, D])
        u_r = sb("u_r", [128, D])
        a_x = [sb(f"a_x{b}", [128, 2, D]) for b in range(2)]
        a_n = [sb(f"a_n{b}", [128, 2, D]) for b in range(2)]
        a_st = [sb(f"a_st{b}", [128, 2, 3]) for b in range(2)]
        a_ve = [sb(f"a_ve{b}", [128, 2]) for b in range(2)]
        a_rs = [sb(f"a_rs{b}", [128, 2]) for b in range(2)]
        k_x = [sb(f"k_x{b}", [128, D]) for b in range(K_RING)]
        k_t = [sb(f"k_t{b}", [128, 2, R]) for b in range(2)]
        k_sq = sb("k_sq", [128, 2 * D])
        k_ss = sb("k_ss", [128, 8])
        k_ve = [sb(f"k_ve{b}", [128, 8]) for b in range(2)]
        k_rs = [sb(f"k_rs{b}", [128, 8]) for b in range(2)]
        k_n = [sb(f"k_n{b}", [128, 2 * D]) for b in range(2)]
        k_sum = sb("k_sum", [128, 2 * D])
        sv = sb("sv", [128, 2])
        kv_t = sb("kv_t", [128, 2, 128])
        kv_a = sb("kv_a", [128, 128])
        kv_b = sb("kv_b", [128, 128])
        t1 = sb("t1", [128, 2, D])
        src_cur = sb("src_cur", [128, KC], I32)
        dst_cur = sb("dst_cur", [128, KC], I32)
        w_cur = sb("w_cur", [128, KC])
        d_loc = sb("d_loc", [128, KC])
        w_loc = sb("w_loc", [128, KC])
        gat = [sb(f"gat{c}", [128, D]) for c in range(KC)]
        hot = [sb(f"hot{c}", [128, R]) for c in range(KC)]
        g_x = sb("g_x", [128, D])
        g_u = sb("g_u", [128, D])
        g_agg = sb("g_agg", [128, D])
        g_out = sb("g_out", [128, D])
        xb_t = sb("xb_t", [128, 2, R])
        x_n = sb("x_n", [128, D])
        x_a = sb("x_a", [128, D])
        x_1 = sb("x_1", [128, D])
        x_h = sb("x_h", [128, D])
        x_st = sb("x_st", [128, 6])
        x_mv = sb("x_mv", [128, 2])
        x_ve = sb("x_ve", [128, 1])
        x_rs = sb("x_rs", [128, 1])
        H = [sb(f"H{q}", [128, 2, D]) for q in range(PAIRS)]
        T = [sb(f"T{q}", [128, 2, D]) for q in range(PAIRS)]
        O = [sb(f"O{q}", [128, 2, D]) for q in range(PAIRS)]
        h_next = [sb(f"h_next{q}", [128, 2, D]) for q in range(PAIRS)]
        x_cur = [sb(f"x_cur{q}", [128, 2, D]) for q in range(PAIRS)]
        st = [sb(f"st{q}", [128, 2, 3]) for q in range(PAIRS)]
        ve = [sb(f"ve{q}", [128, 2]) for q in range(PAIRS)]
        rs = [sb(f"rs{q}", [128, 2]) for q in range(PAIRS)]
        v_t = [sb(f"v_t{b}", [128, 2, 2, R]) for b in range(3)]

        banks = [ctx.enter_context(nc.psum_tensor(f"bank{b}", [128, 512], F32)) for b in range(8)]
        TR = banks[0:3]
        MM = banks[3:6]
        AGG = banks[6]
        XB = banks[7]
        K_TR, K_MM = banks[0:2], banks[3:5]
        K_ACC = [banks[2], banks[5]]
        dst_blocks = dst.rearrange("(b k) -> b k", k=BLOCK)

        block = ctx.enter_context(nc.Block())

        def carry(eng):
            eng.sem_inc(S("passed"), 1)

        def trips_of_f(eng, body):
            with eng.Fori(0, G_ROUNDS) as r:
                with eng.Fori(r * TRIPS, r * TRIPS + (TRIPS - 1)) as t:
                    body(t, r, False, True, True, False)
                body(r * TRIPS + (TRIPS - 1), r, True, True, True, False)
            for r in range(G_ROUNDS, ROUNDS):
                with eng.Fori(r * TRIPS, r * TRIPS + (TRIPS - 1)) as t:
                    body(t, r, False, False, r < ROUNDS - 1, False)
                body(r * TRIPS + TRIPS - 1, r, True, False, r < ROUNDS - 1, r == ROUNDS - 1)

        def x_use(t, g):
            return t * 2 + (EARLY_G + EARLY_X) if g else t + (TILES + EARLY_X)

        def g_use(t):
            return t * 2 + (EARLY_G + EARLY_X + 1)

        @block.sync
        def _(sp):
            sp.dma_start(d_blk[0:BLOCKS, :], dst_blocks).then_inc(S("dst_loaded"), 16)
            sp.wait_ge(S("dst_next_filled"), 1)
            sp.dma_start(d_nxt[0:BLOCKS - 1, :], dst[1:1 + (BLOCKS - 1) * BLOCK].rearrange("(b k) -> b k", k=BLOCK)).then_inc(S("dst_loaded"), 16)
            sp.dma_start(d_nxt[BLOCKS - 1:BLOCKS, 0:BLOCK - 1], dst[(BLOCKS - 1) * BLOCK + 1:E].unsqueeze(0)).then_inc(S("dst_loaded"), 16)
            for t, a in ((w_kv[:, :, 0:D], wk_t), (w_kv[:, :, D:2 * D], wv_t), (w_agg[:], w_gnn), (w_wq[:], wq),
                         (w_wo[:], wo_t), (w_raw[:], wf_t)):
                sp.dma_start(t, a.rearrange("(b p) n -> p b n", p=128)).then_inc(S("weights_loaded"), 16)
            sp.dma_start(c_row[:], bf.partition_broadcast(128)).then_inc(S("weights_loaded"), 16)
            sp.dma_start(bo_row[:], bo.partition_broadcast(128)).then_inc(S("weights_loaded"), 16)
            for b in range(2):
                sp.dma_start(lnw_c[:, b:b + 1], ln_w[b * 128:(b + 1) * 128].unsqueeze(1)).then_inc(S("weights_loaded"), 16)
                sp.dma_start(lnb_c[:, b:b + 1], ln_b[b * 128:(b + 1) * 128].unsqueeze(1)).then_inc(S("weights_loaded"), 16)
                sp.dma_start(gk_row[:, b * HD:(b + 1) * HD], gk.partition_broadcast(128)).then_inc(S("weights_loaded"), 16)
                sp.dma_start(bk_row[:, b * HD:(b + 1) * HD], bk.partition_broadcast(128)).then_inc(S("weights_loaded"), 16)
                sp.dma_start(gv_col[b * HD:(b + 1) * HD, :], gv.unsqueeze(1)).then_inc(S("weights_loaded"), 16)
                sp.dma_start(bv_col[b * HD:(b + 1) * HD, :], bv.unsqueeze(1)).then_inc(S("weights_loaded"), 16)

            def a_load(p, b):
                sp.dma_start(a_x[b][0:R], rows(x, p * 2, 2)).then_inc(S(f"a_loaded{b}"), 16)

            a_load(0, 0)
            a_load(1, 1)
            with sp.Fori(0, TILES // 4 - 1) as i:
                for b in range(2):
                    sp.wait_ge(S("a_normed"), i * 2 + (b + 1))
                    a_load(i * 2 + (b + 2), b)

            sp.wait_ge(S("offsets_ready"), 1)
            n_u = sp.value_load(off_row[0:1, TILES:TILES + 1], min_val=1, max_val=E // UC)
            with sp.Fori(0, n_u) as i:
                sp.wait_ge(S("u_added"), i * 16)
                sp.dma_start(u_src[0:UC], src[bass.ds(i * UC, UC)].unsqueeze(1)).then_inc(S("u_loaded"), 16)
                sp.dma_start(u_dst[0:UC], dst[bass.ds(i * UC, UC)].unsqueeze(1)).then_inc(S("u_loaded"), 16)
                sp.dma_start(u_w[0:UC], ew[bass.ds(i * UC, UC)].unsqueeze(1)).then_inc(S("u_loaded"), 16)
                sp.dma_start(u_row[0:UC], dst[bass.ds(i * UC, UC)].partition_broadcast(UC)).then_inc(S("u_loaded"), 16)

            def g_load(j):
                for c in range(KC):
                    sp.wait_ge(S(f"gathered{c}"), j * 16)
                carry(sp)
                sp.wait_ge(S("edge_scalars_ready"), j * 2)
                off = sp.value_load(off_row[0:1, bass.ds(j, 1)], min_val=0, max_val=E - CAP)
                for t, a in ((src_cur, src), (dst_cur, dst), (w_cur, ew)):
                    sp.dma_start(t[:], a[bass.ds(off, CAP)].rearrange("(p k) -> p k", k=KC)).then_inc(S("edges_loaded"), 16)

            def g_rows(j):
                sp.wait_ge(S("messages_copied"), j)
                sp.dma_start(g_u[0:R], gen_d[bass.ds(j * R, R), :]).then_inc(S("g_rows_loaded"), 16)
                sp.wait_ge(S("g_done"), j)
                sp.dma_start(g_x[0:R], x[bass.ds(j * R, R), :]).then_inc(S("g_rows_loaded"), 16)

            def g_store(j):
                sp.wait_ge(S("g_done"), j + 1)
                sp.dma_start(x1a_d[bass.ds(j * R, R), :], g_out[0:R]).then_inc(S("g_stored"), 16)

            def x_load(i):
                sp.wait_ge(S("x_summed"), i)
                sp.wait_ge(S("g_stored"), i * 16 + 16)
                sp.dma_start(x_n[0:R], xn_d[bass.ds(i * R, R), :]).then_inc(S("x_rows_loaded"), 16)
                sp.dma_start(x_a[0:R], x1a_d[bass.ds(i * R, R), :]).then_inc(S("x_rows_loaded"), 16)

            def x_store(i):
                sp.wait_ge(S("x_summed"), i + 1)
                sp.dma_start(x1_d[bass.ds(i * R, R), :], x_1[0:R]).then_inc(S("x_sum_stored"), 16)
                sp.wait_ge(S("x_normed"), i + 1)
                sp.dma_start(h0_d[bass.ds(i * R, R), :], x_h[0:R]).then_inc(S("x_h_stored"), 16)

            def load_h(r):
                sp.wait_ge(S("h_next_used"), r * PAIRS)
                carry(sp)
                sp.wait_ge(S("x_h_stored"), (r + 1) * (ROUND * 16))
                for q in range(PAIRS):
                    sp.dma_start(h_next[q][0:R], rows(h0_d, r * ROUND + 2 * q, 2)).then_inc(S(f"h_next_loaded{q}"), 16)

            def load_x(r):
                sp.wait_ge(S("out_ready"), r * PAIRS)
                carry(sp)
                sp.wait_ge(S("x_sum_stored"), (r + 1) * (ROUND * 16))
                for q in range(PAIRS):
                    sp.dma_start(x_cur[q][0:R], rows(x1_d, r * ROUND + 2 * q, 2)).then_inc(S(f"x_cur_loaded{q}"), 16)

            for b in range(2):
                sp.wait_ge(S(f"a_stored{b}"), 16 * (TILES // 4))
            sp.wait_ge(S("u_added"), n_u * 16)

            def k_load(t, b):
                sp.dma_start(k_x[b][0:R], xn_d[bass.ds(t * R, R), :]).then_inc(S(f"k_loaded{b}"), 16)

            for b in range(K_RING):
                k_load(b, b)

            def b_trip(i, last):
                for s in range(KV_STEPS):
                    t = i * KV_STEPS + s
                    for g in range(2):
                        if B_G[g].first == s:
                            g_load(i * 2 + g)
                    if s == 0:
                        g_rows(i * 2)
                    if not (last and s + K_RING >= KV_STEPS):
                        sp.wait_ge(S("k_transposed"), t + 1)
                        k_load(t + K_RING, s % K_RING)
                    if s == B_G[0].read + 1:
                        g_store(i * 2)
                        g_rows(i * 2 + 1)
                    if s == B_G[1].read:
                        g_store(i * 2 + 1)

            with sp.Fori(0, LAST_B) as i:
                b_trip(i, False)
            b_trip(LAST_B, True)

            with sp.Fori(0, EARLY_X) as i:
                x_load(i)
                x_store(i)
            load_h(0)

            def f_trip(t, r, end, g, xx, last):
                if g:
                    g_load(t + EARLY_G)
                    g_rows(t + EARLY_G)
                if xx:
                    x_load(t + EARLY_X)
                if end:
                    load_x(r)
                if xx:
                    x_store(t + EARLY_X)
                if end and not last:
                    load_h(r + 1)
                if g:
                    g_store(t + EARLY_G)
                if end:
                    for q in range(PAIRS):
                        sp.wait_ge(S("out_ready"), r * PAIRS + (q + 1))
                        sp.dma_start(rows(out, r * ROUND + 2 * q, 2), O[q][0:R]).then_inc(S(f"out_stored{q}"), 16)

            trips_of_f(sp, f_trip)
            for q in range(PAIRS):
                sp.wait_ge(S(f"out_stored{q}"), 16 * ROUNDS)
            sp.wait_ge(S("zeroed"), 16 * (TILES // 2 + 1))

        @block.gpsimd
        def _(pool):
            pool.memset(d_nxt[:], 1 << 20).then_inc(S("dst_next_filled"), 1)
            pool.memset(ident[:], 0.0).then_inc(S("pool_own"), 1)
            pool.memset(below[:], 0.0).then_inc(S("pool_own"), 1)
            pool.iota(iota_i[:], pattern=[[1, R]], base=0, channel_multiplier=0).then_inc(S("iotas_made"), 1)
            pool.iota(base_i[:], pattern=[[R, TILES]], base=0, channel_multiplier=0).then_inc(S("iotas_made"), 1)
            pool.iota(lane_i[:, 0:1], pattern=[[0, 1]], base=N, channel_multiplier=1).then_inc(S("iotas_made"), 1)
            pool.iota(lane_i[:, 1:3], pattern=[[R, 2]], base=0, channel_multiplier=R).then_inc(S("iotas_made"), 1)
            pool.wait_ge(S("pool_own"), 2)
            pool.affine_select(out=ident[:], in_=ident[:], compare_op=ALU.not_equal, fill=1.0, base=0,
                               pattern=[[-1, 128]], channel_multiplier=1).then_inc(S("masks_made"), 1)
            pool.affine_select(out=below[:], in_=below[:], compare_op=ALU.is_ge, fill=1.0, base=0,
                               pattern=[[1, R]], channel_multiplier=-1).then_inc(S("masks_made"), 1)
            pool.wait_ge(S("blocks_found"), 1)
            for k in range(2):
                pool.indirect_dma_start(d_row[k][0:TILES, :], None, dst_blocks,
                                        bass.IndirectOffsetOnAxis(ap=blk_i[0:TILES, k:k + 1], axis=0)).then_inc(S("blocks_gathered"), 16)

            def rstd(out_, var, n, after, value, done):
                pool.wait_ge(S(after), value)
                pool.tensor_tensor(out_, var, minus_half[0:R, 0:n], ALU.pow).then_inc(S(done), 1)

            with pool.Fori(0, TILES // 4) as i:
                for b in range(2):
                    rstd(a_rs[b][0:R], a_ve[b][0:R], 2, "a_variance", i * 2 + (b + 1), "a_rstd")

            for b in range(2):
                pool.wait_ge(S(f"a_stored{b}"), 16 * (TILES // 4))
            pool.wait_ge(S("zeroed"), 16 * (TILES // 2 + 1))
            pool.wait_ge(S("offsets_ready"), 1)
            n_u = pool.value_load(off_row[0:1, TILES:TILES + 1], min_val=1, max_val=E // UC)
            with pool.Fori(0, n_u) as i:
                pool.wait_ge(S("u_loaded"), i * 64 + 64)
                carry(pool)
                pool.indirect_dma_start(u_g[0:UC, :], None, xn_d,
                                        bass.IndirectOffsetOnAxis(ap=u_src[0:UC, 0:1], axis=0)).then_inc(S("u_gathered"), 16)
                pool.wait_ge(S("u_rows_ready"), i + 1)
                carry(pool)
                pool.indirect_dma_start(gen_d, bass.IndirectOffsetOnAxis(ap=u_idx[0:UC, 0:1], axis=0), u_r[0:UC, :], None,
                                        compute_op=ALU.add).then_inc(S("u_added"), 16)
                pool.wait_ge(S("u_added"), i * 16 + 16)

            def gather(j, c):
                if c == 0:
                    pool.wait_ge(S("edges_loaded"), j * 48 + 48)
                pool.wait_ge(S("chunks_multiplied"), j * KC + (c + 1))
                carry(pool)
                pool.indirect_dma_start(gat[c][:], None, xn_d, bass.IndirectOffsetOnAxis(ap=src_cur[:, c:c + 1], axis=0)).then_inc(S(f"gathered{c}"), 16)

            rstd(k_rs[0][0:R], k_ve[0][0:R], 8, "k_variance", 1, "k_rstd")

            def b_trip(i, last):
                for s in range(KV_STEPS):
                    for g in range(2):
                        for c in B_G[g].gather[s]:
                            gather(i * 2 + g, c)
                    if not (last and s + 1 >= KV_STEPS):
                        b = (s + 1) % 2
                        rstd(k_rs[b][0:R], k_ve[b][0:R], 8, "k_variance", i * KV_STEPS + (s + 2), "k_rstd")

            with pool.Fori(0, LAST_B) as i:
                b_trip(i, False)
            b_trip(LAST_B, True)

            def x_rstd(i):
                rstd(x_rs[0:R], x_ve[0:R], 1, "x_variance", i + 1, "x_rstd")

            with pool.Fori(0, EARLY_X) as i:
                x_rstd(i)

            def f_rstd(n, q):
                rstd(rs[q][0:R], ve[q][0:R], 2, "variance", n + 1, "rstd")

            f_rstd(0, 0)
            f_rstd(1, 1)

            def f_trip(t, r, end, g, xx, last):
                for s in range(SLOTS):
                    if g:
                        for c in F_G.gather[s]:
                            gather(t + EARLY_G, c)
                    if not (last and s + 2 >= SLOTS):
                        f_rstd(t * SLOTS + (s + 2), (s + 2) % PAIRS)
                    if xx and s == X_VAR:
                        x_rstd(t + EARLY_X)

            trips_of_f(pool, f_trip)

        @block.scalar
        def _(act):
            act.wait_ge(S("zeros_made"), 1)
            with act.Fori(0, TILES // 2) as i:
                act.dma_start(rows(gen_d, i * 2, 2), zeros[0:R]).then_inc(S("zeroed"), 16)
            act.dma_start(gen_d[N:N + R, :], zeros[0:R, 0, :]).then_inc(S("zeroed"), 16)
            with act.Fori(0, TILES // 4) as i:
                for b in range(2):
                    act.wait_ge(S("a_normed"), i * 2 + (b + 1))
                    act.dma_start(rows(xn_d, i * 4 + 2 * b, 2), a_n[b][0:R]).then_inc(S(f"a_stored{b}"), 16)

            def xb_copy(v):
                act.wait_ge(S("xb_transposed"), v + 1)
                nc.scalar.activation(xb_t[:].rearrange("p b r -> p (b r)"), XB[:, 0:2 * R], ACT.Copy).then_inc(S("xb_copied"), 1)

            def k_copy(t, b):
                act.wait_ge(S("k_transposed"), t + 1)
                nc.scalar.activation(k_t[b][:].rearrange("p b r -> p (b r)"), K_TR[b][:, 0:2 * R], ACT.Copy).then_inc(S("k_copied"), 1)

            def k_square(t, b):
                act.wait_ge(S("k_projected"), t + 1)
                act.wait_ge(S("k_squares_summed"), t)
                nc.scalar.activation(k_sq[0:R], K_MM[b][0:R, :], ACT.Square).then_inc(S("k_squared"), 1)

            k_copy(0, 0)
            k_copy(1, 1)
            k_square(0, 0)

            def b_trip(i, last):
                for s in range(KV_STEPS):
                    t = i * KV_STEPS + s
                    if not (last and s + 2 >= KV_STEPS):
                        k_copy(t + 2, s % 2)
                    if not (last and s + 1 >= KV_STEPS):
                        k_square(t + 1, (s + 1) % 2)
                    for g in range(2):
                        if B_G[g].transpose == s:
                            xb_copy(i * 2 + g)

            with act.Fori(0, LAST_B) as i:
                b_trip(i, False)
            b_trip(LAST_B, True)

            with act.Fori(0, EARLY_X) as i:
                xb_copy(i + EARLY_G)

            def tanh(n, q):
                act.wait_ge(S("h_ready"), n + 1)
                nc.scalar.activation(T[q][0:R], H[q][0:R], ACT.Tanh).then_inc(S("tanh_done"), 1)

            def silu(n, q):
                act.wait_ge(S("u_done"), n + 1)
                nc.scalar.activation(T[q][0:R], T[q][0:R], ACT.Silu).then_inc(S("silu_done"), 1)

            def copy_t(n, b, last):
                if last:
                    act.wait_ge(S("multiplied"), n - 2)
                act.wait_ge(S("transposed"), n + 1)
                nc.scalar.activation(v_t[b][:].rearrange("p t b r -> p (t b r)"), TR[b][:, 0:4 * R], ACT.Copy).then_inc(S("transposed_copied"), 1)

            tanh(0, 0)
            tanh(1, 1)
            silu(0, 0)
            tanh(2, 2)
            silu(1, 1)
            copy_t(0, 0, False)
            tanh(3, 3)
            silu(2, 2)

            def f_trip(t, r, end, g, xx, last):
                for s in range(SLOTS):
                    n = t * SLOTS + s
                    if not (last and s + 1 >= SLOTS):
                        copy_t(n + 1, (s + 1) % 3, last)
                    if not (last and s + 4 >= SLOTS):
                        tanh(n + 4, (s + 4) % PAIRS)
                    if not (last and s + 3 >= SLOTS):
                        silu(n + 3, (s + 3) % PAIRS)
                    if xx and s == X_TRANSPOSE:
                        xb_copy(x_use(t, g))
                    if g and s == F_G.transpose:
                        xb_copy(g_use(t))

            trips_of_f(act, f_trip)

        @block.vector
        def _(dve):
            count = [0]

            def link(ins):
                count[0] += 1
                ins.then_inc(S("vector_own"), 1)
                dve.wait_ge(S("vector_own"), count[0])

            v = nc.vector
            v.memset(zeros[:], 0.0).then_inc(S("zeros_made"), 1)
            v.memset(ones[:], 1.0).then_inc(S("ones_made"), 1)
            v.memset(minus_half[:], -0.5).then_inc(S("vector_const"), 1)
            v.memset(k_sum[:], 0.0).then_inc(S("vector_const"), 1)
            v.memset(kv_t[:], 0.0).then_inc(S("vector_const"), 1)
            v.memset(p_t[:], 0.0).then_inc(S("vector_const"), 1)
            dve.wait_ge(S("iotas_made"), 4)
            v.tensor_copy(iota_f[:], iota_i[:]).then_inc(S("vector_const"), 1)
            v.tensor_copy(base_f[:], base_i[:]).then_inc(S("vector_const"), 1)
            v.tensor_copy(lane_f[:], lane_i[:]).then_inc(S("vector_const"), 1)
            dve.wait_ge(S("vector_const"), 7)

            dve.wait_ge(S("dst_loaded"), 48)
            dve.wait_ge(S("masks_made"), 2)
            link(v.tensor_copy(p_t[0:BLOCKS, 12:13], d_blk[0:BLOCKS, 0:1]))
            v.tensor_scalar(heads[0:BLOCKS, 0:BLOCKS], ident[0:BLOCKS, 0:BLOCKS], p_t[0:BLOCKS, 12:13], None, ALU.mult).then_inc(S("heads_ready"), 1)
            link(v.tensor_tensor(d_cmp[0:BLOCKS, :], d_nxt[0:BLOCKS, :], d_blk[0:BLOCKS, :], ALU.is_lt))
            link(v.tensor_reduce(p_t[0:BLOCKS, 9:10], d_cmp[0:BLOCKS, :], AX_X, ALU.add))
            dve.wait_ge(S("heads_spread"), 1)
            for k in range(2):
                link(v.tensor_scalar(d_cmp[0:TILES, 0:BLOCKS], XB[0:TILES, 0:BLOCKS], lane_f[0:TILES, 1 + k:2 + k], None, ALU.is_lt))
                link(v.tensor_reduce(p_t[0:TILES, k:k + 1], d_cmp[0:TILES, 0:BLOCKS], AX_X, ALU.add))
            link(v.tensor_scalar(p_t[0:TILES, 2:4], p_t[0:TILES, 0:2], -1.0, 0.0, ALU.add, ALU.max))
            v.tensor_copy(blk_i[0:TILES, :], p_t[0:TILES, 2:4]).then_inc(S("blocks_found"), 1)
            dve.wait_ge(S("blocks_gathered"), 32)
            for k in range(2):
                link(v.tensor_scalar(d_cmp[0:TILES, :], d_row[k][0:TILES, :], lane_f[0:TILES, 1 + k:2 + k], None, ALU.is_lt))
                link(v.tensor_reduce(p_t[0:TILES, 4 + k:5 + k], d_cmp[0:TILES, :], AX_X, ALU.add))
            link(v.scalar_tensor_tensor(out=p_t[0:TILES, 6:8], in0=p_t[0:TILES, 2:4], scalar=float(BLOCK), in1=p_t[0:TILES, 4:6], op0=ALU.mult, op1=ALU.add))
            link(v.tensor_tensor(p_t[0:TILES, 8:9], p_t[0:TILES, 7:8], p_t[0:TILES, 6:7], ALU.subtract))
            link(v.tensor_scalar(p_t[0:TILES, 8:9], p_t[0:TILES, 8:9], float(CAP), None, ALU.is_gt))
            link(v.tensor_tensor(p_t[0:BLOCKS, 9:10], p_t[0:BLOCKS, 9:10], p_t[0:BLOCKS, 8:9], ALU.add))
            link(v.tensor_scalar(p_t[0:TILES, 10:11], p_t[0:TILES, 6:7], float(E - CAP), None, ALU.min))
            v.tensor_scalar(heads[0:TILES, 0:TILES], ident[0:TILES, 0:TILES], p_t[0:TILES, 10:11], None, ALU.mult).then_inc(S("windows_ready"), 1)
            dve.wait_ge(S("windows_spread"), 1)
            v.tensor_copy(off_row[0:1, 0:TILES], XB[0:1, 128:128 + TILES]).then_inc(S("vector_own2"), 1)
            link(v.tensor_scalar(ok_col[:, 1:2], XB[:, 256:257], 1.0, None, ALU.min))
            link(v.tensor_scalar(ok_col[:, 0:1], ok_col[:, 1:2], -1.0, 1.0, ALU.mult, ALU.add))
            dve.wait_ge(S("vector_own2"), 1)
            v.tensor_scalar(off_row[0:1, TILES:TILES + 1], ok_col[0:1, 1:2], float(E // UC - 1), 1.0, ALU.mult, ALU.add).then_inc(S("offsets_ready"), 1)

            dve.wait_ge(S("weights_loaded"), 20 * 16)
            for b in range(2):
                heads_of = w_kv[:, b, :].rearrange("p (h d) -> p h d", d=HD)
                link(v.tensor_reduce(w_mean[:, b, :], heads_of, AX_X, ALU.add))
                link(v.tensor_scalar(w_mean[:, b, :], w_mean[:, b, :], 1.0 / HD, None, ALU.mult))
                v.tensor_tensor(heads_of, heads_of, w_mean[:, b, :].unsqueeze(2).broadcast_to([128, 8, HD]), ALU.subtract).then_inc(S("w_kv_ready"), 1)
            for b in range(2):
                link(v.tensor_scalar(w_ffn[:, b, :], w_raw[:, b, :], lnw_c[:, b:b + 1], None, ALU.mult))
                link(v.tensor_scalar(lnb_b[:, b, :], ones[:], lnb_c[:, b:b + 1], None, ALU.mult))
            v.memset(p_t[:, 20:21], 0.0).then_inc(S("w_scaled"), 1)
            dve.wait_ge(S("w_summed"), 1)
            for b in range(2):
                link(v.scalar_tensor_tensor(out=w_ffn[:, b, :], in0=AGG[:, 0:D], scalar=-1.0 / D, in1=w_ffn[:, b, :], op0=ALU.mult, op1=ALU.add))
            link(v.tensor_tensor(c_row[:], XB[:, 0:D], c_row[:], ALU.add))
            v.memset(p_t[:, 21:22], 0.0).then_inc(S("w_ffn_ready"), 1)

            def a_bn(i, b):
                dve.wait_ge(S(f"a_loaded{b}"), i * 16 + 16)
                v.bn_stats(a_st[b][0:R].rearrange("p t k -> p (t k)"), a_x[b][0:R].rearrange("p t f -> p f t")).then_inc(S("a_stats"), 1)

            def a_var(i, b):
                dve.wait_ge(S("a_stats"), i * 2 + (b + 1))
                v.tensor_scalar(a_ve[b][0:R], a_st[b][0:R, :, 2], 1.0 / D, EPS, ALU.mult, ALU.add).then_inc(S("a_variance"), 1)

            def a_norm(i, b):
                dve.wait_ge(S("a_rstd"), i * 2 + (b + 1))
                dve.wait_ge(S(f"a_stored{b}"), i * 16)
                for t in range(2):
                    last = v.tensor_scalar(a_n[b][0:R, t, :], a_x[b][0:R, t, :], a_st[b][0:R, t, 1:2], a_rs[b][0:R, t:t + 1], ALU.subtract, ALU.mult)
                last.then_inc(S("a_normed"), 1)

            a_bn(0, 0)
            a_var(0, 0)
            with dve.Fori(0, TILES // 4 - 1) as i:
                a_bn(i, 1)
                a_var(i, 1)
                a_norm(i, 0)
                a_bn(i + 1, 0)
                a_var(i + 1, 0)
                a_norm(i, 1)
            a_bn(TILES // 4 - 1, 1)
            a_var(TILES // 4 - 1, 1)
            a_norm(TILES // 4 - 1, 0)
            a_norm(TILES // 4 - 1, 1)

            dve.wait_ge(S("offsets_ready"), 1)
            n_u = dve.value_load(off_row[0:1, TILES:TILES + 1], min_val=1, max_val=E // UC)
            with dve.Fori(0, n_u) as i:
                def u_link(ins, name):
                    ins.then_inc(S(name), 1)
                    dve.wait_ge(S(name), i + 1)

                dve.wait_ge(S("u_loaded"), i * 64 + 64)
                u_link(v.tensor_copy(u_t[0:UC, 0:1], u_dst[0:UC]), "u_dst_float")
                u_link(v.tensor_scalar(u_t[0:UC, 1:2], u_w[0:UC], ok_col[0:UC, 1:2], None, ALU.mult), "u_weight")
                u_link(v.tensor_scalar(u_eq[0:UC], u_row[0:UC], u_t[0:UC, 0:1], None, ALU.is_equal), "u_equal")
                u_link(v.tensor_tensor(u_low[0:UC], u_eq[0:UC], below[0:UC], ALU.mult), "u_earlier")
                u_link(v.tensor_reduce(u_t[0:UC, 2:3], u_low[0:UC], AX_X, ALU.max), "u_repeated")
                u_link(v.tensor_tensor(u_t[0:UC, 3:4], lane_f[0:UC, 0:1], u_t[0:UC, 0:1], ALU.subtract), "u_to_spare")
                u_link(v.tensor_tensor(u_t[0:UC, 3:4], u_t[0:UC, 3:4], u_t[0:UC, 2:3], ALU.mult), "u_shift")
                u_link(v.tensor_tensor(u_t[0:UC, 3:4], u_t[0:UC, 3:4], u_t[0:UC, 0:1], ALU.add), "u_row_number")
                u_link(v.tensor_copy(u_idx[0:UC], u_t[0:UC, 3:4]), "u_index")
                dve.wait_ge(S("u_gathered"), i * 16 + 16)
                v.tensor_scalar(u_gw[0:UC], u_g[0:UC], u_t[0:UC, 1:2], None, ALU.mult).then_inc(S("u_weighted"), 1)
                dve.wait_ge(S("u_multiplied"), i + 1)
                v.tensor_copy(u_r[0:UC], XB[0:UC, 0:D]).then_inc(S("u_rows_ready"), 1)

            def g_scalars(j):
                dve.wait_ge(S("edges_loaded"), j * 48 + 48)
                dve.wait_ge(S("hot_ready"), j * KC)
                v.tensor_scalar(d_loc[:], dst_cur[:], base_f[:, bass.ds(j, 1)], None, ALU.subtract).then_inc(S("edge_scalars_ready"), 1)
                v.tensor_scalar(w_loc[:], w_cur[:], ok_col[:, 0:1], None, ALU.mult).then_inc(S("edge_scalars_ready"), 1)

            def g_hot(j, c):
                if c == 0:
                    dve.wait_ge(S("edge_scalars_ready"), j * 2 + 2)
                dve.wait_ge(S("chunks_multiplied"), j * KC + (c + 1))
                v.tensor_scalar(hot[c][:], iota_f[:], d_loc[:, c:c + 1], w_loc[:, c:c + 1], ALU.is_equal, ALU.mult).then_inc(S("hot_ready"), 1)

            def g_copy(j):
                dve.wait_ge(S("g_rows_loaded"), j * 32 + 32)
                dve.wait_ge(S("chunks_multiplied"), j * KC + 2 * KC)
                v.tensor_tensor(g_agg[0:R], AGG[0:R, 0:D], g_u[0:R], ALU.add).then_inc(S("messages_copied"), 1)

            def g_read(j, use):
                dve.wait_ge(S("g_stored"), j * 16)
                dve.wait_ge(S("xb_multiplied"), use + 1)
                v.scalar_tensor_tensor(out=g_out[0:R], in0=XB[0:R, 0:D], scalar=0.0, in1=g_x[0:R], op0=ALU.max, op1=ALU.add).then_inc(S("g_done"), 1)

            def k_stats(t, b):
                dve.wait_ge(S("k_squared"), t + 1)
                v.tensor_reduce(k_ss[0:R], k_sq[0:R].rearrange("p (h d) -> p h d", d=HD), AX_X, ALU.add).then_inc(S("k_squares_summed"), 1)
                dve.wait_ge(S("k_squares_summed"), t + 1)
                v.tensor_scalar(k_ve[b][0:R], k_ss[0:R], 1.0 / HD, EPS, ALU.mult, ALU.add).then_inc(S("k_variance"), 1)

            def k_norm(t, b, outers):
                dve.wait_ge(S("k_rstd"), t + 1)
                if outers is not None:
                    dve.wait_ge(S("k_outer_done"), outers)
                v.tensor_tensor(k_n[b][0:R].rearrange("p (h d) -> p h d", d=HD), K_MM[b][0:R].rearrange("p (h d) -> p h d", d=HD),
                                k_rs[b][0:R].unsqueeze(2).broadcast_to([R, 8, HD]), ALU.mult).then_inc(S("k_normed"), 1)
                dve.wait_ge(S("k_normed"), t + 1)
                dve.wait_ge(S("k_added"), t)
                v.tensor_tensor(k_sum[0:R], k_sum[0:R], k_n[b][0:R], ALU.add).then_inc(S("k_added"), 1)

            k_stats(0, 0)
            k_norm(0, 0, None)

            def b_trip(i, last):
                for s in range(KV_STEPS):
                    t = i * KV_STEPS + s
                    more = not (last and s + 1 >= KV_STEPS)
                    if more:
                        k_stats(t + 1, (s + 1) % 2)
                    for g in range(2):
                        if B_G[g].first == s:
                            g_scalars(i * 2 + g)
                        for c in B_G[g].hot[s]:
                            g_hot(i * 2 + g, c)
                    if more:
                        k_norm(t + 1, (s + 1) % 2, t)
                    for g in range(2):
                        if B_G[g].copy == s:
                            g_copy(i * 2 + g)
                        if B_G[g].read == s:
                            g_read(i * 2 + g, i * 2 + g)

            with dve.Fori(0, LAST_B) as i:
                b_trip(i, False)
            b_trip(LAST_B, True)

            dve.wait_ge(S("k_outer_done"), TILES)
            dve.wait_ge(S("sums_spread"), 1)
            for hp in range(2):
                link(v.tensor_copy(sv[:, hp:hp + 1], XB[:, 256 + hp:257 + hp]))
                link(v.tensor_tensor(kv_a[:], K_ACC[hp][:, 0:128], gk_row[:], ALU.mult))
                link(v.tensor_scalar(kv_b[:], bk_row[:], sv[:, hp:hp + 1], None, ALU.mult))
                link(v.tensor_tensor(kv_a[:], kv_a[:], kv_b[:], ALU.add))
                link(v.tensor_scalar(kv_a[:], kv_a[:], gv_col[:, 0:1], None, ALU.mult))
                link(v.tensor_tensor(kv_b[:], XB[:, hp * 128:(hp + 1) * 128], gk_row[:], ALU.mult))
                link(v.scalar_tensor_tensor(out=kv_b[:], in0=bk_row[:], scalar=float(N), in1=kv_b[:], op0=ALU.mult, op1=ALU.add))
                link(v.tensor_scalar(kv_b[:], kv_b[:], bv_col[:, 0:1], None, ALU.mult))
                link(v.tensor_tensor(kv_a[:], kv_a[:], kv_b[:], ALU.add))
                for h in range(2):
                    part = slice(h * HD, (h + 1) * HD)
                    v.tensor_scalar(kv_t[part, hp, part], kv_a[part, part], 1.0 / N, None, ALU.mult).then_inc(S("kv_ready"), 1)
                dve.wait_ge(S("kv_ready"), 2 * hp + 2)
            for hp in range(2):
                dve.wait_ge(S("kv_wo_done"), hp + 1)
                v.tensor_copy(t1[:, hp, :], (AGG, XB)[hp][:, 0:D]).then_inc(S("kv_wo_copied"), 1)
            for b in range(2):
                dve.wait_ge(S("mix_done"), b + 1)
                v.tensor_copy(w_mix[:, b, :], K_TR[b][:, 0:D]).then_inc(S("mix_copied"), 1)

            def x_bias(i):
                dve.wait_ge(S("x_rows_loaded"), i * 32 + 32)
                v.tensor_tensor(x_a[0:R], x_a[0:R], bo_row[0:R], ALU.add).then_inc(S("x_biased"), 1)

            def x_read(i, use):
                dve.wait_ge(S("x_sum_stored"), i * 16)
                dve.wait_ge(S("x_biased"), i + 1)
                dve.wait_ge(S("xb_multiplied"), use + 1)
                v.tensor_tensor(x_1[0:R], XB[0:R, 0:D], x_a[0:R], ALU.add).then_inc(S("x_summed"), 1)

            def x_stats(i):
                dve.wait_ge(S("x_summed"), i + 1)
                v.bn_stats(x_st[0:R], x_1[0:R]).then_inc(S("x_stats"), 1)

            def x_mean(i):
                dve.wait_ge(S("x_stats"), i + 1)
                carry(dve)
                v.bn_aggr(x_mv[0:R], x_st[0:R]).then_inc(S("x_mean"), 1)

            def x_var(i):
                dve.wait_ge(S("x_mean"), i + 1)
                v.tensor_scalar(x_ve[0:R], x_mv[0:R, 1:2], EPS, None, ALU.add).then_inc(S("x_variance"), 1)

            def x_norm(i):
                dve.wait_ge(S("x_h_stored"), i * 16)
                dve.wait_ge(S("x_rstd"), i + 1)
                v.tensor_scalar(x_h[0:R], x_1[0:R], x_mv[0:R, 0:1], x_rs[0:R, 0:1], ALU.subtract, ALU.mult).then_inc(S("x_normed"), 1)

            with dve.Fori(0, EARLY_X) as i:
                x_bias(i)
                x_read(i, i + EARLY_G)
                x_stats(i)
                x_mean(i)
                x_var(i)
                x_norm(i)

            for q in range(PAIRS):
                dve.wait_ge(S(f"h_next_loaded{q}"), 16)
                v.tensor_copy(H[q][0:R], h_next[q][0:R]).then_inc(S("h_ready"), 1)
            dve.wait_ge(S("h_ready"), PAIRS)
            dve.sem_inc(S("h_next_used"), PAIRS)

            def f_sum(n, q):
                dve.wait_ge(S("tanh_done"), n + 1)
                v.scalar_tensor_tensor(out=T[q][0:R], in0=T[q][0:R], scalar=0.01, in1=H[q][0:R], op0=ALU.mult, op1=ALU.add).then_inc(S("u_done"), 1)

            def f_stats(n, q):
                dve.wait_ge(S("silu_done"), n + 1)
                v.bn_stats(st[q][0:R].rearrange("p t k -> p (t k)"), T[q][0:R].rearrange("p t f -> p f t")).then_inc(S("stats"), 1)

            def f_var(n, q):
                dve.wait_ge(S("stats"), n + 1)
                v.tensor_scalar(ve[q][0:R], st[q][0:R, :, 2], 1.0 / D, EPS, ALU.mult, ALU.add).then_inc(S("variance"), 1)

            def f_scale(n, q, b):
                dve.wait_ge(S("rstd"), n + 1)
                dve.wait_ge(S("multiplied"), n + 1)
                for t in range(2):
                    last = v.scalar_tensor_tensor(out=H[q][0:R, t, :], in0=MM[b][0:R, t * D:(t + 1) * D], scalar=rs[q][0:R, t:t + 1],
                                                  in1=c_row[0:R], op0=ALU.mult, op1=ALU.add)
                last.then_inc(S("h_ready"), 1)

            def f_end(n, q, b, r, last_round):
                dve.wait_ge(S(f"x_cur_loaded{q}"), r * 16 + 16)
                v.tensor_tensor(x_cur[q][0:R], x_cur[q][0:R], c_row[0:R].unsqueeze(1).broadcast_to([R, 2, D]), ALU.add).then_inc(S("c_added"), 1)
                dve.wait_ge(S("rstd"), n + 1)
                dve.wait_ge(S("multiplied"), n + 1)
                dve.wait_ge(S("c_added"), r * PAIRS + (q + 1))
                dve.wait_ge(S(f"out_stored{q}"), r * 16)
                for t in range(2):
                    o = v.scalar_tensor_tensor(out=O[q][0:R, t, :], in0=MM[b][0:R, t * D:(t + 1) * D], scalar=rs[q][0:R, t:t + 1],
                                               in1=x_cur[q][0:R, t, :], op0=ALU.mult, op1=ALU.add)
                o.then_inc(S("out_ready"), 1)
                if not last_round:
                    dve.wait_ge(S(f"h_next_loaded{q}"), r * 16 + 32)
                    v.tensor_copy(H[q][0:R], h_next[q][0:R]).then_inc(S("h_ready"), 1)

            f_sum(0, 0)
            f_sum(1, 1)
            f_stats(0, 0)
            f_var(0, 0)
            f_sum(2, 2)
            f_stats(1, 1)
            f_var(1, 1)

            def f_trip(t, r, end, g, xx, last):
                for s in range(SLOTS):
                    n = t * SLOTS + s
                    q = s % PAIRS
                    if not (last and s + 3 >= SLOTS):
                        f_sum(n + 3, (s + 3) % PAIRS)
                    if not (last and s + 2 >= SLOTS):
                        f_stats(n + 2, (s + 2) % PAIRS)
                    if g:
                        j = t + EARLY_G
                        if s == F_G.first:
                            g_scalars(j)
                        for c in F_G.hot[s]:
                            g_hot(j, c)
                    if xx:
                        i = t + EARLY_X
                        for at, part in ((X_BIAS, x_bias), (X_STATS, x_stats), (X_MEAN, x_mean), (X_VAR, x_var), (X_NORM, x_norm)):
                            if s == at:
                                part(i)
                    if end and s >= SLOTS - PAIRS:
                        f_end(n, q, s % 3, r, last)
                        if not last and s == SLOTS - 1:
                            dve.wait_ge(S("h_ready"), n + (1 + PAIRS))
                            dve.sem_inc(S("h_next_used"), PAIRS)
                    else:
                        f_scale(n, q, s % 3)
                    if not (last and s + 2 >= SLOTS):
                        f_var(n + 2, (s + 2) % PAIRS)
                    if xx and s == X_MULTIPLY:
                        x_read(t + EARLY_X, x_use(t, g))
                    if g and s == F_G.copy:
                        g_copy(t + EARLY_G)
                    if g and s == F_G.read:
                        g_read(t + EARLY_G, g_use(t))

            trips_of_f(dve, f_trip)

        @block.tensor
        def _(pe):
            mm, tp = nc.tensor.matmul, nc.tensor.transpose
            pe.sem_inc(S("chunks_multiplied"), KC)
            pe.wait_ge(S("ones_made"), 1)
            pe.wait_ge(S("heads_ready"), 1)
            mm(XB[:, 0:BLOCKS], ones[0:BLOCKS, :], heads[0:BLOCKS, 0:BLOCKS], start=True, stop=True).then_inc(S("heads_spread"), 1)
            pe.wait_ge(S("windows_ready"), 1)
            mm(XB[:, 128:128 + TILES], ones[0:TILES, :], heads[0:TILES, 0:TILES], start=True, stop=True)
            mm(XB[:, 256:257], ones[0:BLOCKS, :], p_t[0:BLOCKS, 9:10], start=True, stop=True).then_inc(S("windows_spread"), 1)
            pe.wait_ge(S("w_scaled"), 1)
            pe.wait_ge(S("offsets_ready"), 1)
            for b in range(2):
                mm(AGG[:, 0:D], ones[:], w_ffn[:, b, :], start=b == 0, stop=b == 1)
            for b in range(2):
                last = mm(XB[:, 0:D], lnb_b[:, b, :], w_raw[:, b, :], start=b == 0, stop=b == 1)
            last.then_inc(S("w_summed"), 1)
            pe.wait_ge(S("w_ffn_ready"), 1)
            n_u = pe.value_load(off_row[0:1, TILES:TILES + 1], min_val=1, max_val=E // UC)
            with pe.Fori(0, n_u) as i:
                pe.wait_ge(S("u_weighted"), i + 1)
                mm(XB[0:UC, 0:D], u_eq[0:UC, 0:UC], u_gw[0:UC, :], start=True, stop=True).then_inc(S("u_multiplied"), 1)
            pe.wait_ge(S("u_rows_ready"), n_u)

            def g_chunk(j, c):
                pe.wait_ge(S(f"gathered{c}"), j * 16 + 16)
                pe.wait_ge(S("hot_ready"), j * KC + (c + 1))
                if c == 0:
                    pe.wait_ge(S("messages_copied"), j)
                mm(AGG[0:R, 0:D], hot[c][:], gat[c][:], start=c == 0, stop=c == KC - 1).then_inc(S("chunks_multiplied"), 1)

            def xb_transpose(rows_, gs, xs):
                if gs is not None:
                    pe.wait_ge(S("g_done"), gs)
                if xs is not None:
                    pe.wait_ge(S("x_summed"), xs)
                for b in range(2):
                    last = tp(XB[:, b * R:(b + 1) * R], rows_[0:R, b * 128:(b + 1) * 128], ident[0:R, 0:R])
                last.then_inc(S("xb_transposed"), 1)

            def xb_multiply(w, use):
                pe.wait_ge(S("xb_copied"), use + 1)
                for b in range(2):
                    last = mm(XB[0:R, 0:D], xb_t[:, b, :], w[:, b, :], start=b == 0, stop=b == 1)
                last.then_inc(S("xb_multiplied"), 1)

            def g_transpose(j, gs, xs):
                pe.wait_ge(S("messages_copied"), j + 1)
                xb_transpose(g_agg, gs, xs)

            def x_transpose(i, gs, xs):
                pe.wait_ge(S("x_rows_loaded"), i * 32 + 32)
                xb_transpose(x_n, gs, xs)

            def k_transpose(loads, s):
                b, c = s % 2, s % K_RING
                pe.wait_ge(S(f"k_loaded{c}"), loads * 16)
                for h in range(2):
                    last = tp(K_TR[b][:, h * R:(h + 1) * R], k_x[c][0:R, h * 128:(h + 1) * 128], ident[0:R, 0:R])
                last.then_inc(S("k_transposed"), 1)

            def k_project(t, b):
                pe.wait_ge(S("k_copied"), t + 1)
                for h in range(2):
                    last = mm(K_MM[b][0:R, :], k_t[b][:, h, :], w_kv[:, h, :], start=h == 0, stop=h == 1)
                last.then_inc(S("k_projected"), 1)

            def k_outer(t, b, first, final):
                pe.wait_ge(S("k_normed"), t + 1)
                for hp in range(2):
                    last = mm(K_ACC[hp][:, 0:128], k_n[b][0:R, D + hp * 128:D + (hp + 1) * 128], k_n[b][0:R, hp * 128:(hp + 1) * 128],
                              start=first, stop=final)
                last.then_inc(S("k_outer_done"), 1)

            pe.wait_ge(S("w_kv_ready"), 2)
            k_transpose(1, 0)
            k_transpose(1, 1)
            k_project(0, 0)

            def b_trip(i, first, last):
                for s in range(KV_STEPS):
                    t = i * KV_STEPS + s
                    if not (last and s + 2 >= KV_STEPS):
                        k_transpose(i * (KV_STEPS // K_RING) + ((s + 2) // K_RING + 1), s + 2)
                    if not (last and s + 1 >= KV_STEPS):
                        k_project(t + 1, (s + 1) % 2)
                    for g in range(2):
                        if B_G[g].transpose == s:
                            g_transpose(i * 2 + g, i * 2 + g, None)
                        for c in B_G[g].mul[s]:
                            g_chunk(i * 2 + g, c)
                    k_outer(t, s % 2, first and s == 0, last and s == KV_STEPS - 1)
                    for g in range(2):
                        if B_G[g].multiply == s:
                            xb_multiply(w_agg, i * 2 + g)

            b_trip(0, True, False)
            with pe.Fori(1, LAST_B) as i:
                b_trip(i, False, False)
            b_trip(LAST_B, False, True)

            pe.wait_ge(S("g_done"), EARLY_G)
            pe.wait_ge(S("k_added"), TILES)
            for hp in range(2):
                mm(XB[:, hp * 128:(hp + 1) * 128], ones[0:R, :], k_sum[0:R, hp * 128:(hp + 1) * 128], start=True, stop=True)
            for hp in range(2):
                last = mm(XB[:, 256 + hp:257 + hp], k_sum[0:R, D + hp * 128:D + (hp + 1) * 128], ones[0:R, 0:1], start=True, stop=True)
            last.then_inc(S("sums_spread"), 1)
            pe.wait_ge(S("kv_ready"), 4)
            for hp in range(2):
                mm((AGG, XB)[hp][:, 0:D], kv_t[:, hp, :], w_wo[:, hp, :], start=True, stop=True).then_inc(S("kv_wo_done"), 1)
            pe.wait_ge(S("kv_wo_copied"), 2)
            for b in range(2):
                for hp in range(2):
                    last = mm(K_TR[b][:, 0:D], w_wq[:, hp, b * 128:(b + 1) * 128], t1[:, hp, :], start=hp == 0, stop=hp == 1)
                last.then_inc(S("mix_done"), 1)
            pe.wait_ge(S("mix_copied"), 2)

            with pe.Fori(0, EARLY_X) as i:
                x_transpose(i, None, i)
                xb_multiply(w_mix, i + EARLY_G)

            def f_transpose(n, q, b):
                pe.wait_ge(S("silu_done"), n + 1)
                for t in range(2):
                    for h in range(2):
                        last = tp(TR[b][:, (t * 2 + h) * R:(t * 2 + h + 1) * R], T[q][0:R, t, h * 128:(h + 1) * 128], ident[0:R, 0:R])
                last.then_inc(S("transposed"), 1)

            def f_multiply(n, b, r, outs):
                pe.wait_ge(S("transposed_copied"), n + 1)
                if outs > 0:
                    pe.wait_ge(S("out_ready"), r * PAIRS + outs)
                else:
                    pe.wait_ge(S("h_ready"), n + (PAIRS - 2))
                for t in range(2):
                    for h in range(2):
                        last = mm(MM[b][0:R, t * D:(t + 1) * D], v_t[b][:, t, h, :], w_ffn[:, h, :], start=h == 0, stop=h == 1)
                last.then_inc(S("multiplied"), 1)

            f_transpose(0, 0, 0)

            def f_trip(t, r, end, g, xx, last):
                for s in range(SLOTS):
                    n = t * SLOTS + s
                    if not (last and s + 1 >= SLOTS):
                        f_transpose(n + 1, (s + 1) % PAIRS, (s + 1) % 3)
                    if xx and s == X_TRANSPOSE:
                        x_transpose(t + EARLY_X, t + EARLY_G if g else TILES, t + EARLY_X)
                    if xx and s == X_MULTIPLY:
                        xb_multiply(w_mix, x_use(t, g))
                    if g:
                        if s == F_G.transpose:
                            g_transpose(t + EARLY_G, t + EARLY_G, t + EARLY_X + 1)
                        if s == F_G.multiply:
                            xb_multiply(w_agg, g_use(t))
                        for c in F_G.mul[s]:
                            g_chunk(t + EARLY_G, c)
                    f_multiply(n, s % 3, r, s - 3 - (SLOTS - PAIRS) + 1 if last else 0)

            trips_of_f(pe, f_trip)


_INS = ["x", "src", "dst", "ew", "w_gnn", "wq", "wk_t", "wv_t", "wo_t", "bo", "gk", "bk", "gv", "bv", "ln_w", "ln_b", "wf_t", "bf"]


def kernel(**inputs):
    import numpy as _np
    import concourse.bacc as _bacc
    from concourse import mybir as _mybir
    from concourse.bass_utils import run_bass_kernel_spmd as _run

    a = {k: _np.asarray(t) for k, t in inputs.items()}
    laid = {
        "x": a["x"], "src": a["src"], "dst": a["dst"], "ew": a["edge_weight"], "w_gnn": a["L0_gnn_weight"],
        "wq": a["L0_mix_wq"], "wk_t": a["L0_mix_wk"].T, "wv_t": a["L0_mix_wv"].T, "wo_t": a["L0_mix_wo"].T, "bo": a["L0_mix_bo"],
        "gk": a["L0_mix_ln_k_g"], "bk": a["L0_mix_ln_k_b"], "gv": a["L0_mix_ln_v_g"], "bv": a["L0_mix_ln_v_b"],
        "ln_w": a["L0_ffn_ln_w"], "ln_b": a["L0_ffn_ln_b"], "wf_t": a["L0_ffn_W"].T, "bf": a["L0_ffn_b"],
    }
    nc = _bacc.Bacc("TRN2", target_bir_lowering=False, num_devices=1)
    arrays, args = {}, []
    for name in _INS:
        t = _np.ascontiguousarray(laid[name])
        arrays[f"in_{name}"] = t
        args.append(nc.dram_tensor(f"in_{name}", t.shape, _mybir.dt.from_np(t.dtype), kind="ExternalInput").ap())
    args.append(nc.dram_tensor("out_rows", (N, D), _mybir.dt.float32, kind="ExternalOutput").ap())
    build(nc, *args)
    r = _run(nc, [arrays], core_ids=[0])
    return _np.asarray(r.results[0]["out_rows"])
```

```python
from contextlib import ExitStack

import concourse.bass as bass
from concourse import mybir

F32 = mybir.dt.float32
I32 = mybir.dt.int32
U32 = mybir.dt.uint32
ALU = mybir.AluOpType
ACT = mybir.ActivationFunctionType
AX_X = mybir.AxisListType.X

N, D, E = 12500, 256, 200000
HEADS, HD = 4, 64
STEPS = 30
EPS = 1e-5
R = 125
TILES = N // R
KC = 17
CAP = KC * 128
PAIRS = 5
ROUND = 2 * PAIRS
ROUNDS = TILES // ROUND
SLOTS = 3 * PAIRS
TRIPS = STEPS // 3
NSLOT = ROUNDS * TRIPS * SLOTS
EARLY_G = 20
EARLY_X = 10
A_RING = 5
A_LOOPS = TILES // 2 // A_RING
KV_STEPS = 10
K_RING = 5
LAST_B = TILES // KV_STEPS - 1
G_ROUNDS = (TILES - EARLY_G) // ROUND
UC = 125
BLOCKS, BLOCK = 125, 1600


def spread(n, steps):
    return [list(range(n * s // steps, n * (s + 1) // steps)) for s in range(steps)]


class Plan:
    def __init__(self, steps, first, over, hot_lag, mul_lag, tail):
        self.gather = [[] for _ in range(steps)]
        self.hot = [[] for _ in range(steps)]
        self.mul = [[] for _ in range(steps)]
        for k, chunks in enumerate(spread(KC, over)):
            self.gather[first + k] += chunks
            self.hot[first + k + hot_lag] += chunks
            self.mul[first + k + mul_lag] += chunks
        self.first = first
        self.copy, self.transpose, self.multiply, self.read = tail


F_G = Plan(SLOTS, 0, 10, 1, 2, (11, 13, 14, 14))
B_G = [Plan(KV_STEPS, 0, 4, 1, 1, (4, 5, 6, 6)), Plan(KV_STEPS, 4, 4, 1, 1, (8, 9, 9, 9))]
X_BIAS, X_TRANSPOSE, X_MULTIPLY, X_STATS, X_MEAN, X_VAR, X_NORM = 0, 1, 3, 4, 5, 6, 8


def build(nc, x, src, dst, ew, w_gnn, wq, wk_t, wv_t, wo_t, bo, gk, bk, gv, bv, ln_w, ln_b, wf_t, bf, out):
    xn_d = nc.dram_tensor("xn_d", [N, D], F32).ap()
    x1a_d = nc.dram_tensor("x1a_d", [N, D], F32).ap()
    x1_d = nc.dram_tensor("x1_d", [N, D], F32).ap()
    h0_d = nc.dram_tensor("h0_d", [N, D], F32).ap()
    gen_d = nc.dram_tensor("gen_d", [N + R, D], F32).ap()

    def rows(t, tile, n=1):
        return t[bass.ds(tile * R, n * R), :].rearrange("(t p) f -> p t f", p=R)

    ctx = ExitStack()
    with ctx:
        def sb(name, shape, dt=F32):
            return ctx.enter_context(nc.sbuf_tensor(name, shape, dt))

        made = {}

        def S(name):
            if name not in made:
                made[name] = ctx.enter_context(nc.semaphore(name))
            return made[name]

        ident = sb("ident", [128, 128])
        ones = sb("ones", [128, 128])
        iota_i = sb("iota_i", [128, R], I32)
        iota_f = sb("iota_f", [128, R])
        lane_i = sb("lane_i", [128, 3], I32)
        lane_f = sb("lane_f", [128, 3])
        below = sb("below", [128, R])
        base_i = sb("base_i", [128, TILES], I32)
        base_f = sb("base_f", [128, TILES])
        minus_half = sb("minus_half", [128, 8])
        zeros = sb("zeros", [128, 2, D])
        w_kv = sb("w_kv", [128, 2, 2 * D])
        w_mean = sb("w_mean", [128, 2, 8])
        w_agg = sb("w_agg", [128, 2, D])
        w_wq = sb("w_wq", [128, 2, D])
        w_wo = sb("w_wo", [128, 2, D])
        w_raw = sb("w_raw", [128, 2, D])
        w_ffn = sb("w_ffn", [128, 2, D])
        w_mix = sb("w_mix", [128, 2, D])
        lnw_c = sb("lnw_c", [128, 2])
        lnb_c = sb("lnb_c", [128, 2])
        lnb_b = sb("lnb_b", [128, 2, 128])
        c_row = sb("c_row", [128, D])
        bo_row = sb("bo_row", [128, D])
        gk_row = sb("gk_row", [128, 128])
        bk_row = sb("bk_row", [128, 128])
        gv_col = sb("gv_col", [128, 1])
        bv_col = sb("bv_col", [128, 1])
        d_blk = sb("d_blk", [128, BLOCK], I32)
        d_nxt = sb("d_nxt", [128, BLOCK], I32)
        d_cmp = sb("d_cmp", [128, BLOCK])
        d_row = [sb(f"d_row{k}", [128, BLOCK], I32) for k in range(2)]
        heads = sb("heads", [128, 128])
        p_t = sb("p_t", [128, 24])
        blk_i = sb("blk_i", [128, 2], I32)
        off_row = sb("off_row", [1, TILES + 4], I32)
        ok_col = sb("ok_col", [128, 2])
        u_src = sb("u_src", [128, 1], I32)
        u_dst = sb("u_dst", [128, 1], I32)
        u_w = sb("u_w", [128, 1])
        u_row = sb("u_row", [128, R], I32)
        u_eq = sb("u_eq", [128, R])
        u_low = sb("u_low", [128, R])
        u_t = sb("u_t", [128, 4])
        u_idx = sb("u_idx", [128, 1], I32)
        u_g = sb("u_g", [128, D])
        u_gw = sb("u_gw", [128, D])
        u_r = sb("u_r", [128, D])
        a_x = [sb(f"a_x{b}", [128, 2, D]) for b in range(A_RING)]
        a_n = [sb(f"a_n{b}", [128, 2, D]) for b in range(A_RING)]
        a_st = [sb(f"a_st{b}", [128, 2, 3]) for b in range(A_RING)]
        a_ve = [sb(f"a_ve{b}", [128, 2]) for b in range(A_RING)]
        a_rs = [sb(f"a_rs{b}", [128, 2]) for b in range(A_RING)]
        k_x = [sb(f"k_x{b}", [128, D]) for b in range(K_RING)]
        k_t = [sb(f"k_t{b}", [128, 2, R]) for b in range(2)]
        k_sq = sb("k_sq", [128, 2 * D])
        k_ss = sb("k_ss", [128, 8])
        k_ve = [sb(f"k_ve{b}", [128, 8]) for b in range(2)]
        k_rs = [sb(f"k_rs{b}", [128, 8]) for b in range(2)]
        k_n = [sb(f"k_n{b}", [128, 2 * D]) for b in range(2)]
        k_sum = sb("k_sum", [128, 2 * D])
        sv = sb("sv", [128, 2])
        kv_t = sb("kv_t", [128, 2, 128])
        kv_a = sb("kv_a", [128, 128])
        kv_b = sb("kv_b", [128, 128])
        t1 = sb("t1", [128, 2, D])
        src_cur = sb("src_cur", [128, KC], I32)
        dst_cur = sb("dst_cur", [128, KC], I32)
        w_cur = sb("w_cur", [128, KC])
        d_loc = sb("d_loc", [128, KC])
        w_loc = sb("w_loc", [128, KC])
        gat = [sb(f"gat{c}", [128, D]) for c in range(KC)]
        hot = [sb(f"hot{c}", [128, R]) for c in range(KC)]
        g_x = sb("g_x", [128, D])
        g_u = sb("g_u", [128, D])
        g_agg = sb("g_agg", [128, D])
        g_out = sb("g_out", [128, D])
        xb_t = sb("xb_t", [128, 2, R])
        x_n = sb("x_n", [128, D])
        x_a = sb("x_a", [128, D])
        x_1 = sb("x_1", [128, D])
        x_h = sb("x_h", [128, D])
        x_st = sb("x_st", [128, 6])
        x_mv = sb("x_mv", [128, 2])
        x_ve = sb("x_ve", [128, 1])
        x_rs = sb("x_rs", [128, 1])
        H = [sb(f"H{q}", [128, 2, D]) for q in range(PAIRS)]
        T = [sb(f"T{q}", [128, 2, D]) for q in range(PAIRS)]
        O = [sb(f"O{q}", [128, 2, D]) for q in range(PAIRS)]
        h_next = [sb(f"h_next{q}", [128, 2, D]) for q in range(PAIRS)]
        x_cur = [sb(f"x_cur{q}", [128, 2, D]) for q in range(PAIRS)]
        st = [sb(f"st{q}", [128, 2, 3]) for q in range(PAIRS)]
        ve = [sb(f"ve{q}", [128, 2]) for q in range(PAIRS)]
        rs = [sb(f"rs{q}", [128, 2]) for q in range(PAIRS)]
        v_t = [sb(f"v_t{b}", [128, 2, 2, R]) for b in range(3)]

        banks = [ctx.enter_context(nc.psum_tensor(f"bank{b}", [128, 512], F32)) for b in range(8)]
        TR = banks[0:3]
        MM = banks[3:6]
        AGG = banks[6]
        XB = banks[7]
        K_TR, K_MM = banks[0:2], banks[3:5]
        K_ACC = [banks[2], banks[5]]
        dst_blocks = dst.rearrange("(b k) -> b k", k=BLOCK)

        block = ctx.enter_context(nc.Block())

        def carry(eng):
            eng.sem_inc(S("passed"), 1)

        def trips_of_f(eng, body):
            with eng.Fori(0, G_ROUNDS) as r:
                with eng.Fori(r * TRIPS, r * TRIPS + (TRIPS - 1)) as t:
                    body(t, r, False, True, True, False)
                body(r * TRIPS + (TRIPS - 1), r, True, True, True, False)
            for r in range(G_ROUNDS, ROUNDS):
                with eng.Fori(r * TRIPS, r * TRIPS + (TRIPS - 1)) as t:
                    body(t, r, False, False, r < ROUNDS - 1, False)
                body(r * TRIPS + TRIPS - 1, r, True, False, r < ROUNDS - 1, r == ROUNDS - 1)

        def x_use(t, g):
            return t * 2 + EARLY_G if g else t + TILES

        def g_use(t):
            return t * 2 + (EARLY_G + 1)

        @block.sync
        def _(sp):
            sp.dma_start(d_blk[0:BLOCKS, :], dst_blocks).then_inc(S("dst_loaded"), 16)
            sp.wait_ge(S("dst_next_filled"), 1)
            sp.dma_start(d_nxt[0:BLOCKS - 1, :], dst[1:1 + (BLOCKS - 1) * BLOCK].rearrange("(b k) -> b k", k=BLOCK)).then_inc(S("dst_loaded"), 16)
            sp.dma_start(d_nxt[BLOCKS - 1:BLOCKS, 0:BLOCK - 1], dst[(BLOCKS - 1) * BLOCK + 1:E].unsqueeze(0)).then_inc(S("dst_loaded"), 16)
            for t, a in ((w_kv[:, :, 0:D], wk_t), (w_kv[:, :, D:2 * D], wv_t), (w_agg[:], w_gnn), (w_wq[:], wq),
                         (w_wo[:], wo_t), (w_raw[:], wf_t)):
                sp.dma_start(t, a.rearrange("(b p) n -> p b n", p=128)).then_inc(S("weights_loaded"), 16)
            sp.dma_start(c_row[:], bf.partition_broadcast(128)).then_inc(S("weights_loaded"), 16)
            sp.dma_start(bo_row[:], bo.partition_broadcast(128)).then_inc(S("weights_loaded"), 16)
            for b in range(2):
                sp.dma_start(lnw_c[:, b:b + 1], ln_w[b * 128:(b + 1) * 128].unsqueeze(1)).then_inc(S("weights_loaded"), 16)
                sp.dma_start(lnb_c[:, b:b + 1], ln_b[b * 128:(b + 1) * 128].unsqueeze(1)).then_inc(S("weights_loaded"), 16)
                sp.dma_start(gk_row[:, b * HD:(b + 1) * HD], gk.partition_broadcast(128)).then_inc(S("weights_loaded"), 16)
                sp.dma_start(bk_row[:, b * HD:(b + 1) * HD], bk.partition_broadcast(128)).then_inc(S("weights_loaded"), 16)
                sp.dma_start(gv_col[b * HD:(b + 1) * HD, :], gv.unsqueeze(1)).then_inc(S("weights_loaded"), 16)
                sp.dma_start(bv_col[b * HD:(b + 1) * HD, :], bv.unsqueeze(1)).then_inc(S("weights_loaded"), 16)

            def a_load(p, b):
                sp.dma_start(a_x[b][0:R], rows(x, p * 2, 2)).then_inc(S(f"a_loaded{b}"), 16)

            for b in range(A_RING):
                a_load(b, b)
            with sp.Fori(0, A_LOOPS - 1) as i:
                for b in range(A_RING):
                    sp.wait_ge(S("a_normed"), i * A_RING + (b + 1))
                    a_load(i * A_RING + (b + A_RING), b)

            sp.wait_ge(S("offsets_ready"), 1)
            n_u = sp.value_load(off_row[0:1, TILES:TILES + 1], min_val=1, max_val=E // UC)
            with sp.Fori(0, n_u) as i:
                sp.wait_ge(S("u_added"), i * 16)
                sp.dma_start(u_src[0:UC], src[bass.ds(i * UC, UC)].unsqueeze(1)).then_inc(S("u_loaded"), 16)
                sp.dma_start(u_dst[0:UC], dst[bass.ds(i * UC, UC)].unsqueeze(1)).then_inc(S("u_loaded"), 16)
                sp.dma_start(u_w[0:UC], ew[bass.ds(i * UC, UC)].unsqueeze(1)).then_inc(S("u_loaded"), 16)
                sp.dma_start(u_row[0:UC], dst[bass.ds(i * UC, UC)].partition_broadcast(UC)).then_inc(S("u_loaded"), 16)

            def g_load(j):
                for c in range(KC):
                    sp.wait_ge(S(f"gathered{c}"), j * 16)
                carry(sp)
                sp.wait_ge(S("edge_scalars_ready"), j * 2)
                off = sp.value_load(off_row[0:1, bass.ds(j, 1)], min_val=0, max_val=E - CAP)
                for t, a in ((src_cur, src), (dst_cur, dst), (w_cur, ew)):
                    sp.dma_start(t[:], a[bass.ds(off, CAP)].rearrange("(p k) -> p k", k=KC)).then_inc(S("edges_loaded"), 16)

            def g_rows(j):
                sp.wait_ge(S("messages_copied"), j)
                sp.dma_start(g_u[0:R], gen_d[bass.ds(j * R, R), :]).then_inc(S("g_rows_loaded"), 16)
                sp.wait_ge(S("g_done"), j)
                sp.dma_start(g_x[0:R], x[bass.ds(j * R, R), :]).then_inc(S("g_rows_loaded"), 16)

            def g_store(j):
                sp.wait_ge(S("g_done"), j + 1)
                sp.dma_start(x1a_d[bass.ds(j * R, R), :], g_out[0:R]).then_inc(S("g_stored"), 16)

            def x_load(i):
                sp.wait_ge(S("x_summed"), i)
                sp.wait_ge(S("g_stored"), i * 16 + (EARLY_X + 1) * 16)
                sp.dma_start(x_n[0:R], xn_d[bass.ds(i * R + EARLY_X * R, R), :]).then_inc(S("x_rows_loaded"), 16)
                sp.dma_start(x_a[0:R], x1a_d[bass.ds(i * R + EARLY_X * R, R), :]).then_inc(S("x_rows_loaded"), 16)

            def x_store(i):
                sp.wait_ge(S("x_summed"), i + 1)
                sp.dma_start(x1_d[bass.ds(i * R + EARLY_X * R, R), :], x_1[0:R]).then_inc(S("x_sum_stored"), 16)
                sp.wait_ge(S("x_normed"), i + 1)
                sp.dma_start(h0_d[bass.ds(i * R + EARLY_X * R, R), :], x_h[0:R]).then_inc(S("x_h_stored"), 16)

            def load_h(r, pairs):
                sp.wait_ge(S("h_next_used"), r * PAIRS)
                for q in pairs:
                    carry(sp)
                    sp.wait_ge(S("x_h_stored"), r * (ROUND * 16) + (q + 1) * 32)
                    sp.dma_start(h_next[q][0:R], rows(h0_d, r * ROUND + (ROUND + 2 * q), 2)).then_inc(S(f"h_next_loaded{q}"), 16)

            def load_x(r):
                sp.wait_ge(S("early_x_stored"), 16 * PAIRS)
                sp.wait_ge(S("out_ready"), r * PAIRS)
                carry(sp)
                sp.wait_ge(S("x_sum_stored"), r * (ROUND * 16))
                for q in range(PAIRS):
                    sp.dma_start(x_cur[q][0:R], rows(x1_d, r * ROUND + 2 * q, 2)).then_inc(S(f"x_cur_loaded{q}"), 16)

            for b in range(A_RING):
                sp.wait_ge(S(f"a_stored{b}"), 16 * A_LOOPS)
            sp.wait_ge(S("u_added"), n_u * 16)

            def k_load(t, b):
                sp.dma_start(k_x[b][0:R], xn_d[bass.ds(t * R, R), :]).then_inc(S(f"k_loaded{b}"), 16)

            for b in range(K_RING):
                k_load(b, b)

            def b_trip(i, last):
                for s in range(KV_STEPS):
                    t = i * KV_STEPS + s
                    for g in range(2):
                        if B_G[g].first == s:
                            g_load(i * 2 + g)
                    if s == 0:
                        g_rows(i * 2)
                    if not (last and s + K_RING >= KV_STEPS):
                        sp.wait_ge(S("k_transposed"), t + 1)
                        k_load(t + K_RING, s % K_RING)
                    if s == B_G[0].read + 1:
                        g_store(i * 2)
                        g_rows(i * 2 + 1)
                    if s == B_G[1].read:
                        g_store(i * 2 + 1)

            with sp.Fori(0, LAST_B) as i:
                b_trip(i, False)
            b_trip(LAST_B, True)

            for q in range(PAIRS):
                sp.wait_ge(S("g_stored"), 16 * (2 * q + 2))
                sp.dma_start(T[q][0:R], rows(xn_d, 2 * q, 2)).then_inc(S(f"early_rows_loaded{q}"), 16)
                sp.dma_start(O[q][0:R], rows(x1a_d, 2 * q, 2)).then_inc(S(f"early_rows_loaded{q}"), 16)
            g_load(EARLY_G)
            x_load(0)
            for q in range(PAIRS):
                sp.wait_ge(S("early_summed"), q + 1)
                sp.dma_start(rows(x1_d, 2 * q, 2), x_cur[q][0:R]).then_inc(S("early_x_stored"), 16)

            def f_trip(t, r, end, g, xx, last):
                if g:
                    g_rows(t + EARLY_G)
                if end:
                    load_x(r)
                if end and not last:
                    load_h(r, range(PAIRS - 1))
                if xx:
                    x_store(t)
                    if not (end and not g):
                        x_load(t + 1)
                if end and not last:
                    load_h(r, range(PAIRS - 1, PAIRS))
                if g:
                    g_load(t + (EARLY_G + 1))
                    g_store(t + EARLY_G)
                if end:
                    for q in range(PAIRS):
                        sp.wait_ge(S("out_ready"), r * PAIRS + (q + 1))
                        sp.dma_start(rows(out, r * ROUND + 2 * q, 2), O[q][0:R]).then_inc(S(f"out_stored{q}"), 16)

            trips_of_f(sp, f_trip)
            for q in range(PAIRS):
                sp.wait_ge(S(f"out_stored{q}"), 16 * ROUNDS)
            sp.wait_ge(S("edges_loaded"), 48 * (TILES + 1))
            sp.wait_ge(S("zeroed"), 16 * (TILES // 2 + 1))

        @block.gpsimd
        def _(pool):
            pool.memset(d_nxt[:], 1 << 20).then_inc(S("dst_next_filled"), 1)
            pool.memset(ident[:], 0.0).then_inc(S("pool_own"), 1)
            pool.memset(below[:], 0.0).then_inc(S("pool_own"), 1)
            pool.iota(iota_i[:], pattern=[[1, R]], base=0, channel_multiplier=0).then_inc(S("iotas_made"), 1)
            pool.iota(base_i[:], pattern=[[R, TILES]], base=0, channel_multiplier=0).then_inc(S("iotas_made"), 1)
            pool.iota(lane_i[:, 0:1], pattern=[[0, 1]], base=N, channel_multiplier=1).then_inc(S("iotas_made"), 1)
            pool.iota(lane_i[:, 1:3], pattern=[[R, 2]], base=0, channel_multiplier=R).then_inc(S("iotas_made"), 1)
            pool.wait_ge(S("pool_own"), 2)
            pool.affine_select(out=ident[:], in_=ident[:], compare_op=ALU.not_equal, fill=1.0, base=0,
                               pattern=[[-1, 128]], channel_multiplier=1).then_inc(S("masks_made"), 1)
            pool.affine_select(out=below[:], in_=below[:], compare_op=ALU.is_ge, fill=1.0, base=0,
                               pattern=[[1, R]], channel_multiplier=-1).then_inc(S("masks_made"), 1)
            pool.wait_ge(S("blocks_found"), 1)
            for k in range(2):
                pool.indirect_dma_start(d_row[k][0:TILES, :], None, dst_blocks,
                                        bass.IndirectOffsetOnAxis(ap=blk_i[0:TILES, k:k + 1], axis=0)).then_inc(S("blocks_gathered"), 16)

            def rstd(out_, var, n, after, value, done):
                pool.wait_ge(S(after), value)
                pool.tensor_tensor(out_, var, minus_half[0:R, 0:n], ALU.pow).then_inc(S(done), 1)

            with pool.Fori(0, A_LOOPS) as i:
                for b in range(A_RING):
                    rstd(a_rs[b][0:R], a_ve[b][0:R], 2, "a_variance", i * A_RING + (b + 1), "a_rstd")

            for b in range(A_RING):
                pool.wait_ge(S(f"a_stored{b}"), 16 * A_LOOPS)
            pool.wait_ge(S("zeroed"), 16 * (TILES // 2 + 1))
            pool.wait_ge(S("offsets_ready"), 1)
            n_u = pool.value_load(off_row[0:1, TILES:TILES + 1], min_val=1, max_val=E // UC)
            with pool.Fori(0, n_u) as i:
                pool.wait_ge(S("u_loaded"), i * 64 + 64)
                carry(pool)
                pool.indirect_dma_start(u_g[0:UC, :], None, xn_d,
                                        bass.IndirectOffsetOnAxis(ap=u_src[0:UC, 0:1], axis=0)).then_inc(S("u_gathered"), 16)
                pool.wait_ge(S("u_rows_ready"), i + 1)
                carry(pool)
                pool.indirect_dma_start(gen_d, bass.IndirectOffsetOnAxis(ap=u_idx[0:UC, 0:1], axis=0), u_r[0:UC, :], None,
                                        compute_op=ALU.add).then_inc(S("u_added"), 16)
                pool.wait_ge(S("u_added"), i * 16 + 16)

            def gather(j, c):
                if c == 0:
                    pool.wait_ge(S("edges_loaded"), j * 48 + 48)
                pool.wait_ge(S("chunks_multiplied"), j * KC + (c + 1))
                carry(pool)
                pool.indirect_dma_start(gat[c][:], None, xn_d, bass.IndirectOffsetOnAxis(ap=src_cur[:, c:c + 1], axis=0)).then_inc(S(f"gathered{c}"), 16)

            for b in range(2):
                rstd(k_rs[b][0:R], k_ve[b][0:R], 8, "k_variance", b + 1, "k_rstd")

            def b_trip(i, last):
                for s in range(KV_STEPS):
                    chunks = [(g, c) for g in range(2) for c in B_G[g].gather[s]]
                    for g, c in chunks[:2]:
                        gather(i * 2 + g, c)
                    if not (last and s + 2 >= KV_STEPS):
                        rstd(k_rs[s % 2][0:R], k_ve[s % 2][0:R], 8, "k_variance", i * KV_STEPS + (s + 3), "k_rstd")
                    for g, c in chunks[2:]:
                        gather(i * 2 + g, c)

            with pool.Fori(0, LAST_B) as i:
                b_trip(i, False)
            b_trip(LAST_B, True)

            for q in range(PAIRS):
                rstd(rs[q][0:R], ve[q][0:R], 2, "early_variance", q + 1, "early_rstd")

            def x_rstd(i):
                rstd(x_rs[0:R], x_ve[0:R], 1, "x_variance", i + 1, "x_rstd")

            def f_rstd(n, q):
                rstd(rs[q][0:R], ve[q][0:R], 2, "variance", n + 1, "rstd")

            f_rstd(0, 0)
            f_rstd(1, 1)

            def f_trip(t, r, end, g, xx, last):
                for s in range(SLOTS):
                    if g:
                        for c in F_G.gather[s]:
                            gather(t + EARLY_G, c)
                    if not (last and s + 2 >= SLOTS):
                        f_rstd(t * SLOTS + (s + 2), (s + 2) % PAIRS)
                    if xx and s == X_VAR:
                        x_rstd(t)

            trips_of_f(pool, f_trip)

        @block.scalar
        def _(act):
            act.wait_ge(S("zeros_made"), 1)
            with act.Fori(0, TILES // 2) as i:
                act.dma_start(rows(gen_d, i * 2, 2), zeros[0:R]).then_inc(S("zeroed"), 16)
            act.dma_start(gen_d[N:N + R, :], zeros[0:R, 0, :]).then_inc(S("zeroed"), 16)
            with act.Fori(0, A_LOOPS) as i:
                for b in range(A_RING):
                    act.wait_ge(S("a_normed"), i * A_RING + (b + 1))
                    act.dma_start(rows(xn_d, i * (2 * A_RING) + 2 * b, 2), a_n[b][0:R]).then_inc(S(f"a_stored{b}"), 16)

            def xb_copy(v):
                act.wait_ge(S("xb_transposed"), v + 1)
                nc.scalar.activation(xb_t[:].rearrange("p b r -> p (b r)"), XB[:, 0:2 * R], ACT.Copy).then_inc(S("xb_copied"), 1)

            def k_copy(t, b):
                act.wait_ge(S("k_transposed"), t + 1)
                nc.scalar.activation(k_t[b][:].rearrange("p b r -> p (b r)"), K_TR[b][:, 0:2 * R], ACT.Copy).then_inc(S("k_copied"), 1)

            def k_square(t, b):
                act.wait_ge(S("k_projected"), t + 1)
                act.wait_ge(S("k_squares_summed"), t)
                nc.scalar.activation(k_sq[0:R], K_MM[b][0:R, :], ACT.Square).then_inc(S("k_squared"), 1)

            k_copy(0, 0)
            k_copy(1, 1)
            k_square(0, 0)
            k_copy(2, 0)
            k_square(1, 1)

            def b_trip(i, last):
                for s in range(KV_STEPS):
                    t = i * KV_STEPS + s
                    if not (last and s + 3 >= KV_STEPS):
                        k_copy(t + 3, (s + 3) % 2)
                    if not (last and s + 2 >= KV_STEPS):
                        k_square(t + 2, s % 2)
                    for g in range(2):
                        if B_G[g].transpose == s:
                            xb_copy(i * 2 + g)

            with act.Fori(0, LAST_B) as i:
                b_trip(i, False)
            b_trip(LAST_B, True)

            for q in range(PAIRS):
                b = q % 3
                act.wait_ge(S("early_transposed"), q + 1)
                if q >= 3:
                    act.wait_ge(S("early_multiplied"), q - 2)
                nc.scalar.activation(v_t[b][:].rearrange("p t b r -> p (t b r)"), TR[b][:, 0:4 * R], ACT.Copy).then_inc(S("early_copied"), 1)

            def tanh(n, q):
                act.wait_ge(S("h_ready"), n + 1)
                nc.scalar.activation(T[q][0:R], H[q][0:R], ACT.Tanh).then_inc(S("tanh_done"), 1)

            def silu(n, q):
                act.wait_ge(S("u_done"), n + 1)
                nc.scalar.activation(T[q][0:R], T[q][0:R], ACT.Silu).then_inc(S("silu_done"), 1)

            def copy_t(n, b, last):
                if last:
                    act.wait_ge(S("multiplied"), n - 2)
                act.wait_ge(S("transposed"), n + 1)
                nc.scalar.activation(v_t[b][:].rearrange("p t b r -> p (t b r)"), TR[b][:, 0:4 * R], ACT.Copy).then_inc(S("transposed_copied"), 1)

            tanh(0, 0)
            tanh(1, 1)
            silu(0, 0)
            tanh(2, 2)
            silu(1, 1)
            copy_t(0, 0, False)
            tanh(3, 3)
            silu(2, 2)

            def f_trip(t, r, end, g, xx, last):
                for s in range(SLOTS):
                    n = t * SLOTS + s
                    if not (last and s + 1 >= SLOTS):
                        copy_t(n + 1, (s + 1) % 3, last)
                    if not (last and s + 4 >= SLOTS):
                        tanh(n + 4, (s + 4) % PAIRS)
                    if not (last and s + 3 >= SLOTS):
                        silu(n + 3, (s + 3) % PAIRS)
                    if xx and s == X_TRANSPOSE:
                        xb_copy(x_use(t, g))
                    if g and s == F_G.transpose:
                        xb_copy(g_use(t))

            trips_of_f(act, f_trip)

        @block.vector
        def _(dve):
            count = [0]

            def link(ins):
                count[0] += 1
                ins.then_inc(S("vector_own"), 1)
                dve.wait_ge(S("vector_own"), count[0])

            v = nc.vector
            v.memset(zeros[:], 0.0).then_inc(S("zeros_made"), 1)
            v.memset(ones[:], 1.0).then_inc(S("ones_made"), 1)
            v.memset(minus_half[:], -0.5).then_inc(S("vector_const"), 1)
            v.memset(k_sum[:], 0.0).then_inc(S("vector_const"), 1)
            v.memset(kv_t[:], 0.0).then_inc(S("vector_const"), 1)
            v.memset(p_t[:], 0.0).then_inc(S("vector_const"), 1)
            dve.wait_ge(S("iotas_made"), 4)
            v.tensor_copy(iota_f[:], iota_i[:]).then_inc(S("vector_const"), 1)
            v.tensor_copy(base_f[:], base_i[:]).then_inc(S("vector_const"), 1)
            v.tensor_copy(lane_f[:], lane_i[:]).then_inc(S("vector_const"), 1)
            dve.wait_ge(S("vector_const"), 7)

            dve.wait_ge(S("dst_loaded"), 48)
            dve.wait_ge(S("masks_made"), 2)
            link(v.tensor_copy(p_t[0:BLOCKS, 12:13], d_blk[0:BLOCKS, 0:1]))
            v.tensor_scalar(heads[0:BLOCKS, 0:BLOCKS], ident[0:BLOCKS, 0:BLOCKS], p_t[0:BLOCKS, 12:13], None, ALU.mult).then_inc(S("heads_ready"), 1)
            link(v.tensor_tensor(d_cmp[0:BLOCKS, :], d_nxt[0:BLOCKS, :], d_blk[0:BLOCKS, :], ALU.is_lt))
            link(v.tensor_reduce(p_t[0:BLOCKS, 9:10], d_cmp[0:BLOCKS, :], AX_X, ALU.add))
            dve.wait_ge(S("heads_spread"), 1)
            for k in range(2):
                link(v.tensor_scalar(d_cmp[0:TILES, 0:BLOCKS], XB[0:TILES, 0:BLOCKS], lane_f[0:TILES, 1 + k:2 + k], None, ALU.is_lt))
                link(v.tensor_reduce(p_t[0:TILES, k:k + 1], d_cmp[0:TILES, 0:BLOCKS], AX_X, ALU.add))
            link(v.tensor_scalar(p_t[0:TILES, 2:4], p_t[0:TILES, 0:2], -1.0, 0.0, ALU.add, ALU.max))
            v.tensor_copy(blk_i[0:TILES, :], p_t[0:TILES, 2:4]).then_inc(S("blocks_found"), 1)
            dve.wait_ge(S("blocks_gathered"), 32)
            for k in range(2):
                link(v.tensor_scalar(d_cmp[0:TILES, :], d_row[k][0:TILES, :], lane_f[0:TILES, 1 + k:2 + k], None, ALU.is_lt))
                link(v.tensor_reduce(p_t[0:TILES, 4 + k:5 + k], d_cmp[0:TILES, :], AX_X, ALU.add))
            link(v.scalar_tensor_tensor(out=p_t[0:TILES, 6:8], in0=p_t[0:TILES, 2:4], scalar=float(BLOCK), in1=p_t[0:TILES, 4:6], op0=ALU.mult, op1=ALU.add))
            link(v.tensor_tensor(p_t[0:TILES, 8:9], p_t[0:TILES, 7:8], p_t[0:TILES, 6:7], ALU.subtract))
            link(v.tensor_scalar(p_t[0:TILES, 8:9], p_t[0:TILES, 8:9], float(CAP), None, ALU.is_gt))
            link(v.tensor_tensor(p_t[0:BLOCKS, 9:10], p_t[0:BLOCKS, 9:10], p_t[0:BLOCKS, 8:9], ALU.add))
            link(v.tensor_scalar(p_t[0:TILES, 10:11], p_t[0:TILES, 6:7], float(E - CAP), None, ALU.min))
            v.tensor_scalar(heads[0:TILES, 0:TILES], ident[0:TILES, 0:TILES], p_t[0:TILES, 10:11], None, ALU.mult).then_inc(S("windows_ready"), 1)
            dve.wait_ge(S("windows_spread"), 1)
            v.tensor_copy(off_row[0:1, 0:TILES], XB[0:1, 128:128 + TILES]).then_inc(S("vector_own2"), 1)
            link(v.tensor_scalar(ok_col[:, 1:2], XB[:, 256:257], 1.0, None, ALU.min))
            link(v.tensor_scalar(ok_col[:, 0:1], ok_col[:, 1:2], -1.0, 1.0, ALU.mult, ALU.add))
            dve.wait_ge(S("vector_own2"), 1)
            v.tensor_scalar(off_row[0:1, TILES:TILES + 1], ok_col[0:1, 1:2], float(E // UC - 1), 1.0, ALU.mult, ALU.add).then_inc(S("offsets_ready"), 1)

            dve.wait_ge(S("weights_loaded"), 20 * 16)
            for b in range(2):
                heads_of = w_kv[:, b, :].rearrange("p (h d) -> p h d", d=HD)
                link(v.tensor_reduce(w_mean[:, b, :], heads_of, AX_X, ALU.add))
                link(v.tensor_scalar(w_mean[:, b, :], w_mean[:, b, :], 1.0 / HD, None, ALU.mult))
                v.tensor_tensor(heads_of, heads_of, w_mean[:, b, :].unsqueeze(2).broadcast_to([128, 8, HD]), ALU.subtract).then_inc(S("w_kv_ready"), 1)
            for b in range(2):
                link(v.tensor_scalar(w_ffn[:, b, :], w_raw[:, b, :], lnw_c[:, b:b + 1], None, ALU.mult))
                link(v.tensor_scalar(lnb_b[:, b, :], ones[:], lnb_c[:, b:b + 1], None, ALU.mult))
            v.memset(p_t[:, 20:21], 0.0).then_inc(S("w_scaled"), 1)
            dve.wait_ge(S("w_summed"), 1)
            for b in range(2):
                link(v.scalar_tensor_tensor(out=w_ffn[:, b, :], in0=AGG[:, 0:D], scalar=-1.0 / D, in1=w_ffn[:, b, :], op0=ALU.mult, op1=ALU.add))
            link(v.tensor_tensor(c_row[:], XB[:, 0:D], c_row[:], ALU.add))
            v.memset(p_t[:, 21:22], 0.0).then_inc(S("w_ffn_ready"), 1)

            def a_bn(i, b):
                dve.wait_ge(S(f"a_loaded{b}"), i * 16 + 16)
                v.bn_stats(a_st[b][0:R].rearrange("p t k -> p (t k)"), a_x[b][0:R].rearrange("p t f -> p f t")).then_inc(S("a_stats"), 1)

            def a_var(i, b):
                dve.wait_ge(S("a_stats"), i * A_RING + (b + 1))
                v.tensor_scalar(a_ve[b][0:R], a_st[b][0:R, :, 2], 1.0 / D, EPS, ALU.mult, ALU.add).then_inc(S("a_variance"), 1)

            def a_norm(i, b):
                dve.wait_ge(S("a_rstd"), i * A_RING + (b + 1))
                dve.wait_ge(S(f"a_stored{b}"), i * 16)
                for t in range(2):
                    last = v.tensor_scalar(a_n[b][0:R, t, :], a_x[b][0:R, t, :], a_st[b][0:R, t, 1:2], a_rs[b][0:R, t:t + 1], ALU.subtract, ALU.mult)
                last.then_inc(S("a_normed"), 1)

            a_bn(0, 0)
            a_var(0, 0)
            def a_loop(i, last):
                for b in range(A_RING):
                    if b < A_RING - 1:
                        a_bn(i, b + 1)
                        a_var(i, b + 1)
                    elif not last:
                        a_bn(i + 1, 0)
                        a_var(i + 1, 0)
                    a_norm(i, b)

            with dve.Fori(0, A_LOOPS - 1) as i:
                a_loop(i, False)
            a_loop(A_LOOPS - 1, True)

            dve.wait_ge(S("offsets_ready"), 1)
            n_u = dve.value_load(off_row[0:1, TILES:TILES + 1], min_val=1, max_val=E // UC)
            with dve.Fori(0, n_u) as i:
                def u_link(ins, name):
                    ins.then_inc(S(name), 1)
                    dve.wait_ge(S(name), i + 1)

                dve.wait_ge(S("u_loaded"), i * 64 + 64)
                u_link(v.tensor_copy(u_t[0:UC, 0:1], u_dst[0:UC]), "u_dst_float")
                u_link(v.tensor_scalar(u_t[0:UC, 1:2], u_w[0:UC], ok_col[0:UC, 1:2], None, ALU.mult), "u_weight")
                u_link(v.tensor_scalar(u_eq[0:UC], u_row[0:UC], u_t[0:UC, 0:1], None, ALU.is_equal), "u_equal")
                u_link(v.tensor_tensor(u_low[0:UC], u_eq[0:UC], below[0:UC], ALU.mult), "u_earlier")
                u_link(v.tensor_reduce(u_t[0:UC, 2:3], u_low[0:UC], AX_X, ALU.max), "u_repeated")
                u_link(v.tensor_tensor(u_t[0:UC, 3:4], lane_f[0:UC, 0:1], u_t[0:UC, 0:1], ALU.subtract), "u_to_spare")
                u_link(v.tensor_tensor(u_t[0:UC, 3:4], u_t[0:UC, 3:4], u_t[0:UC, 2:3], ALU.mult), "u_shift")
                u_link(v.tensor_tensor(u_t[0:UC, 3:4], u_t[0:UC, 3:4], u_t[0:UC, 0:1], ALU.add), "u_row_number")
                u_link(v.tensor_copy(u_idx[0:UC], u_t[0:UC, 3:4]), "u_index")
                dve.wait_ge(S("u_gathered"), i * 16 + 16)
                v.tensor_scalar(u_gw[0:UC], u_g[0:UC], u_t[0:UC, 1:2], None, ALU.mult).then_inc(S("u_weighted"), 1)
                dve.wait_ge(S("u_multiplied"), i + 1)
                v.tensor_copy(u_r[0:UC], XB[0:UC, 0:D]).then_inc(S("u_rows_ready"), 1)

            def g_scalars(j):
                dve.wait_ge(S("edges_loaded"), j * 48 + 48)
                dve.wait_ge(S("hot_ready"), j * KC)
                v.tensor_scalar(d_loc[:], dst_cur[:], base_f[:, bass.ds(j, 1)], None, ALU.subtract).then_inc(S("edge_scalars_ready"), 1)
                v.tensor_scalar(w_loc[:], w_cur[:], ok_col[:, 0:1], None, ALU.mult).then_inc(S("edge_scalars_ready"), 1)

            def g_hot(j, c):
                if c == 0:
                    dve.wait_ge(S("edge_scalars_ready"), j * 2 + 2)
                dve.wait_ge(S("chunks_multiplied"), j * KC + (c + 1))
                v.tensor_scalar(hot[c][:], iota_f[:], d_loc[:, c:c + 1], w_loc[:, c:c + 1], ALU.is_equal, ALU.mult).then_inc(S("hot_ready"), 1)

            def g_copy(j):
                dve.wait_ge(S("g_rows_loaded"), j * 32 + 32)
                dve.wait_ge(S("chunks_multiplied"), j * KC + 2 * KC)
                v.tensor_tensor(g_agg[0:R], AGG[0:R, 0:D], g_u[0:R], ALU.add).then_inc(S("messages_copied"), 1)

            def g_read(j, use):
                dve.wait_ge(S("g_stored"), j * 16)
                dve.wait_ge(S("xb_multiplied"), use + 1)
                v.scalar_tensor_tensor(out=g_out[0:R], in0=XB[0:R, 0:D], scalar=0.0, in1=g_x[0:R], op0=ALU.max, op1=ALU.add).then_inc(S("g_done"), 1)

            def k_stats(t, b):
                dve.wait_ge(S("k_squared"), t + 1)
                v.tensor_reduce(k_ss[0:R], k_sq[0:R].rearrange("p (h d) -> p h d", d=HD), AX_X, ALU.add).then_inc(S("k_squares_summed"), 1)
                dve.wait_ge(S("k_squares_summed"), t + 1)
                v.tensor_scalar(k_ve[b][0:R], k_ss[0:R], 1.0 / HD, EPS, ALU.mult, ALU.add).then_inc(S("k_variance"), 1)

            def k_norm(t, b, outers):
                dve.wait_ge(S("k_rstd"), t + 1)
                if outers is not None:
                    dve.wait_ge(S("k_outer_done"), outers)
                v.tensor_tensor(k_n[b][0:R].rearrange("p (h d) -> p h d", d=HD), K_MM[b][0:R].rearrange("p (h d) -> p h d", d=HD),
                                k_rs[b][0:R].unsqueeze(2).broadcast_to([R, 8, HD]), ALU.mult).then_inc(S("k_normed"), 1)
                dve.wait_ge(S("k_normed"), t + 1)
                dve.wait_ge(S("k_added"), t)
                v.tensor_tensor(k_sum[0:R], k_sum[0:R], k_n[b][0:R], ALU.add).then_inc(S("k_added"), 1)

            k_stats(0, 0)
            k_norm(0, 0, None)
            k_stats(1, 1)

            def b_trip(i, last):
                for s in range(KV_STEPS):
                    t = i * KV_STEPS + s
                    more = not (last and s + 1 >= KV_STEPS)
                    if more:
                        k_norm(t + 1, (s + 1) % 2, t)
                    for g in range(2):
                        if B_G[g].first == s:
                            g_scalars(i * 2 + g)
                        for c in B_G[g].hot[s]:
                            g_hot(i * 2 + g, c)
                    if not (last and s + 2 >= KV_STEPS):
                        k_stats(t + 2, s % 2)
                    for g in range(2):
                        if B_G[g].copy == s:
                            g_copy(i * 2 + g)
                        if B_G[g].read == s:
                            g_read(i * 2 + g, i * 2 + g)

            with dve.Fori(0, LAST_B) as i:
                b_trip(i, False)
            b_trip(LAST_B, True)

            dve.wait_ge(S("k_outer_done"), TILES)
            dve.wait_ge(S("sums_spread"), 1)
            for hp in range(2):
                link(v.tensor_copy(sv[:, hp:hp + 1], XB[:, 256 + hp:257 + hp]))
                link(v.tensor_tensor(kv_a[:], K_ACC[hp][:, 0:128], gk_row[:], ALU.mult))
                link(v.tensor_scalar(kv_b[:], bk_row[:], sv[:, hp:hp + 1], None, ALU.mult))
                link(v.tensor_tensor(kv_a[:], kv_a[:], kv_b[:], ALU.add))
                link(v.tensor_scalar(kv_a[:], kv_a[:], gv_col[:, 0:1], None, ALU.mult))
                link(v.tensor_tensor(kv_b[:], XB[:, hp * 128:(hp + 1) * 128], gk_row[:], ALU.mult))
                link(v.scalar_tensor_tensor(out=kv_b[:], in0=bk_row[:], scalar=float(N), in1=kv_b[:], op0=ALU.mult, op1=ALU.add))
                link(v.tensor_scalar(kv_b[:], kv_b[:], bv_col[:, 0:1], None, ALU.mult))
                link(v.tensor_tensor(kv_a[:], kv_a[:], kv_b[:], ALU.add))
                for h in range(2):
                    part = slice(h * HD, (h + 1) * HD)
                    v.tensor_scalar(kv_t[part, hp, part], kv_a[part, part], 1.0 / N, None, ALU.mult).then_inc(S("kv_ready"), 1)
                dve.wait_ge(S("kv_ready"), 2 * hp + 2)
            for hp in range(2):
                dve.wait_ge(S("kv_wo_done"), hp + 1)
                v.tensor_copy(t1[:, hp, :], (AGG, XB)[hp][:, 0:D]).then_inc(S("kv_wo_copied"), 1)
            for b in range(2):
                dve.wait_ge(S("mix_done"), b + 1)
                v.tensor_copy(w_mix[:, b, :], K_TR[b][:, 0:D]).then_inc(S("mix_copied"), 1)

            def x_bias(i):
                dve.wait_ge(S("x_rows_loaded"), i * 32 + 32)
                v.tensor_tensor(x_a[0:R], x_a[0:R], bo_row[0:R], ALU.add).then_inc(S("x_biased"), 1)

            def x_read(i, use):
                dve.wait_ge(S("x_sum_stored"), i * 16)
                dve.wait_ge(S("x_biased"), i + 1)
                dve.wait_ge(S("xb_multiplied"), use + 1)
                v.tensor_tensor(x_1[0:R], XB[0:R, 0:D], x_a[0:R], ALU.add).then_inc(S("x_summed"), 1)

            def x_stats(i):
                dve.wait_ge(S("x_summed"), i + 1)
                v.bn_stats(x_st[0:R], x_1[0:R]).then_inc(S("x_stats"), 1)

            def x_mean(i):
                dve.wait_ge(S("x_stats"), i + 1)
                carry(dve)
                v.bn_aggr(x_mv[0:R], x_st[0:R]).then_inc(S("x_mean"), 1)

            def x_var(i):
                dve.wait_ge(S("x_mean"), i + 1)
                v.tensor_scalar(x_ve[0:R], x_mv[0:R, 1:2], EPS, None, ALU.add).then_inc(S("x_variance"), 1)

            def x_norm(i):
                dve.wait_ge(S("x_h_stored"), i * 16)
                dve.wait_ge(S("x_rstd"), i + 1)
                v.tensor_scalar(x_h[0:R], x_1[0:R], x_mv[0:R, 0:1], x_rs[0:R, 0:1], ALU.subtract, ALU.mult).then_inc(S("x_normed"), 1)

            def early_norm(q):
                dve.wait_ge(S("early_rstd"), q + 1)
                for t in range(2):
                    last = v.tensor_scalar(H[q][0:R, t, :], x_cur[q][0:R, t, :], st[q][0:R, t, 1:2], rs[q][0:R, t:t + 1], ALU.subtract, ALU.mult)
                last.then_inc(S("h_ready"), 1)

            for q in range(PAIRS):
                dve.wait_ge(S(f"early_rows_loaded{q}"), 32)
                v.tensor_tensor(O[q][0:R], O[q][0:R], bo_row[0:R].unsqueeze(1).broadcast_to([R, 2, D]), ALU.add).then_inc(S("early_biased"), 1)
            for q in range(PAIRS):
                dve.wait_ge(S("early_multiplied"), q + 1)
                dve.wait_ge(S("early_biased"), q + 1)
                v.tensor_tensor(x_cur[q][0:R], MM[q % 3][0:R, :].rearrange("p (t f) -> p t f", t=2), O[q][0:R], ALU.add).then_inc(S("early_summed"), 1)
                dve.wait_ge(S("early_summed"), q + 1)
                v.bn_stats(st[q][0:R].rearrange("p t k -> p (t k)"), x_cur[q][0:R].rearrange("p t f -> p f t")).then_inc(S("early_stats"), 1)
                dve.wait_ge(S("early_stats"), q + 1)
                v.tensor_scalar(ve[q][0:R], st[q][0:R, :, 2], 1.0 / D, EPS, ALU.mult, ALU.add).then_inc(S("early_variance"), 1)
                if q >= 1:
                    early_norm(q - 1)
            early_norm(PAIRS - 1)

            def f_sum(n, q):
                dve.wait_ge(S("tanh_done"), n + 1)
                v.scalar_tensor_tensor(out=T[q][0:R], in0=T[q][0:R], scalar=0.01, in1=H[q][0:R], op0=ALU.mult, op1=ALU.add).then_inc(S("u_done"), 1)

            def f_stats(n, q):
                dve.wait_ge(S("silu_done"), n + 1)
                v.bn_stats(st[q][0:R].rearrange("p t k -> p (t k)"), T[q][0:R].rearrange("p t f -> p f t")).then_inc(S("stats"), 1)

            def f_var(n, q):
                dve.wait_ge(S("stats"), n + 1)
                v.tensor_scalar(ve[q][0:R], st[q][0:R, :, 2], 1.0 / D, EPS, ALU.mult, ALU.add).then_inc(S("variance"), 1)

            def f_scale(n, q, b):
                dve.wait_ge(S("rstd"), n + 1)
                dve.wait_ge(S("multiplied"), n + 1)
                for t in range(2):
                    last = v.scalar_tensor_tensor(out=H[q][0:R, t, :], in0=MM[b][0:R, t * D:(t + 1) * D], scalar=rs[q][0:R, t:t + 1],
                                                  in1=c_row[0:R], op0=ALU.mult, op1=ALU.add)
                last.then_inc(S("h_ready"), 1)

            def f_end(n, q, b, r, last_round):
                dve.wait_ge(S(f"x_cur_loaded{q}"), r * 16 + 16)
                v.tensor_tensor(x_cur[q][0:R], x_cur[q][0:R], c_row[0:R].unsqueeze(1).broadcast_to([R, 2, D]), ALU.add).then_inc(S("c_added"), 1)
                dve.wait_ge(S("rstd"), n + 1)
                dve.wait_ge(S("multiplied"), n + 1)
                dve.wait_ge(S("c_added"), r * PAIRS + (q + 1))
                dve.wait_ge(S(f"out_stored{q}"), r * 16)
                for t in range(2):
                    o = v.scalar_tensor_tensor(out=O[q][0:R, t, :], in0=MM[b][0:R, t * D:(t + 1) * D], scalar=rs[q][0:R, t:t + 1],
                                               in1=x_cur[q][0:R, t, :], op0=ALU.mult, op1=ALU.add)
                o.then_inc(S("out_ready"), 1)
                if not last_round:
                    dve.wait_ge(S(f"h_next_loaded{q}"), r * 16 + 16)
                    v.tensor_copy(H[q][0:R], h_next[q][0:R]).then_inc(S("h_ready"), 1)

            f_sum(0, 0)
            f_sum(1, 1)
            f_stats(0, 0)
            f_var(0, 0)
            f_sum(2, 2)
            f_stats(1, 1)
            f_var(1, 1)

            def f_trip(t, r, end, g, xx, last):
                for s in range(SLOTS):
                    n = t * SLOTS + s
                    q = s % PAIRS
                    if not (last and s + 3 >= SLOTS):
                        f_sum(n + 3, (s + 3) % PAIRS)
                    if not (last and s + 2 >= SLOTS):
                        f_stats(n + 2, (s + 2) % PAIRS)
                    if g:
                        j = t + EARLY_G
                        if s == F_G.first:
                            g_scalars(j)
                        for c in F_G.hot[s]:
                            g_hot(j, c)
                    if xx:
                        for at, part in ((X_BIAS, x_bias), (X_STATS, x_stats), (X_MEAN, x_mean), (X_VAR, x_var), (X_NORM, x_norm)):
                            if s == at:
                                part(t)
                    if end and s >= SLOTS - PAIRS:
                        f_end(n, q, s % 3, r, last)
                        if not last and s == SLOTS - 1:
                            dve.wait_ge(S("h_ready"), n + (1 + PAIRS))
                            dve.sem_inc(S("h_next_used"), PAIRS)
                    else:
                        f_scale(n, q, s % 3)
                    if not (last and s + 2 >= SLOTS):
                        f_var(n + 2, (s + 2) % PAIRS)
                    if xx and s == X_MULTIPLY:
                        x_read(t, x_use(t, g))
                    if g and s == F_G.copy:
                        g_copy(t + EARLY_G)
                    if g and s == F_G.read:
                        g_read(t + EARLY_G, g_use(t))

            trips_of_f(dve, f_trip)

        @block.tensor
        def _(pe):
            mm, tp = nc.tensor.matmul, nc.tensor.transpose
            pe.sem_inc(S("chunks_multiplied"), KC)
            pe.wait_ge(S("ones_made"), 1)
            pe.wait_ge(S("heads_ready"), 1)
            mm(XB[:, 0:BLOCKS], ones[0:BLOCKS, :], heads[0:BLOCKS, 0:BLOCKS], start=True, stop=True).then_inc(S("heads_spread"), 1)
            pe.wait_ge(S("windows_ready"), 1)
            mm(XB[:, 128:128 + TILES], ones[0:TILES, :], heads[0:TILES, 0:TILES], start=True, stop=True)
            mm(XB[:, 256:257], ones[0:BLOCKS, :], p_t[0:BLOCKS, 9:10], start=True, stop=True).then_inc(S("windows_spread"), 1)
            pe.wait_ge(S("w_scaled"), 1)
            pe.wait_ge(S("offsets_ready"), 1)
            for b in range(2):
                mm(AGG[:, 0:D], ones[:], w_ffn[:, b, :], start=b == 0, stop=b == 1)
            for b in range(2):
                last = mm(XB[:, 0:D], lnb_b[:, b, :], w_raw[:, b, :], start=b == 0, stop=b == 1)
            last.then_inc(S("w_summed"), 1)
            pe.wait_ge(S("w_ffn_ready"), 1)
            n_u = pe.value_load(off_row[0:1, TILES:TILES + 1], min_val=1, max_val=E // UC)
            with pe.Fori(0, n_u) as i:
                pe.wait_ge(S("u_weighted"), i + 1)
                mm(XB[0:UC, 0:D], u_eq[0:UC, 0:UC], u_gw[0:UC, :], start=True, stop=True).then_inc(S("u_multiplied"), 1)
            pe.wait_ge(S("u_rows_ready"), n_u)

            def g_chunk(j, c):
                pe.wait_ge(S(f"gathered{c}"), j * 16 + 16)
                pe.wait_ge(S("hot_ready"), j * KC + (c + 1))
                if c == 0:
                    pe.wait_ge(S("messages_copied"), j)
                mm(AGG[0:R, 0:D], hot[c][:], gat[c][:], start=c == 0, stop=c == KC - 1).then_inc(S("chunks_multiplied"), 1)

            def xb_transpose(rows_, gs, xs):
                if gs is not None:
                    pe.wait_ge(S("g_done"), gs)
                if xs is not None:
                    pe.wait_ge(S("x_summed"), xs)
                for b in range(2):
                    last = tp(XB[:, b * R:(b + 1) * R], rows_[0:R, b * 128:(b + 1) * 128], ident[0:R, 0:R])
                last.then_inc(S("xb_transposed"), 1)

            def xb_multiply(w, use):
                pe.wait_ge(S("xb_copied"), use + 1)
                for b in range(2):
                    last = mm(XB[0:R, 0:D], xb_t[:, b, :], w[:, b, :], start=b == 0, stop=b == 1)
                last.then_inc(S("xb_multiplied"), 1)

            def g_transpose(j, gs, xs):
                pe.wait_ge(S("messages_copied"), j + 1)
                xb_transpose(g_agg, gs, xs)

            def x_transpose(i, gs, xs):
                pe.wait_ge(S("x_rows_loaded"), i * 32 + 32)
                xb_transpose(x_n, gs, xs)

            def k_transpose(loads, s):
                b, c = s % 2, s % K_RING
                pe.wait_ge(S(f"k_loaded{c}"), loads * 16)
                for h in range(2):
                    last = tp(K_TR[b][:, h * R:(h + 1) * R], k_x[c][0:R, h * 128:(h + 1) * 128], ident[0:R, 0:R])
                last.then_inc(S("k_transposed"), 1)

            def k_project(t, b, normed):
                pe.wait_ge(S("k_copied"), t + 1)
                if normed is not None:
                    pe.wait_ge(S("k_normed"), normed)
                for h in range(2):
                    last = mm(K_MM[b][0:R, :], k_t[b][:, h, :], w_kv[:, h, :], start=h == 0, stop=h == 1)
                last.then_inc(S("k_projected"), 1)

            def k_outer(t, b, first, final):
                pe.wait_ge(S("k_normed"), t + 1)
                for hp in range(2):
                    last = mm(K_ACC[hp][:, 0:128], k_n[b][0:R, D + hp * 128:D + (hp + 1) * 128], k_n[b][0:R, hp * 128:(hp + 1) * 128],
                              start=first, stop=final)
                last.then_inc(S("k_outer_done"), 1)

            pe.wait_ge(S("w_kv_ready"), 2)
            k_transpose(1, 0)
            k_transpose(1, 1)
            k_project(0, 0, None)
            k_transpose(1, 2)
            k_project(1, 1, None)

            def b_trip(i, first, last):
                for s in range(KV_STEPS):
                    t = i * KV_STEPS + s
                    if not (last and s + 3 >= KV_STEPS):
                        k_transpose(i * (KV_STEPS // K_RING) + ((s + 3) // K_RING + 1), s + 3)
                    if not (last and s + 2 >= KV_STEPS):
                        k_project(t + 2, s % 2, t + 1)
                    for g in range(2):
                        if B_G[g].transpose == s:
                            g_transpose(i * 2 + g, i * 2 + g, None)
                        for c in B_G[g].mul[s]:
                            g_chunk(i * 2 + g, c)
                    k_outer(t, s % 2, first and s == 0, last and s == KV_STEPS - 1)
                    for g in range(2):
                        if B_G[g].multiply == s:
                            xb_multiply(w_agg, i * 2 + g)

            b_trip(0, True, False)
            with pe.Fori(1, LAST_B) as i:
                b_trip(i, False, False)
            b_trip(LAST_B, False, True)

            pe.wait_ge(S("g_done"), EARLY_G)
            pe.wait_ge(S("k_added"), TILES)
            for hp in range(2):
                mm(XB[:, hp * 128:(hp + 1) * 128], ones[0:R, :], k_sum[0:R, hp * 128:(hp + 1) * 128], start=True, stop=True)
            for hp in range(2):
                last = mm(XB[:, 256 + hp:257 + hp], k_sum[0:R, D + hp * 128:D + (hp + 1) * 128], ones[0:R, 0:1], start=True, stop=True)
            last.then_inc(S("sums_spread"), 1)
            pe.wait_ge(S("kv_ready"), 4)
            for hp in range(2):
                mm((AGG, XB)[hp][:, 0:D], kv_t[:, hp, :], w_wo[:, hp, :], start=True, stop=True).then_inc(S("kv_wo_done"), 1)
            pe.wait_ge(S("kv_wo_copied"), 2)
            for b in range(2):
                for hp in range(2):
                    last = mm(K_TR[b][:, 0:D], w_wq[:, hp, b * 128:(b + 1) * 128], t1[:, hp, :], start=hp == 0, stop=hp == 1)
                last.then_inc(S("mix_done"), 1)
            pe.wait_ge(S("mix_copied"), 2)

            def early_transpose(q):
                pe.wait_ge(S(f"early_rows_loaded{q}"), 32)
                if q >= 3:
                    pe.wait_ge(S("early_copied"), q - 2)
                for t in range(2):
                    for h in range(2):
                        last = tp(TR[q % 3][:, (t * 2 + h) * R:(t * 2 + h + 1) * R], T[q][0:R, t, h * 128:(h + 1) * 128], ident[0:R, 0:R])
                last.then_inc(S("early_transposed"), 1)

            early_transpose(0)
            for q in range(PAIRS):
                if q + 1 < PAIRS:
                    early_transpose(q + 1)
                pe.wait_ge(S("early_copied"), q + 1)
                if q >= 3:
                    pe.wait_ge(S("early_summed"), q - 2)
                for t in range(2):
                    for h in range(2):
                        last = mm(MM[q % 3][0:R, t * D:(t + 1) * D], v_t[q % 3][:, t, h, :], w_mix[:, h, :], start=h == 0, stop=h == 1)
                last.then_inc(S("early_multiplied"), 1)

            def f_transpose(n, q, b):
                pe.wait_ge(S("silu_done"), n + 1)
                for t in range(2):
                    for h in range(2):
                        last = tp(TR[b][:, (t * 2 + h) * R:(t * 2 + h + 1) * R], T[q][0:R, t, h * 128:(h + 1) * 128], ident[0:R, 0:R])
                last.then_inc(S("transposed"), 1)

            def f_multiply(n, b, r, outs):
                pe.wait_ge(S("transposed_copied"), n + 1)
                if outs > 0:
                    pe.wait_ge(S("out_ready"), r * PAIRS + outs)
                else:
                    pe.wait_ge(S("h_ready"), n + (PAIRS - 2))
                for t in range(2):
                    for h in range(2):
                        last = mm(MM[b][0:R, t * D:(t + 1) * D], v_t[b][:, t, h, :], w_ffn[:, h, :], start=h == 0, stop=h == 1)
                last.then_inc(S("multiplied"), 1)

            f_transpose(0, 0, 0)

            def f_trip(t, r, end, g, xx, last):
                for s in range(SLOTS):
                    n = t * SLOTS + s
                    if not (last and s + 1 >= SLOTS):
                        f_transpose(n + 1, (s + 1) % PAIRS, (s + 1) % 3)
                    if xx and s == X_TRANSPOSE:
                        x_transpose(t, t + EARLY_G if g else TILES, t)
                    if xx and s == X_MULTIPLY:
                        xb_multiply(w_mix, x_use(t, g))
                    if g:
                        if s == F_G.transpose:
                            g_transpose(t + EARLY_G, t + EARLY_G, t + 1)
                        if s == F_G.multiply:
                            xb_multiply(w_agg, g_use(t))
                        for c in F_G.mul[s]:
                            g_chunk(t + EARLY_G, c)
                    f_multiply(n, s % 3, r, s - 3 - (SLOTS - PAIRS) + 1 if last else 0)

            trips_of_f(pe, f_trip)


_INS = ["x", "src", "dst", "ew", "w_gnn", "wq", "wk_t", "wv_t", "wo_t", "bo", "gk", "bk", "gv", "bv", "ln_w", "ln_b", "wf_t", "bf"]


def kernel(**inputs):
    import numpy as _np
    import concourse.bacc as _bacc
    from concourse import mybir as _mybir
    from concourse.bass_utils import run_bass_kernel_spmd as _run

    a = {k: _np.asarray(t) for k, t in inputs.items()}
    laid = {
        "x": a["x"], "src": a["src"], "dst": a["dst"], "ew": a["edge_weight"], "w_gnn": a["L0_gnn_weight"],
        "wq": a["L0_mix_wq"], "wk_t": a["L0_mix_wk"].T, "wv_t": a["L0_mix_wv"].T, "wo_t": a["L0_mix_wo"].T, "bo": a["L0_mix_bo"],
        "gk": a["L0_mix_ln_k_g"], "bk": a["L0_mix_ln_k_b"], "gv": a["L0_mix_ln_v_g"], "bv": a["L0_mix_ln_v_b"],
        "ln_w": a["L0_ffn_ln_w"], "ln_b": a["L0_ffn_ln_b"], "wf_t": a["L0_ffn_W"].T, "bf": a["L0_ffn_b"],
    }
    nc = _bacc.Bacc("TRN2", target_bir_lowering=False, num_devices=1)
    arrays, args = {}, []
    for name in _INS:
        t = _np.ascontiguousarray(laid[name])
        arrays[f"in_{name}"] = t
        args.append(nc.dram_tensor(f"in_{name}", t.shape, _mybir.dt.from_np(t.dtype), kind="ExternalInput").ap())
    args.append(nc.dram_tensor("out_rows", (N, D), _mybir.dt.float32, kind="ExternalOutput").ap())
    build(nc, *args)
    r = _run(nc, [arrays], core_ids=[0])
    return _np.asarray(r.results[0]["out_rows"])
```

```python
from contextlib import ExitStack

import concourse.bass as bass
from concourse import mybir

F32 = mybir.dt.float32
F32R = mybir.dt.float32r
I32 = mybir.dt.int32
ALU = mybir.AluOpType
ACT = mybir.ActivationFunctionType
AX_X = mybir.AxisListType.X

N, D, E = 12500, 256, 200000
HEADS, HD = 4, 64
STEPS = 30
EPS = 1e-5
R = 125
TILES = N // R
KC = 17
CAP = KC * 128
PAIRS = 5
ROUND = 2 * PAIRS
ROUNDS = TILES // ROUND
SLOTS = 3 * PAIRS
TRIPS = STEPS // 3
NSLOT = ROUNDS * TRIPS * SLOTS
EARLY_G = 20
EARLY_X = 10
A_RING = 5
A_LOOPS = TILES // 2 // A_RING
KV_STEPS = 10
F_EDGES = 48 * (EARLY_G // 2 + 1)
K_RING = 5
LAST_B = TILES // KV_STEPS - 1
G_ROUNDS = (TILES - EARLY_G) // ROUND
UC = 125
BLOCKS, BLOCK = 125, 1600


def spread(n, steps):
    return [list(range(n * s // steps, n * (s + 1) // steps)) for s in range(steps)]


def grouped(counts):
    assert sum(counts) == KC
    return [list(range(sum(counts[:k]), sum(counts[:k + 1]))) for k in range(len(counts))]


class Plan:
    def __init__(self, steps, first, groups, hot_lag, mul_lag, tail):
        self.gather = [[] for _ in range(steps)]
        self.hot = [[] for _ in range(steps)]
        self.mul = [[] for _ in range(steps)]
        for k, chunks in enumerate(groups):
            self.gather[first + k] += chunks
            self.hot[first + k + hot_lag] += chunks
            self.mul[first + k + mul_lag] += chunks
        self.first = first
        self.copy, self.transpose, self.multiply, self.read = tail


F_GROUPS = grouped((2, 1, 2, 1, 2, 1, 2, 1, 2, 1, 2))
F_G = Plan(SLOTS, 0, F_GROUPS, 1, 2, (12, 13, 14, 14))
B_G = [Plan(KV_STEPS, 0, spread(KC, 4), 1, 1, (4, 5, 6, 6)), Plan(KV_STEPS, 4, spread(KC, 4), 1, 1, (8, 9, 9, 9))]
SPLIT = (3, 6, 9, 12)
X_BIAS, X_TRANSPOSE, X_MULTIPLY, X_STATS, X_MEAN, X_VAR, X_NORM = 0, 1, 3, 4, 5, 6, 8


def build(nc, x, src, dst, ew, w_gnn, wq, wk_t, wv_t, wo_t, bo, gk, bk, gv, bv, ln_w, ln_b, wf_t, bf, out):
    xn_d = nc.dram_tensor("xn_d", [N, D], F32).ap()
    x1a_d = nc.dram_tensor("x1a_d", [N, D], F32).ap()
    x1_d = nc.dram_tensor("x1_d", [N, D], F32).ap()
    h0_d = nc.dram_tensor("h0_d", [N, D], F32).ap()
    gen_d = nc.dram_tensor("gen_d", [N + R, D], F32).ap()

    def rows(t, tile, n=1):
        return t[bass.ds(tile * R, n * R), :].rearrange("(t p) f -> p t f", p=R)

    ctx = ExitStack()
    with ctx:
        def sb(name, shape, dt=F32):
            return ctx.enter_context(nc.sbuf_tensor(name, shape, dt))

        made = {}

        def S(name):
            if name not in made:
                made[name] = ctx.enter_context(nc.semaphore(name))
            return made[name]

        ident = sb("ident", [128, 128])
        ones = sb("ones", [128, 128])
        iota_i = sb("iota_i", [128, R], I32)
        iota_f = sb("iota_f", [128, R])
        lane_i = sb("lane_i", [128, 3], I32)
        lane_f = sb("lane_f", [128, 3])
        below = sb("below", [128, R])
        base_i = sb("base_i", [128, TILES], I32)
        base_f = sb("base_f", [128, TILES])
        minus_half = sb("minus_half", [128, 8])
        zeros = sb("zeros", [128, 2, D])
        w_kv = sb("w_kv", [128, 2, 2 * D])
        w_mean = sb("w_mean", [128, 2, 8])
        w_agg = sb("w_agg", [128, 2, D])
        w_wq = sb("w_wq", [128, 2, D])
        w_wo = sb("w_wo", [128, 2, D])
        w_raw = sb("w_raw", [128, 2, D])
        w_ffn = sb("w_ffn", [128, 2, D])
        w_mix = sb("w_mix", [128, 2, D])
        w_high = sb("w_high", [128, 2, D], F32R)
        w_low = sb("w_low", [128, 2, D], F32R)
        lnw_c = sb("lnw_c", [128, 2])
        lnb_c = sb("lnb_c", [128, 2])
        lnb_b = sb("lnb_b", [128, 2, 128])
        c_row = sb("c_row", [128, D])
        bo_row = sb("bo_row", [128, D])
        gk_row = sb("gk_row", [128, 128])
        bk_row = sb("bk_row", [128, 128])
        gv_col = sb("gv_col", [128, 1])
        bv_col = sb("bv_col", [128, 1])
        d_blk = sb("d_blk", [128, BLOCK], I32)
        d_nxt = sb("d_nxt", [128, BLOCK], I32)
        d_cmp = sb("d_cmp", [128, BLOCK])
        d_row = (d_blk, d_nxt)
        heads = sb("heads", [128, 128])
        p_t = sb("p_t", [128, 24])
        blk_i = sb("blk_i", [128, 2], I32)
        off_row = sb("off_row", [1, TILES + 4], I32)
        gen_row = sb("gen_row", [1, TILES], I32)
        ok_col = sb("ok_col", [128, 2])
        u_src = sb("u_src", [128, 1], I32)
        u_dst = sb("u_dst", [128, 1], I32)
        u_w = sb("u_w", [128, 1])
        u_row = sb("u_row", [128, R], I32)
        u_eq = sb("u_eq", [128, R])
        u_low = sb("u_low", [128, R])
        u_t = sb("u_t", [128, 4])
        u_idx = sb("u_idx", [128, 1], I32)
        u_g = sb("u_g", [128, D])
        u_gw = sb("u_gw", [128, D])
        u_r = sb("u_r", [128, D])
        a_x = [sb(f"a_x{b}", [128, 2, D]) for b in range(A_RING)]
        a_n = [sb(f"a_n{b}", [128, 2, D]) for b in range(A_RING)]
        a_st = [sb(f"a_st{b}", [128, 2, 3]) for b in range(A_RING)]
        a_ve = [sb(f"a_ve{b}", [128, 2]) for b in range(A_RING)]
        a_sh = [sb(f"a_sh{b}", [128, 2]) for b in range(A_RING)]
        a_rs = [sb(f"a_rs{b}", [128, 2]) for b in range(A_RING)]
        k_x = [sb(f"k_x{b}", [128, D]) for b in range(K_RING)]
        k_t = [sb(f"k_t{b}", [128, 2, R]) for b in range(2)]
        k_sq = sb("k_sq", [128, 2 * D])
        k_ss = sb("k_ss", [128, 8])
        k_sd = [sb(f"k_sd{b}", [128, 8]) for b in range(2)]
        eps_col = sb("eps_col", [128, 1])
        k_rs = [sb(f"k_rs{b}", [128, 8]) for b in range(2)]
        k_n = [sb(f"k_n{b}", [128, 2 * D]) for b in range(2)]
        k_sum = sb("k_sum", [128, 2 * D])
        sv = sb("sv", [128, 2])
        kv_t = sb("kv_t", [128, 2, 128])
        kv_a = sb("kv_a", [128, 128])
        kv_b = sb("kv_b", [128, 128])
        t1 = sb("t1", [128, 2, D])
        src_cur = [sb(f"src_cur{e}", [128, KC], I32) for e in range(2)]
        dst_cur = [sb(f"dst_cur{e}", [128, KC], I32) for e in range(2)]
        w_cur = [sb(f"w_cur{e}", [128, KC]) for e in range(2)]
        d_loc = sb("d_loc", [128, KC])
        w_loc = sb("w_loc", [128, KC])
        gat = [sb(f"gat{c}", [128, D]) for c in range(KC)]
        hot = [sb(f"hot{c}", [128, R]) for c in range(KC)]
        g_x = sb("g_x", [128, D])
        g_u = sb("g_u", [128, D])
        g_agg = sb("g_agg", [128, D])
        g_c = sb("g_c", [128, D])
        g_r = sb("g_r", [128, D])
        x_r = sb("x_r", [128, D])
        g_out = sb("g_out", [128, D])
        xb_t = sb("xb_t", [128, 2, R])
        x_n = sb("x_n", [128, D])
        x_a = sb("x_a", [128, D])
        x_1 = sb("x_1", [128, D])
        x_h = sb("x_h", [128, D])
        x_st = sb("x_st", [128, 6])
        x_mv = sb("x_mv", [128, 2])
        x_ve = sb("x_ve", [128, 1])
        x_rs = sb("x_rs", [128, 1])
        H = [sb(f"H{q}", [128, 2, D]) for q in range(PAIRS)]
        T = [sb(f"T{q}", [128, 2, D]) for q in range(PAIRS)]
        O = [sb(f"O{q}", [128, 2, D]) for q in range(PAIRS)]
        h_next = [sb(f"h_next{q}", [128, 2, D]) for q in range(PAIRS)]
        x_cur = [sb(f"x_cur{q}", [128, 2, D]) for q in range(PAIRS)]
        st = [sb(f"st{q}", [128, 2, 3]) for q in range(PAIRS)]
        ve = [sb(f"ve{q}", [128, 2]) for q in range(PAIRS)]
        rs = [sb(f"rs{q}", [128, 2]) for q in range(PAIRS)]
        v_t = [sb(f"v_t{b}", [128, 2, 2, R]) for b in range(3)]
        v_high = [sb(f"v_high{b}", [128, 2, 2, R], F32R) for b in range(3)]
        v_low = [sb(f"v_low{b}", [128, 2, 2, R], F32R) for b in range(3)]

        banks = [ctx.enter_context(nc.psum_tensor(f"bank{b}", [128, 512], F32)) for b in range(8)]
        TR = banks[0:3]
        MM = banks[3:6]
        AGG = banks[6]
        XB = banks[7]
        K_TR, K_MM = banks[0:2], banks[3:5]
        K_ACC = [banks[2], banks[5]]
        dst_blocks = dst.rearrange("(b k) -> b k", k=BLOCK)

        block = ctx.enter_context(nc.Block())

        def carry(eng):
            eng.sem_inc(S("passed"), 1)

        def trips_of_f(eng, body):
            with eng.Fori(0, G_ROUNDS) as r:
                with eng.Fori(r * TRIPS, r * TRIPS + (TRIPS - 1)) as t:
                    body(t, r, False, True, True, False)
                body(r * TRIPS + (TRIPS - 1), r, True, True, True, False)
            for r in range(G_ROUNDS, ROUNDS):
                with eng.Fori(r * TRIPS, r * TRIPS + (TRIPS - 1)) as t:
                    body(t, r, False, False, r < ROUNDS - 1, False)
                body(r * TRIPS + TRIPS - 1, r, True, False, r < ROUNDS - 1, r == ROUNDS - 1)

        def splits(t, s):
            return t * len(SPLIT) + len([k for k in SPLIT if k <= s])

        def x_use(t, g):
            return t * 2 + EARLY_G if g else t + TILES

        def g_use(t):
            return t * 2 + (EARLY_G + 1)

        @block.sync
        def _(sp):
            sp.dma_start(d_blk[0:BLOCKS, :], dst_blocks).then_inc(S("dst_loaded"), 16)
            sp.wait_ge(S("dst_next_filled"), 1)
            sp.dma_start(d_nxt[0:BLOCKS - 1, :], dst[1:1 + (BLOCKS - 1) * BLOCK].rearrange("(b k) -> b k", k=BLOCK)).then_inc(S("dst_loaded"), 16)
            sp.dma_start(d_nxt[BLOCKS - 1:BLOCKS, 0:BLOCK - 1], dst[(BLOCKS - 1) * BLOCK + 1:E].unsqueeze(0)).then_inc(S("dst_loaded"), 16)
            def a_load(p, b):
                sp.dma_start(a_x[b][0:R], rows(x, p * 2, 2)).then_inc(S(f"a_loaded{b}"), 16)

            for b in range(A_RING):
                a_load(b, b)
            for t, a in ((w_kv[:, :, 0:D], wk_t), (w_kv[:, :, D:2 * D], wv_t), (w_agg[:], w_gnn), (w_wq[:], wq),
                         (w_wo[:], wo_t), (w_raw[:], wf_t)):
                sp.dma_start(t, a.rearrange("(b p) n -> p b n", p=128)).then_inc(S("weights_loaded"), 16)
            sp.dma_start(c_row[:], bf.partition_broadcast(128)).then_inc(S("weights_loaded"), 16)
            sp.dma_start(bo_row[:], bo.partition_broadcast(128)).then_inc(S("weights_loaded"), 16)
            for b in range(2):
                sp.dma_start(lnw_c[:, b:b + 1], ln_w[b * 128:(b + 1) * 128].unsqueeze(1)).then_inc(S("weights_loaded"), 16)
                sp.dma_start(lnb_c[:, b:b + 1], ln_b[b * 128:(b + 1) * 128].unsqueeze(1)).then_inc(S("weights_loaded"), 16)
                sp.dma_start(gk_row[:, b * HD:(b + 1) * HD], gk.partition_broadcast(128)).then_inc(S("weights_loaded"), 16)
                sp.dma_start(bk_row[:, b * HD:(b + 1) * HD], bk.partition_broadcast(128)).then_inc(S("weights_loaded"), 16)
                sp.dma_start(gv_col[b * HD:(b + 1) * HD, :], gv.unsqueeze(1)).then_inc(S("weights_loaded"), 16)
                sp.dma_start(bv_col[b * HD:(b + 1) * HD, :], bv.unsqueeze(1)).then_inc(S("weights_loaded"), 16)

            def a_store(i, b):
                sp.wait_ge(S("a_normed"), i * A_RING + (b + 1))
                sp.dma_start(rows(xn_d, i * (2 * A_RING) + 2 * b, 2), a_n[b][0:R]).then_inc(S(f"a_stored{b}"), 16)

            with sp.Fori(0, A_LOOPS - 1) as i:
                for b in range(A_RING):
                    a_store(i, b)
                    a_load(i * A_RING + (b + A_RING), b)
            for b in range(A_RING):
                a_store(A_LOOPS - 1, b)

            sp.wait_ge(S("offsets_ready"), 1)
            n_u = sp.value_load(off_row[0:1, TILES:TILES + 1], min_val=1, max_val=E // UC)
            with sp.Fori(0, n_u) as i:
                sp.wait_ge(S("u_added"), i * 16)
                sp.dma_start(u_src[0:UC], src[bass.ds(i * UC, UC)].unsqueeze(1)).then_inc(S("u_loaded"), 16)
                sp.dma_start(u_dst[0:UC], dst[bass.ds(i * UC, UC)].unsqueeze(1)).then_inc(S("u_loaded"), 16)
                sp.dma_start(u_w[0:UC], ew[bass.ds(i * UC, UC)].unsqueeze(1)).then_inc(S("u_loaded"), 16)
                sp.dma_start(u_row[0:UC], dst[bass.ds(i * UC, UC)].partition_broadcast(UC)).then_inc(S("u_loaded"), 16)

            def g_load(j, e, before):
                if before is not None:
                    for c in range(KC):
                        sp.wait_ge(S(f"gathered{c}"), before * 16)
                    carry(sp)
                    sp.wait_ge(S("edge_scalars_ready"), before * 2)
                off = sp.value_load(off_row[0:1, bass.ds(j, 1)], min_val=0, max_val=E - CAP)
                for t, a in ((src_cur, src), (dst_cur, dst), (w_cur, ew)):
                    sp.dma_start(t[e][:], a[bass.ds(off, CAP)].rearrange("(p k) -> p k", k=KC)).then_inc(S(f"edges_loaded{e}"), 16)

            def g_rows(j):
                sp.wait_ge(S("messages_copied"), j)
                row = sp.value_load(gen_row[0:1, bass.ds(j, 1)], min_val=0, max_val=N - R)
                sp.dma_start(g_u[0:R], gen_d[bass.ds(row, R), :]).then_inc(S("g_rows_loaded"), 16)
                sp.wait_ge(S("g_done"), j)
                sp.dma_start(g_x[0:R], x[bass.ds(j * R, R), :]).then_inc(S("g_rows_loaded"), 16)

            def g_store(j):
                sp.wait_ge(S("g_done"), j + 1)
                sp.dma_start(x1a_d[bass.ds(j * R, R), :], g_out[0:R]).then_inc(S("g_stored"), 16)

            def x_load(i):
                sp.wait_ge(S("x_summed"), i)
                sp.wait_ge(S("g_stored"), i * 16 + (EARLY_X + 1) * 16)
                sp.dma_start(x_n[0:R], xn_d[bass.ds(i * R + EARLY_X * R, R), :]).then_inc(S("x_rows_loaded"), 16)
                sp.dma_start(x_a[0:R], x1a_d[bass.ds(i * R + EARLY_X * R, R), :]).then_inc(S("x_rows_loaded"), 16)

            def x_store(i):
                sp.wait_ge(S("x_summed"), i + 1)
                sp.dma_start(x1_d[bass.ds(i * R + EARLY_X * R, R), :], x_1[0:R]).then_inc(S("x_sum_stored"), 16)
                sp.wait_ge(S("x_normed"), i + 1)
                sp.dma_start(h0_d[bass.ds(i * R + EARLY_X * R, R), :], x_h[0:R]).then_inc(S("x_h_stored"), 16)

            def load_h(r, pairs):
                sp.wait_ge(S("h_next_used"), r * PAIRS)
                for q in pairs:
                    carry(sp)
                    sp.wait_ge(S("x_h_stored"), r * (ROUND * 16) + (q + 1) * 32)
                    sp.dma_start(h_next[q][0:R], rows(h0_d, r * ROUND + (ROUND + 2 * q), 2)).then_inc(S(f"h_next_loaded{q}"), 16)

            def load_x(r):
                sp.wait_ge(S("early_x_stored"), 16 * PAIRS)
                sp.wait_ge(S("out_ready"), r * PAIRS)
                carry(sp)
                sp.wait_ge(S("x_sum_stored"), r * (ROUND * 16))
                for q in range(PAIRS):
                    sp.dma_start(x_cur[q][0:R], rows(x1_d, r * ROUND + 2 * q, 2)).then_inc(S(f"x_cur_loaded{q}"), 16)

            for b in range(A_RING):
                sp.wait_ge(S(f"a_stored{b}"), 16 * A_LOOPS)
            sp.wait_ge(S("u_added"), n_u * 16)

            def k_load(t, b):
                sp.dma_start(k_x[b][0:R], xn_d[bass.ds(t * R, R), :]).then_inc(S(f"k_loaded{b}"), 16)

            for b in range(K_RING):
                k_load(b, b)

            def b_trip(i, last):
                for s in range(KV_STEPS):
                    t = i * KV_STEPS + s
                    if s == B_G[0].first + 5:
                        g_load(i * 2 + 2, 0, i * 2 + 1)
                    if s == B_G[1].first + 5 and not last:
                        g_load(i * 2 + 3, 1, i * 2 + 2)
                    if s == 0:
                        g_rows(i * 2)
                    if not (last and s + K_RING >= KV_STEPS):
                        sp.wait_ge(S("k_transposed"), t + 1)
                        k_load(t + K_RING, s % K_RING)
                    if s == B_G[0].read + 1:
                        g_store(i * 2)
                        g_rows(i * 2 + 1)
                    if s == B_G[1].read:
                        g_store(i * 2 + 1)

            for g in range(2):
                g_load(g, g, None)
            with sp.Fori(0, LAST_B) as i:
                b_trip(i, False)
            b_trip(LAST_B, True)

            for q in range(PAIRS):
                sp.wait_ge(S("g_stored"), 16 * (2 * q + 2))
                sp.dma_start(T[q][0:R], rows(xn_d, 2 * q, 2)).then_inc(S(f"early_rows_loaded{q}"), 16)
                sp.dma_start(O[q][0:R], rows(x1a_d, 2 * q, 2)).then_inc(S(f"early_rows_loaded{q}"), 16)
            x_load(0)
            for q in range(PAIRS):
                sp.wait_ge(S("early_summed"), q + 1)
                sp.dma_start(rows(x1_d, 2 * q, 2), x_cur[q][0:R]).then_inc(S("early_x_stored"), 16)

            def f_trip(t, r, end, g, xx, last):
                if g:
                    g_rows(t + EARLY_G)
                if end:
                    load_x(r)
                if end and not last:
                    load_h(r, range(PAIRS - 1))
                if xx:
                    x_store(t)
                    if not (end and not g):
                        x_load(t + 1)
                if end and not last:
                    load_h(r, range(PAIRS - 1, PAIRS))
                if g:
                    g_load(t + (EARLY_G + 1), 0, t + (EARLY_G + 1))
                    g_store(t + EARLY_G)
                if end:
                    for q in range(PAIRS):
                        sp.wait_ge(S("out_ready"), r * PAIRS + (q + 1))
                        sp.dma_start(rows(out, r * ROUND + 2 * q, 2), O[q][0:R]).then_inc(S(f"out_stored{q}"), 16)

            trips_of_f(sp, f_trip)
            for q in range(PAIRS):
                sp.wait_ge(S(f"out_stored{q}"), 16 * ROUNDS)
            sp.wait_ge(S("edges_loaded0"), F_EDGES + 48 * (TILES - EARLY_G))

        @block.gpsimd
        def _(pool):
            pool.memset(d_nxt[:], 1 << 20).then_inc(S("dst_next_filled"), 1)
            pool.memset(ident[:], 0.0).then_inc(S("pool_own"), 1)
            pool.memset(below[:], 0.0).then_inc(S("pool_own"), 1)
            pool.iota(iota_i[:], pattern=[[1, R]], base=0, channel_multiplier=0).then_inc(S("iotas_made"), 1)
            pool.iota(base_i[:], pattern=[[R, TILES]], base=0, channel_multiplier=0).then_inc(S("iotas_made"), 1)
            pool.iota(lane_i[:, 0:1], pattern=[[0, 1]], base=N, channel_multiplier=1).then_inc(S("iotas_made"), 1)
            pool.iota(lane_i[:, 1:3], pattern=[[R, 2]], base=0, channel_multiplier=R).then_inc(S("iotas_made"), 1)
            pool.wait_ge(S("pool_own"), 2)
            pool.affine_select(out=ident[:], in_=ident[:], compare_op=ALU.not_equal, fill=1.0, base=0,
                               pattern=[[-1, 128]], channel_multiplier=1).then_inc(S("masks_made"), 1)
            pool.affine_select(out=below[:], in_=below[:], compare_op=ALU.is_ge, fill=1.0, base=0,
                               pattern=[[1, R]], channel_multiplier=-1).then_inc(S("masks_made"), 1)
            pool.wait_ge(S("blocks_found"), 1)
            for k in range(2):
                pool.indirect_dma_start(d_row[k][0:TILES, :], None, dst_blocks,
                                        bass.IndirectOffsetOnAxis(ap=blk_i[0:TILES, k:k + 1], axis=0)).then_inc(S("blocks_gathered"), 16)

            def rstd(out_, var, n, after, value, done):
                pool.wait_ge(S(after), value)
                pool.tensor_tensor(out_, var, minus_half[0:R, 0:n], ALU.pow).then_inc(S(done), 1)

            with pool.Fori(0, A_LOOPS) as i:
                for b in range(A_RING):
                    rstd(a_rs[b][0:R], a_ve[b][0:R], 2, "a_variance", i * A_RING + (b + 1), "a_rstd")

            for b in range(A_RING):
                pool.wait_ge(S(f"a_stored{b}"), 16 * A_LOOPS)
            pool.wait_ge(S("offsets_ready"), 1)
            n_zero = pool.value_load(off_row[0:1, TILES + 1:TILES + 2], min_val=1, max_val=TILES // 2)
            n_u = pool.value_load(off_row[0:1, TILES:TILES + 1], min_val=1, max_val=E // UC)
            pool.wait_ge(S("zeroed"), n_zero * 16 + 16)
            carry(pool)
            with pool.Fori(0, n_u) as i:
                pool.wait_ge(S("u_loaded"), i * 64 + 64)
                carry(pool)
                pool.indirect_dma_start(u_g[0:UC, :], None, xn_d,
                                        bass.IndirectOffsetOnAxis(ap=u_src[0:UC, 0:1], axis=0)).then_inc(S("u_gathered"), 16)
                pool.wait_ge(S("u_rows_ready"), i + 1)
                carry(pool)
                pool.indirect_dma_start(gen_d, bass.IndirectOffsetOnAxis(ap=u_idx[0:UC, 0:1], axis=0), u_r[0:UC, :], None,
                                        compute_op=ALU.add).then_inc(S("u_added"), 16)
                pool.wait_ge(S("u_added"), i * 16 + 16)

            def gather(j, c, e, loads):
                if c == 0:
                    pool.wait_ge(S(f"edges_loaded{e}"), loads)
                pool.wait_ge(S("chunks_multiplied"), j * KC + (c + 1))
                carry(pool)
                pool.indirect_dma_start(gat[c][:], None, xn_d, bass.IndirectOffsetOnAxis(ap=src_cur[e][:, c:c + 1], axis=0)).then_inc(S(f"gathered{c}"), 16)


            def b_trip(i, last):
                for s in range(KV_STEPS):
                    for g in range(2):
                        for c in B_G[g].gather[s]:
                            gather(i * 2 + g, c, g, i * 48 + 48)

            with pool.Fori(0, LAST_B) as i:
                b_trip(i, False)
            b_trip(LAST_B, True)

            for q in range(PAIRS):
                rstd(rs[q][0:R], ve[q][0:R], 2, "early_variance", q + 1, "early_rstd")

            def x_bias(i):
                pool.wait_ge(S("x_rows_loaded"), i * 32 + 32)
                pool.tensor_tensor(x_a[0:R], x_a[0:R], bo_row[0:R], ALU.add).then_inc(S("x_biased"), 1)

            def x_sum(i):
                pool.wait_ge(S("x_sum_stored"), i * 16)
                pool.wait_ge(S("x_normed"), i)
                pool.wait_ge(S("x_biased"), i + 1)
                pool.wait_ge(S("attention_copied"), i + 1)
                pool.tensor_tensor(x_1[0:R], x_r[0:R], x_a[0:R], ALU.add).then_inc(S("x_summed"), 1)

            def g_add_uncovered(j, t):
                pool.wait_ge(S("g_rows_loaded"), j * 32 + 32)
                pool.wait_ge(S("sums_copied"), t + 1)
                pool.tensor_tensor(g_agg[0:R], g_c[0:R], g_u[0:R], ALU.add).then_inc(S("messages_copied"), 1)

            def g_add_x(j, t):
                pool.wait_ge(S("g_stored"), j * 16)
                pool.wait_ge(S("relu_done"), t + 1)
                pool.tensor_tensor(g_out[0:R], g_r[0:R], g_x[0:R], ALU.add).then_inc(S("g_done"), 1)

            def x_rstd(i):
                rstd(x_rs[0:R], x_ve[0:R], 1, "x_variance", i + 1, "x_rstd")

            def f_rstd(n, q):
                rstd(rs[q][0:R], ve[q][0:R], 2, "variance", n + 1, "rstd")

            f_rstd(0, 0)
            f_rstd(1, 1)

            def f_trip(t, r, end, g, xx, last):
                for s in range(SLOTS):
                    if g:
                        for c in F_G.gather[s]:
                            gather(t + EARLY_G, c, 0, t * 48 + F_EDGES)
                    if not (last and s + 2 >= SLOTS):
                        f_rstd(t * SLOTS + (s + 2), (s + 2) % PAIRS)
                    if xx and s == X_BIAS:
                        x_bias(t)
                    if xx and s == X_MULTIPLY:
                        x_sum(t)
                    if xx and s == X_VAR:
                        x_rstd(t)
                    if g and s == F_G.copy:
                        g_add_uncovered(t + EARLY_G, t)
                    if g and s == F_G.read:
                        g_add_x(t + EARLY_G, t)

            trips_of_f(pool, f_trip)

        @block.scalar
        def _(act):
            def a_norm(i, b):
                act.wait_ge(S("a_shifts"), i * A_RING + (b + 1))
                act.wait_ge(S(f"a_stored{b}"), i * 16)
                for t in range(2):
                    last = nc.scalar.activation(a_n[b][0:R, t, :], a_x[b][0:R, t, :], ACT.Identity, bias=a_sh[b][0:R, t:t + 1], scale=a_rs[b][0:R, t:t + 1])
                last.then_inc(S("a_normed"), 1)

            with act.Fori(0, A_LOOPS) as i:
                for b in range(A_RING):
                    a_norm(i, b)
            act.wait_ge(S("zeros_made"), 1)
            act.dma_start(gen_d[N:N + R, :], zeros[0:R, 0, :]).then_inc(S("zeroed"), 16)
            act.wait_ge(S("offsets_ready"), 1)
            n_zero = act.value_load(off_row[0:1, TILES + 1:TILES + 2], min_val=1, max_val=TILES // 2)
            with act.Fori(0, n_zero) as i:
                act.dma_start(rows(gen_d, i * 2, 2), zeros[0:R]).then_inc(S("zeroed"), 16)

            def xb_copy(v):
                act.wait_ge(S("xb_transposed"), v + 1)
                nc.scalar.activation(xb_t[:].rearrange("p b r -> p (b r)"), XB[:, 0:2 * R], ACT.Copy).then_inc(S("xb_copied"), 1)

            def x_copy(t, use):
                act.wait_ge(S("x_summed"), t)
                act.wait_ge(S("xb_multiplied"), use + 1)
                nc.scalar.activation(x_r[0:R], XB[0:R, 0:D], ACT.Copy).then_inc(S("attention_copied"), 1)

            def g_sums(j):
                act.wait_ge(S("chunks_multiplied"), j * KC + 2 * KC)
                nc.scalar.activation(g_c[0:R], AGG[0:R, 0:D], ACT.Copy).then_inc(S("sums_copied"), 1)

            def g_relu(t):
                act.wait_ge(S("xb_multiplied"), g_use(t) + 1)
                nc.scalar.activation(g_r[0:R], XB[0:R, 0:D], ACT.Relu).then_inc(S("relu_done"), 1)

            def k_copy(t, b):
                act.wait_ge(S("k_transposed"), t + 1)
                nc.scalar.activation(k_t[b][:].rearrange("p b r -> p (b r)"), K_TR[b][:, 0:2 * R], ACT.Copy).then_inc(S("k_copied"), 1)

            def k_square(t, b):
                act.wait_ge(S("k_projected"), t + 1)
                act.wait_ge(S("k_squares_summed"), t)
                nc.scalar.activation(k_sq[0:R], K_MM[b][0:R, :], ACT.Square).then_inc(S("k_squared"), 1)
                act.wait_ge(S("k_squares_summed"), t + 1)
                nc.scalar.activation(k_sd[b][0:R], k_ss[0:R], ACT.Sqrt, bias=eps_col[0:R, 0:1], scale=1.0 / HD).then_inc(S("k_deviation"), 1)

            k_copy(0, 0)
            k_copy(1, 1)
            k_square(0, 0)
            k_copy(2, 0)
            k_square(1, 1)

            def b_trip(i, last):
                for s in range(KV_STEPS):
                    t = i * KV_STEPS + s
                    if not (last and s + 3 >= KV_STEPS):
                        k_copy(t + 3, (s + 3) % 2)
                    if not (last and s + 2 >= KV_STEPS):
                        k_square(t + 2, s % 2)
                    for g in range(2):
                        if B_G[g].transpose == s:
                            xb_copy(i * 2 + g)

            with act.Fori(0, LAST_B) as i:
                b_trip(i, False)
            b_trip(LAST_B, True)

            for q in range(PAIRS):
                b = q % 3
                act.wait_ge(S("early_transposed"), q + 1)
                if q >= 3:
                    act.wait_ge(S("early_multiplied"), q - 2)
                nc.scalar.activation(v_t[b][:].rearrange("p t b r -> p (t b r)"), TR[b][:, 0:4 * R], ACT.Copy).then_inc(S("early_copied"), 1)

            def tanh(n, q):
                act.wait_ge(S("h_ready"), n + 1)
                nc.scalar.activation(T[q][0:R], H[q][0:R], ACT.Tanh).then_inc(S("tanh_done"), 1)

            def silu(n, q):
                act.wait_ge(S("u_done"), n + 1)
                nc.scalar.activation(T[q][0:R], T[q][0:R], ACT.Silu).then_inc(S("silu_done"), 1)

            def copy_t(n, b, split, multiplied):
                if multiplied is not None:
                    act.wait_ge(S("multiplied"), multiplied)
                act.wait_ge(S("transposed"), n + 1)
                nc.scalar.activation((v_high if split else v_t)[b][:].rearrange("p t b r -> p (t b r)"), TR[b][:, 0:4 * R], ACT.Copy).then_inc(S("transposed_copied"), 1)

            tanh(0, 0)
            tanh(1, 1)
            silu(0, 0)
            tanh(2, 2)
            silu(1, 1)
            copy_t(0, 0, 0 in SPLIT, None)
            tanh(3, 3)
            silu(2, 2)
            copy_t(1, 1, 1 in SPLIT, None)

            def f_trip(t, r, end, g, xx, last):
                for s in range(SLOTS):
                    n = t * SLOTS + s
                    if g and s == F_G.multiply:
                        xb_copy(g_use(t))
                    if not (last and s + 3 >= SLOTS):
                        silu(n + 3, (s + 3) % PAIRS)
                    if not (last and s + 4 >= SLOTS):
                        tanh(n + 4, (s + 4) % PAIRS)
                    if not (last and s + 2 >= SLOTS):
                        copy_t(n + 2, (s + 2) % 3, (s + 2) % SLOTS in SPLIT, n)
                    if xx and s == X_TRANSPOSE:
                        xb_copy(x_use(t, g))
                    if xx and s == X_MULTIPLY:
                        x_copy(t, x_use(t, g))
                    if g and s == F_G.copy:
                        g_sums(t + EARLY_G)
                    if g and s == F_G.read:
                        g_relu(t)

            trips_of_f(act, f_trip)

        @block.vector
        def _(dve):
            count = [0]

            def link(ins):
                count[0] += 1
                ins.then_inc(S("vector_own"), 1)
                dve.wait_ge(S("vector_own"), count[0])

            v = nc.vector
            v.memset(zeros[:], 0.0).then_inc(S("zeros_made"), 1)
            v.memset(ones[:], 1.0).then_inc(S("ones_made"), 1)
            v.memset(minus_half[:], -0.5).then_inc(S("vector_const"), 1)
            v.memset(eps_col[:], EPS).then_inc(S("vector_const"), 1)
            v.memset(k_sum[:], 0.0).then_inc(S("vector_const"), 1)
            v.memset(kv_t[:], 0.0).then_inc(S("vector_const"), 1)
            v.memset(p_t[:], 0.0).then_inc(S("vector_const"), 1)
            dve.wait_ge(S("iotas_made"), 4)
            v.tensor_copy(iota_f[:], iota_i[:]).then_inc(S("vector_const"), 1)
            v.tensor_copy(base_f[:], base_i[:]).then_inc(S("vector_const"), 1)
            v.tensor_copy(lane_f[:], lane_i[:]).then_inc(S("vector_const"), 1)
            dve.wait_ge(S("vector_const"), 8)

            dve.wait_ge(S("dst_loaded"), 48)
            dve.wait_ge(S("masks_made"), 2)
            link(v.tensor_copy(p_t[0:BLOCKS, 12:13], d_blk[0:BLOCKS, 0:1]))
            v.tensor_scalar(heads[0:BLOCKS, 0:BLOCKS], ident[0:BLOCKS, 0:BLOCKS], p_t[0:BLOCKS, 12:13], None, ALU.mult).then_inc(S("heads_ready"), 1)
            link(v.tensor_tensor(d_cmp[0:BLOCKS, :], d_nxt[0:BLOCKS, :], d_blk[0:BLOCKS, :], ALU.is_lt))
            link(v.tensor_reduce(p_t[0:BLOCKS, 9:10], d_cmp[0:BLOCKS, :], AX_X, ALU.add))
            dve.wait_ge(S("heads_spread"), 1)
            for k in range(2):
                link(v.tensor_scalar(d_cmp[0:TILES, 0:BLOCKS], XB[0:TILES, 0:BLOCKS], lane_f[0:TILES, 1 + k:2 + k], None, ALU.is_lt))
                link(v.tensor_reduce(p_t[0:TILES, k:k + 1], d_cmp[0:TILES, 0:BLOCKS], AX_X, ALU.add))
            link(v.tensor_scalar(p_t[0:TILES, 2:4], p_t[0:TILES, 0:2], -1.0, 0.0, ALU.add, ALU.max))
            v.tensor_copy(blk_i[0:TILES, :], p_t[0:TILES, 2:4]).then_inc(S("blocks_found"), 1)
            def a_bn(i, b):
                dve.wait_ge(S(f"a_loaded{b}"), i * 16 + 16)
                v.bn_stats(a_st[b][0:R].rearrange("p t k -> p (t k)"), a_x[b][0:R].rearrange("p t f -> p f t")).then_inc(S("a_stats"), 1)

            def a_var(i, b):
                dve.wait_ge(S("a_stats"), i * A_RING + (b + 1))
                v.tensor_scalar(a_ve[b][0:R], a_st[b][0:R, :, 2], 1.0 / D, EPS, ALU.mult, ALU.add).then_inc(S("a_variance"), 1)

            def a_shift(i, b):
                dve.wait_ge(S("a_rstd"), i * A_RING + (b + 1))
                v.scalar_tensor_tensor(out=a_sh[b][0:R], in0=a_st[b][0:R, :, 1], scalar=-1.0, in1=a_rs[b][0:R], op0=ALU.mult, op1=ALU.mult).then_inc(S("a_shifts"), 1)

            a_bn(0, 0)
            a_var(0, 0)
            def a_loop(i, last):
                for b in range(A_RING):
                    if b < A_RING - 1:
                        a_bn(i, b + 1)
                        a_var(i, b + 1)
                    elif not last:
                        a_bn(i + 1, 0)
                        a_var(i + 1, 0)
                    a_shift(i, b)

            with dve.Fori(0, A_LOOPS - 1) as i:
                a_loop(i, False)
            a_loop(A_LOOPS - 1, True)

            dve.wait_ge(S("blocks_gathered"), 32)
            for k in range(2):
                link(v.tensor_scalar(d_cmp[0:TILES, :], d_row[k][0:TILES, :], lane_f[0:TILES, 1 + k:2 + k], None, ALU.is_lt))
                link(v.tensor_reduce(p_t[0:TILES, 4 + k:5 + k], d_cmp[0:TILES, :], AX_X, ALU.add))
            link(v.scalar_tensor_tensor(out=p_t[0:TILES, 6:8], in0=p_t[0:TILES, 2:4], scalar=float(BLOCK), in1=p_t[0:TILES, 4:6], op0=ALU.mult, op1=ALU.add))
            link(v.tensor_tensor(p_t[0:TILES, 8:9], p_t[0:TILES, 7:8], p_t[0:TILES, 6:7], ALU.subtract))
            link(v.tensor_scalar(p_t[0:TILES, 8:9], p_t[0:TILES, 8:9], float(CAP), None, ALU.is_gt))
            link(v.tensor_tensor(p_t[0:BLOCKS, 9:10], p_t[0:BLOCKS, 9:10], p_t[0:BLOCKS, 8:9], ALU.add))
            link(v.tensor_scalar(p_t[0:TILES, 10:11], p_t[0:TILES, 6:7], float(E - CAP), None, ALU.min))
            v.tensor_scalar(heads[0:TILES, 0:TILES], ident[0:TILES, 0:TILES], p_t[0:TILES, 10:11], None, ALU.mult).then_inc(S("windows_ready"), 1)
            dve.wait_ge(S("windows_spread"), 1)
            v.tensor_copy(off_row[0:1, 0:TILES], XB[0:1, 128:128 + TILES]).then_inc(S("windows_copied"), 1)
            link(v.tensor_scalar(ok_col[:, 1:2], XB[:, 256:257], 1.0, None, ALU.min))
            link(v.tensor_scalar(ok_col[:, 0:1], ok_col[:, 1:2], -1.0, 1.0, ALU.mult, ALU.add))
            dve.wait_ge(S("windows_copied"), 1)
            link(v.tensor_scalar(off_row[0:1, TILES:TILES + 1], ok_col[0:1, 1:2], float(E // UC - 1), 1.0, ALU.mult, ALU.add))
            link(v.tensor_scalar(gen_row[:], base_f[0:1, :], ok_col[0:1, 1:2], None, ALU.mult))
            v.tensor_scalar(off_row[0:1, TILES + 1:TILES + 2], ok_col[0:1, 1:2], float(TILES // 2 - 1), 1.0, ALU.mult, ALU.add).then_inc(S("offsets_ready"), 1)

            dve.wait_ge(S("weights_loaded"), 20 * 16)
            for b in range(2):
                heads_of = w_kv[:, b, :].rearrange("p (h d) -> p h d", d=HD)
                link(v.tensor_reduce(w_mean[:, b, :], heads_of, AX_X, ALU.add))
                link(v.tensor_scalar(w_mean[:, b, :], w_mean[:, b, :], 1.0 / HD, None, ALU.mult))
                v.tensor_tensor(heads_of, heads_of, w_mean[:, b, :].unsqueeze(2).broadcast_to([128, 8, HD]), ALU.subtract).then_inc(S("w_kv_ready"), 1)
            for b in range(2):
                link(v.tensor_scalar(w_ffn[:, b, :], w_raw[:, b, :], lnw_c[:, b:b + 1], None, ALU.mult))
                link(v.tensor_scalar(lnb_b[:, b, :], ones[:], lnb_c[:, b:b + 1], None, ALU.mult))
            v.memset(p_t[:, 20:21], 0.0).then_inc(S("w_scaled"), 1)
            dve.wait_ge(S("w_summed"), 1)
            for b in range(2):
                link(v.scalar_tensor_tensor(out=w_ffn[:, b, :], in0=AGG[:, 0:D], scalar=-1.0 / D, in1=w_ffn[:, b, :], op0=ALU.mult, op1=ALU.add))
            link(v.tensor_tensor(c_row[:], XB[:, 0:D], c_row[:], ALU.add))
            link(v.tensor_copy(w_high[:], w_ffn[:]))
            link(v.tensor_tensor(w_low[:], w_ffn[:], w_high[:], ALU.subtract))
            v.memset(p_t[:, 21:22], 0.0).then_inc(S("w_ffn_ready"), 1)

            dve.wait_ge(S("offsets_ready"), 1)
            n_u = dve.value_load(off_row[0:1, TILES:TILES + 1], min_val=1, max_val=E // UC)
            with dve.Fori(0, n_u) as i:
                def u_link(ins, step):
                    ins.then_inc(S("u_own"), 1)
                    dve.wait_ge(S("u_own"), i * 10 + step)

                dve.wait_ge(S("u_loaded"), i * 64 + 64)
                u_link(v.tensor_copy(u_t[0:UC, 0:1], u_dst[0:UC]), 1)
                u_link(v.tensor_scalar(u_t[0:UC, 1:2], u_w[0:UC], ok_col[0:UC, 1:2], None, ALU.mult), 2)
                u_link(v.tensor_scalar(u_eq[0:UC], u_row[0:UC], u_t[0:UC, 0:1], None, ALU.is_equal), 3)
                u_link(v.tensor_tensor(u_low[0:UC], u_eq[0:UC], below[0:UC], ALU.mult), 4)
                u_link(v.tensor_reduce(u_t[0:UC, 2:3], u_low[0:UC], AX_X, ALU.max), 5)
                u_link(v.tensor_scalar(u_t[0:UC, 2:3], u_t[0:UC, 2:3], ok_col[0:UC, 0:1], None, ALU.max), 6)
                u_link(v.tensor_tensor(u_t[0:UC, 3:4], lane_f[0:UC, 0:1], u_t[0:UC, 0:1], ALU.subtract), 7)
                u_link(v.tensor_tensor(u_t[0:UC, 3:4], u_t[0:UC, 3:4], u_t[0:UC, 2:3], ALU.mult), 8)
                u_link(v.tensor_tensor(u_t[0:UC, 3:4], u_t[0:UC, 3:4], u_t[0:UC, 0:1], ALU.add), 9)
                u_link(v.tensor_copy(u_idx[0:UC], u_t[0:UC, 3:4]), 10)
                dve.wait_ge(S("u_gathered"), i * 16 + 16)
                v.tensor_scalar(u_gw[0:UC], u_g[0:UC], u_t[0:UC, 1:2], None, ALU.mult).then_inc(S("u_weighted"), 1)
                dve.wait_ge(S("u_multiplied"), i + 1)
                v.tensor_copy(u_r[0:UC], XB[0:UC, 0:D]).then_inc(S("u_rows_ready"), 1)

            def g_scalars(j, e, loads):
                dve.wait_ge(S(f"edges_loaded{e}"), loads)
                dve.wait_ge(S("hot_ready"), j * KC)
                v.tensor_scalar(d_loc[:], dst_cur[e][:], base_f[:, bass.ds(j, 1)], None, ALU.subtract).then_inc(S("edge_scalars_ready"), 1)
                v.tensor_scalar(w_loc[:], w_cur[e][:], ok_col[:, 0:1], None, ALU.mult).then_inc(S("edge_scalars_ready"), 1)

            def g_hot(j, c):
                if c == 0:
                    dve.wait_ge(S("edge_scalars_ready"), j * 2 + 2)
                dve.wait_ge(S("chunks_multiplied"), j * KC + (c + 1))
                v.tensor_scalar(hot[c][:], iota_f[:], d_loc[:, c:c + 1], w_loc[:, c:c + 1], ALU.is_equal, ALU.mult).then_inc(S("hot_ready"), 1)

            def g_copy(j):
                dve.wait_ge(S("g_rows_loaded"), j * 32 + 32)
                dve.wait_ge(S("chunks_multiplied"), j * KC + 2 * KC)
                v.tensor_tensor(g_agg[0:R], AGG[0:R, 0:D], g_u[0:R], ALU.add).then_inc(S("messages_copied"), 1)

            def g_read(j, use):
                dve.wait_ge(S("g_stored"), j * 16)
                dve.wait_ge(S("xb_multiplied"), use + 1)
                v.scalar_tensor_tensor(out=g_out[0:R], in0=XB[0:R, 0:D], scalar=0.0, in1=g_x[0:R], op0=ALU.max, op1=ALU.add).then_inc(S("g_done"), 1)

            def k_stats(t):
                dve.wait_ge(S("k_squared"), t + 1)
                v.tensor_reduce(k_ss[0:R], k_sq[0:R].rearrange("p (h d) -> p h d", d=HD), AX_X, ALU.add).then_inc(S("k_squares_summed"), 1)

            def k_norm(t, b, outers):
                dve.wait_ge(S("k_deviation"), t + 1)
                v.reciprocal(k_rs[b][0:R], k_sd[b][0:R]).then_inc(S("k_rstd"), 1)
                dve.wait_ge(S("k_rstd"), t + 1)
                if outers is not None:
                    dve.wait_ge(S("k_outer_done"), outers)
                v.tensor_tensor(k_n[b][0:R].rearrange("p (h d) -> p h d", d=HD), K_MM[b][0:R].rearrange("p (h d) -> p h d", d=HD),
                                k_rs[b][0:R].unsqueeze(2).broadcast_to([R, 8, HD]), ALU.mult).then_inc(S("k_normed"), 1)
                dve.wait_ge(S("k_normed"), t + 1)
                dve.wait_ge(S("k_added"), t)
                v.tensor_tensor(k_sum[0:R], k_sum[0:R], k_n[b][0:R], ALU.add).then_inc(S("k_added"), 1)

            k_stats(0)
            k_norm(0, 0, None)
            k_stats(1)

            def b_trip(i, last):
                for s in range(KV_STEPS):
                    t = i * KV_STEPS + s
                    more = not (last and s + 1 >= KV_STEPS)
                    if more:
                        k_norm(t + 1, (s + 1) % 2, t)
                    for g in range(2):
                        if B_G[g].first == s:
                            g_scalars(i * 2 + g, g, i * 48 + 48)
                        for c in B_G[g].hot[s]:
                            g_hot(i * 2 + g, c)
                    if not (last and s + 2 >= KV_STEPS):
                        k_stats(t + 2)
                    for g in range(2):
                        if B_G[g].copy == s:
                            g_copy(i * 2 + g)
                        if B_G[g].read == s:
                            g_read(i * 2 + g, i * 2 + g)

            with dve.Fori(0, LAST_B) as i:
                b_trip(i, False)
            b_trip(LAST_B, True)

            dve.wait_ge(S("k_outer_done"), TILES)
            dve.wait_ge(S("sums_spread"), 1)
            for hp in range(2):
                link(v.tensor_copy(sv[:, hp:hp + 1], XB[:, 256 + hp:257 + hp]))
                link(v.tensor_tensor(kv_a[:], K_ACC[hp][:, 0:128], gk_row[:], ALU.mult))
                link(v.tensor_scalar(kv_b[:], bk_row[:], sv[:, hp:hp + 1], None, ALU.mult))
                link(v.tensor_tensor(kv_a[:], kv_a[:], kv_b[:], ALU.add))
                link(v.tensor_scalar(kv_a[:], kv_a[:], gv_col[:, 0:1], None, ALU.mult))
                link(v.tensor_tensor(kv_b[:], XB[:, hp * 128:(hp + 1) * 128], gk_row[:], ALU.mult))
                link(v.scalar_tensor_tensor(out=kv_b[:], in0=bk_row[:], scalar=float(N), in1=kv_b[:], op0=ALU.mult, op1=ALU.add))
                link(v.tensor_scalar(kv_b[:], kv_b[:], bv_col[:, 0:1], None, ALU.mult))
                link(v.tensor_tensor(kv_a[:], kv_a[:], kv_b[:], ALU.add))
                for h in range(2):
                    part = slice(h * HD, (h + 1) * HD)
                    v.tensor_scalar(kv_t[part, hp, part], kv_a[part, part], 1.0 / N, None, ALU.mult).then_inc(S("kv_ready"), 1)
                dve.wait_ge(S("kv_ready"), 2 * hp + 2)
            for hp in range(2):
                dve.wait_ge(S("kv_wo_done"), hp + 1)
                v.tensor_copy(t1[:, hp, :], (AGG, XB)[hp][:, 0:D]).then_inc(S("kv_wo_copied"), 1)
            for b in range(2):
                dve.wait_ge(S("mix_done"), b + 1)
                v.tensor_copy(w_mix[:, b, :], K_TR[b][:, 0:D]).then_inc(S("mix_copied"), 1)

            def x_stats(i):
                dve.wait_ge(S("x_summed"), i + 1)
                v.bn_stats(x_st[0:R], x_1[0:R]).then_inc(S("x_stats"), 1)

            def x_mean(i):
                dve.wait_ge(S("x_stats"), i + 1)
                carry(dve)
                v.bn_aggr(x_mv[0:R], x_st[0:R]).then_inc(S("x_mean"), 1)

            def x_var(i):
                dve.wait_ge(S("x_mean"), i + 1)
                v.tensor_scalar(x_ve[0:R], x_mv[0:R, 1:2], EPS, None, ALU.add).then_inc(S("x_variance"), 1)

            def x_norm(i):
                dve.wait_ge(S("x_h_stored"), i * 16)
                dve.wait_ge(S("x_rstd"), i + 1)
                v.tensor_scalar(x_h[0:R], x_1[0:R], x_mv[0:R, 0:1], x_rs[0:R, 0:1], ALU.subtract, ALU.mult).then_inc(S("x_normed"), 1)

            def early_norm(q):
                dve.wait_ge(S("early_rstd"), q + 1)
                for t in range(2):
                    last = v.tensor_scalar(H[q][0:R, t, :], x_cur[q][0:R, t, :], st[q][0:R, t, 1:2], rs[q][0:R, t:t + 1], ALU.subtract, ALU.mult)
                last.then_inc(S("h_ready"), 1)

            for q in range(PAIRS):
                dve.wait_ge(S(f"early_rows_loaded{q}"), 32)
                v.tensor_tensor(O[q][0:R], O[q][0:R], bo_row[0:R].unsqueeze(1).broadcast_to([R, 2, D]), ALU.add).then_inc(S("early_biased"), 1)
            for q in range(PAIRS):
                dve.wait_ge(S("early_multiplied"), q + 1)
                dve.wait_ge(S("early_biased"), q + 1)
                v.tensor_tensor(x_cur[q][0:R], MM[q % 3][0:R, :].rearrange("p (t f) -> p t f", t=2), O[q][0:R], ALU.add).then_inc(S("early_summed"), 1)
                dve.wait_ge(S("early_summed"), q + 1)
                v.bn_stats(st[q][0:R].rearrange("p t k -> p (t k)"), x_cur[q][0:R].rearrange("p t f -> p f t")).then_inc(S("early_stats"), 1)
                dve.wait_ge(S("early_stats"), q + 1)
                v.tensor_scalar(ve[q][0:R], st[q][0:R, :, 2], 1.0 / D, EPS, ALU.mult, ALU.add).then_inc(S("early_variance"), 1)
                if q >= 1:
                    early_norm(q - 1)
            early_norm(PAIRS - 1)

            def f_sum(n, q):
                dve.wait_ge(S("tanh_done"), n + 1)
                v.scalar_tensor_tensor(out=T[q][0:R], in0=T[q][0:R], scalar=0.01, in1=H[q][0:R], op0=ALU.mult, op1=ALU.add).then_inc(S("u_done"), 1)

            def f_stats(n, q):
                dve.wait_ge(S("silu_done"), n + 1)
                v.bn_stats(st[q][0:R].rearrange("p t k -> p (t k)"), T[q][0:R].rearrange("p t f -> p f t")).then_inc(S("stats"), 1)

            def f_var(n, q):
                dve.wait_ge(S("stats"), n + 1)
                v.tensor_scalar(ve[q][0:R], st[q][0:R, :, 2], 1.0 / D, EPS, ALU.mult, ALU.add).then_inc(S("variance"), 1)

            def f_low(n, b):
                dve.wait_ge(S("transposed_copied"), n + 1)
                v.tensor_tensor(v_low[b][:].rearrange("p t b r -> p (t b r)"), TR[b][:, 0:4 * R], v_high[b][:].rearrange("p t b r -> p (t b r)"), ALU.subtract).then_inc(S("low_ready"), 1)

            def f_scale(n, q, b):
                dve.wait_ge(S("rstd"), n + 1)
                dve.wait_ge(S("multiplied"), n + 1)
                for t in range(2):
                    last = v.scalar_tensor_tensor(out=H[q][0:R, t, :], in0=MM[b][0:R, t * D:(t + 1) * D], scalar=rs[q][0:R, t:t + 1],
                                                  in1=c_row[0:R], op0=ALU.mult, op1=ALU.add)
                last.then_inc(S("h_ready"), 1)

            def f_end(n, q, b, r, last_round):
                dve.wait_ge(S(f"x_cur_loaded{q}"), r * 16 + 16)
                v.tensor_tensor(x_cur[q][0:R], x_cur[q][0:R], c_row[0:R].unsqueeze(1).broadcast_to([R, 2, D]), ALU.add).then_inc(S("c_added"), 1)
                dve.wait_ge(S("rstd"), n + 1)
                dve.wait_ge(S("multiplied"), n + 1)
                dve.wait_ge(S("c_added"), r * PAIRS + (q + 1))
                dve.wait_ge(S(f"out_stored{q}"), r * 16)
                for t in range(2):
                    o = v.scalar_tensor_tensor(out=O[q][0:R, t, :], in0=MM[b][0:R, t * D:(t + 1) * D], scalar=rs[q][0:R, t:t + 1],
                                               in1=x_cur[q][0:R, t, :], op0=ALU.mult, op1=ALU.add)
                o.then_inc(S("out_ready"), 1)
                if not last_round:
                    dve.wait_ge(S(f"h_next_loaded{q}"), r * 16 + 16)
                    v.tensor_copy(H[q][0:R], h_next[q][0:R]).then_inc(S("h_ready"), 1)

            f_sum(0, 0)
            f_sum(1, 1)
            f_stats(0, 0)
            f_var(0, 0)
            f_sum(2, 2)
            f_stats(1, 1)
            f_var(1, 1)
            if 0 in SPLIT:
                f_low(0, 0)
            f_sum(3, 3)
            if 1 in SPLIT:
                f_low(1, 1)

            def f_trip(t, r, end, g, xx, last):
                for s in range(SLOTS):
                    n = t * SLOTS + s
                    q = s % PAIRS
                    if not (last and s + 2 >= SLOTS):
                        f_stats(n + 2, (s + 2) % PAIRS)
                    if g:
                        j = t + EARLY_G
                        if s == F_G.first:
                            g_scalars(j, 0, t * 48 + F_EDGES)
                        for c in F_G.hot[s]:
                            g_hot(j, c)
                    if xx:
                        for at, part in ((X_STATS, x_stats), (X_MEAN, x_mean), (X_VAR, x_var), (X_NORM, x_norm)):
                            if s == at:
                                part(t)
                    if not (last and s + 2 >= SLOTS):
                        f_var(n + 2, (s + 2) % PAIRS)
                    if not (last and s + 4 >= SLOTS):
                        f_sum(n + 4, (s + 4) % PAIRS)
                    if not (last and s + 2 >= SLOTS) and (s + 2) % SLOTS in SPLIT:
                        f_low(n + 2, (s + 2) % 3)
                    if end and s >= SLOTS - PAIRS:
                        f_end(n, q, s % 3, r, last)
                        if not last and s == SLOTS - 1:
                            dve.wait_ge(S("h_ready"), n + (1 + PAIRS))
                            dve.sem_inc(S("h_next_used"), PAIRS)
                    else:
                        f_scale(n, q, s % 3)

            trips_of_f(dve, f_trip)

        @block.tensor
        def _(pe):
            mm, tp = nc.tensor.matmul, nc.tensor.transpose
            pe.sem_inc(S("chunks_multiplied"), KC)
            pe.wait_ge(S("ones_made"), 1)
            pe.wait_ge(S("heads_ready"), 1)
            mm(XB[:, 0:BLOCKS], ones[0:BLOCKS, :], heads[0:BLOCKS, 0:BLOCKS], start=True, stop=True).then_inc(S("heads_spread"), 1)
            pe.wait_ge(S("windows_ready"), 1)
            mm(XB[:, 128:128 + TILES], ones[0:TILES, :], heads[0:TILES, 0:TILES], start=True, stop=True)
            mm(XB[:, 256:257], ones[0:BLOCKS, :], p_t[0:BLOCKS, 9:10], start=True, stop=True).then_inc(S("windows_spread"), 1)
            pe.wait_ge(S("w_scaled"), 1)
            pe.wait_ge(S("offsets_ready"), 1)
            for b in range(2):
                mm(AGG[:, 0:D], ones[:], w_ffn[:, b, :], start=b == 0, stop=b == 1)
            for b in range(2):
                last = mm(XB[:, 0:D], lnb_b[:, b, :], w_raw[:, b, :], start=b == 0, stop=b == 1)
            last.then_inc(S("w_summed"), 1)
            pe.wait_ge(S("w_ffn_ready"), 1)
            n_u = pe.value_load(off_row[0:1, TILES:TILES + 1], min_val=1, max_val=E // UC)
            with pe.Fori(0, n_u) as i:
                pe.wait_ge(S("u_weighted"), i + 1)
                mm(XB[0:UC, 0:D], u_eq[0:UC, 0:UC], u_gw[0:UC, :], start=True, stop=True).then_inc(S("u_multiplied"), 1)
            pe.wait_ge(S("u_rows_ready"), n_u)

            def g_chunk(j, c):
                pe.wait_ge(S(f"gathered{c}"), j * 16 + 16)
                pe.wait_ge(S("hot_ready"), j * KC + (c + 1))
                if c == 0:
                    pe.wait_ge(S("messages_copied"), j)
                mm(AGG[0:R, 0:D], hot[c][:], gat[c][:], start=c == 0, stop=c == KC - 1).then_inc(S("chunks_multiplied"), 1)

            def xb_transpose(rows_, gs, xs):
                if gs is not None:
                    pe.wait_ge(S("g_done"), gs)
                if xs is not None:
                    pe.wait_ge(S("x_summed"), xs)
                for b in range(2):
                    last = tp(XB[:, b * R:(b + 1) * R], rows_[0:R, b * 128:(b + 1) * 128], ident[0:R, 0:R])
                last.then_inc(S("xb_transposed"), 1)

            def xb_multiply(w, use):
                pe.wait_ge(S("xb_copied"), use + 1)
                for b in range(2):
                    last = mm(XB[0:R, 0:D], xb_t[:, b, :], w[:, b, :], start=b == 0, stop=b == 1)
                last.then_inc(S("xb_multiplied"), 1)

            def g_transpose(j, gs, xs):
                pe.wait_ge(S("messages_copied"), j + 1)
                xb_transpose(g_agg, gs, xs)

            def x_transpose(i, gs, xs):
                pe.wait_ge(S("x_rows_loaded"), i * 32 + 32)
                xb_transpose(x_n, gs, xs)

            def k_transpose(loads, s):
                b, c = s % 2, s % K_RING
                pe.wait_ge(S(f"k_loaded{c}"), loads * 16)
                for h in range(2):
                    last = tp(K_TR[b][:, h * R:(h + 1) * R], k_x[c][0:R, h * 128:(h + 1) * 128], ident[0:R, 0:R])
                last.then_inc(S("k_transposed"), 1)

            def k_project(t, b, normed):
                pe.wait_ge(S("k_copied"), t + 1)
                if normed is not None:
                    pe.wait_ge(S("k_normed"), normed)
                for h in range(2):
                    last = mm(K_MM[b][0:R, :], k_t[b][:, h, :], w_kv[:, h, :], start=h == 0, stop=h == 1)
                last.then_inc(S("k_projected"), 1)

            def k_outer(t, b, first, final):
                pe.wait_ge(S("k_normed"), t + 1)
                for hp in range(2):
                    last = mm(K_ACC[hp][:, 0:128], k_n[b][0:R, D + hp * 128:D + (hp + 1) * 128], k_n[b][0:R, hp * 128:(hp + 1) * 128],
                              start=first, stop=final)
                last.then_inc(S("k_outer_done"), 1)

            pe.wait_ge(S("w_kv_ready"), 2)
            k_transpose(1, 0)
            k_transpose(1, 1)
            k_project(0, 0, None)
            k_transpose(1, 2)
            k_project(1, 1, None)

            def b_trip(i, first, last):
                for s in range(KV_STEPS):
                    t = i * KV_STEPS + s
                    if not (last and s + 3 >= KV_STEPS):
                        k_transpose(i * (KV_STEPS // K_RING) + ((s + 3) // K_RING + 1), s + 3)
                    if not (last and s + 2 >= KV_STEPS):
                        k_project(t + 2, s % 2, t + 1)
                    for g in range(2):
                        if B_G[g].transpose == s:
                            g_transpose(i * 2 + g, i * 2 + g, None)
                        for c in B_G[g].mul[s]:
                            g_chunk(i * 2 + g, c)
                    k_outer(t, s % 2, first and s == 0, last and s == KV_STEPS - 1)
                    for g in range(2):
                        if B_G[g].multiply == s:
                            xb_multiply(w_agg, i * 2 + g)

            b_trip(0, True, False)
            with pe.Fori(1, LAST_B) as i:
                b_trip(i, False, False)
            b_trip(LAST_B, False, True)

            pe.wait_ge(S("g_done"), EARLY_G)
            pe.wait_ge(S("k_added"), TILES)
            for hp in range(2):
                mm(XB[:, hp * 128:(hp + 1) * 128], ones[0:R, :], k_sum[0:R, hp * 128:(hp + 1) * 128], start=True, stop=True)
            for hp in range(2):
                last = mm(XB[:, 256 + hp:257 + hp], k_sum[0:R, D + hp * 128:D + (hp + 1) * 128], ones[0:R, 0:1], start=True, stop=True)
            last.then_inc(S("sums_spread"), 1)
            pe.wait_ge(S("kv_ready"), 4)
            for hp in range(2):
                mm((AGG, XB)[hp][:, 0:D], kv_t[:, hp, :], w_wo[:, hp, :], start=True, stop=True).then_inc(S("kv_wo_done"), 1)
            pe.wait_ge(S("kv_wo_copied"), 2)
            for b in range(2):
                for hp in range(2):
                    last = mm(K_TR[b][:, 0:D], w_wq[:, hp, b * 128:(b + 1) * 128], t1[:, hp, :], start=hp == 0, stop=hp == 1)
                last.then_inc(S("mix_done"), 1)
            pe.wait_ge(S("mix_copied"), 2)

            def early_transpose(q):
                pe.wait_ge(S(f"early_rows_loaded{q}"), 32)
                if q >= 3:
                    pe.wait_ge(S("early_copied"), q - 2)
                for t in range(2):
                    for h in range(2):
                        last = tp(TR[q % 3][:, (t * 2 + h) * R:(t * 2 + h + 1) * R], T[q][0:R, t, h * 128:(h + 1) * 128], ident[0:R, 0:R])
                last.then_inc(S("early_transposed"), 1)

            early_transpose(0)
            for q in range(PAIRS):
                if q + 1 < PAIRS:
                    early_transpose(q + 1)
                pe.wait_ge(S("early_copied"), q + 1)
                if q >= 3:
                    pe.wait_ge(S("early_summed"), q - 2)
                for t in range(2):
                    for h in range(2):
                        last = mm(MM[q % 3][0:R, t * D:(t + 1) * D], v_t[q % 3][:, t, h, :], w_mix[:, h, :], start=h == 0, stop=h == 1)
                last.then_inc(S("early_multiplied"), 1)

            def f_transpose(n, q, b):
                pe.wait_ge(S("silu_done"), n + 1)
                for t in range(2):
                    for h in range(2):
                        last = tp(TR[b][:, (t * 2 + h) * R:(t * 2 + h + 1) * R], T[q][0:R, t, h * 128:(h + 1) * 128], ident[0:R, 0:R])
                last.then_inc(S("transposed"), 1)

            def f_multiply(n, b, r, outs, low):
                if low is not None:
                    pe.wait_ge(S("low_ready"), low)
                pe.wait_ge(S("transposed_copied"), n + 1)
                if outs > 0:
                    pe.wait_ge(S("out_ready"), r * PAIRS + outs)
                else:
                    pe.wait_ge(S("h_ready"), n + (PAIRS - 2))
                if low is None:
                    parts = ((v_t[b], w_ffn),)
                else:
                    parts = ((v_high[b], w_high), (v_high[b], w_low), (v_low[b], w_high))
                for t in range(2):
                    products = [(rows_[:, t, h, :], w[:, h, :]) for h in range(2) for rows_, w in parts]
                    for k, (rows_, w) in enumerate(products):
                        last = mm(MM[b][0:R, t * D:(t + 1) * D], rows_, w, start=k == 0, stop=k == len(products) - 1)
                last.then_inc(S("multiplied"), 1)

            f_transpose(0, 0, 0)
            f_transpose(1, 1, 1)

            def f_trip(t, r, end, g, xx, last):
                for s in range(SLOTS):
                    n = t * SLOTS + s
                    if not (last and s + 2 >= SLOTS):
                        f_transpose(n + 2, (s + 2) % PAIRS, (s + 2) % 3)
                    if xx and s == X_TRANSPOSE:
                        x_transpose(t, t + EARLY_G if g else TILES, t)
                    if xx and s == X_MULTIPLY:
                        xb_multiply(w_mix, x_use(t, g))
                    if g:
                        if s == F_G.multiply:
                            xb_multiply(w_agg, g_use(t))
                        for c in F_G.mul[s]:
                            g_chunk(t + EARLY_G, c)
                    f_multiply(n, s % 3, r, s - 3 - (SLOTS - PAIRS) + 1 if last else 0,
                               splits(t, s) if s in SPLIT else None)
                    if g and s == F_G.transpose:
                        g_transpose(t + EARLY_G, t + EARLY_G, t + 1)

            trips_of_f(pe, f_trip)


_INS = ["x", "src", "dst", "ew", "w_gnn", "wq", "wk_t", "wv_t", "wo_t", "bo", "gk", "bk", "gv", "bv", "ln_w", "ln_b", "wf_t", "bf"]


def kernel(**inputs):
    import numpy as _np
    import concourse.bacc as _bacc
    from concourse import mybir as _mybir
    from concourse.bass_utils import run_bass_kernel_spmd as _run

    a = {k: _np.asarray(t) for k, t in inputs.items()}
    laid = {
        "x": a["x"], "src": a["src"], "dst": a["dst"], "ew": a["edge_weight"], "w_gnn": a["L0_gnn_weight"],
        "wq": a["L0_mix_wq"], "wk_t": a["L0_mix_wk"].T, "wv_t": a["L0_mix_wv"].T, "wo_t": a["L0_mix_wo"].T, "bo": a["L0_mix_bo"],
        "gk": a["L0_mix_ln_k_g"], "bk": a["L0_mix_ln_k_b"], "gv": a["L0_mix_ln_v_g"], "bv": a["L0_mix_ln_v_b"],
        "ln_w": a["L0_ffn_ln_w"], "ln_b": a["L0_ffn_ln_b"], "wf_t": a["L0_ffn_W"].T, "bf": a["L0_ffn_b"],
    }
    nc = _bacc.Bacc("TRN2", target_bir_lowering=False, num_devices=1)
    arrays, args = {}, []
    for name in _INS:
        t = _np.ascontiguousarray(laid[name])
        arrays[f"in_{name}"] = t
        args.append(nc.dram_tensor(f"in_{name}", t.shape, _mybir.dt.from_np(t.dtype), kind="ExternalInput").ap())
    args.append(nc.dram_tensor("out_rows", (N, D), _mybir.dt.float32, kind="ExternalOutput").ap())
    build(nc, *args)
    r = _run(nc, [arrays], core_ids=[0])
    return _np.asarray(r.results[0]["out_rows"])
```
